# Optimizing a Trainium2 kernel written in Bass

```python
import numpy as np
import jax
import jax.numpy as jnp

def _softmax(x, axis=-1):
    return jax.nn.softmax(x, axis=axis)

def _gelu(x):
    return jax.nn.gelu(x, approximate=True)

def _silu(x):
    return jax.nn.silu(x)

def _sigmoid(x):
    return jax.nn.sigmoid(x)

def _layernorm(x, axis=-1, eps=1e-05):
    m = jnp.mean(x, axis=axis, keepdims=True)
    v = jnp.var(x, axis=axis, keepdims=True)
    return (x - m) / jnp.sqrt(v + eps)

def _scatter_add(tgt, idx, src, axis=0):
    return tgt.at[idx].add(src)

def _segment_sum(src, seg, n):
    return jax.ops.segment_sum(src, seg, n)
kernel_name = 'mk_gnn_resnorm_d4_gnn_r32_54eecd'

def setup_inputs(seed: int=0):
    np.random.seed(seed)
    _w = jnp.asarray

    def _rec_inputs():
        import jax
        import jax.numpy as jnp
        _gk = jax.random.key(seed)
        x = -8.776e-05 + 1 * jax.random.normal(jax.random.fold_in(_gk, 1), (3125, 128), jnp.float32)
        _s = jax.random.randint(jax.random.fold_in(_gk, 2), (50000,), 0, 3125, jnp.int32)
        _d = jax.random.randint(jax.random.fold_in(_gk, 3), (50000,), 0, 3125, jnp.int32)
        _loop = jnp.arange(3125, dtype=jnp.int32)
        src = jnp.concatenate([_s, _d, _loop])
        dst = jnp.concatenate([_d, _s, _loop])
        _o = jnp.argsort(dst, stable=True)
        src = src[_o]
        dst = dst[_o]
        edge_type_5 = jax.random.randint(jax.random.fold_in(_gk, 13), (103125,), 0, 5, jnp.int32)
        node_type_5 = jax.random.randint(jax.random.fold_in(_gk, 14), (3125,), 0, 5, jnp.int32)
        return (x, src, dst, edge_type_5, node_type_5)
    x, src, dst, edge_type_5, node_type_5 = _rec_inputs()

    def _L0_gnn_setup():
        import jax, jax.numpy as jnp
        import numpy as np
        N, E, D, H = (1250, 20000, 128, 8)
        DH = D // H
        EPS = 1e-05

        def _layernorm(x, g, b):
            mu = jnp.mean(x, axis=-1, keepdims=True)
            var = jnp.mean(jnp.square(x - mu), axis=-1, keepdims=True)
            return (x - mu) * jax.lax.rsqrt(var + EPS) * g + b
        key = jax.random.key(seed)
        ks = jax.random.split(key, 12)
        s = 0.02
        return {'feat': jax.random.normal(ks[0], (N, D), dtype=jnp.float32), 'src': jax.random.randint(ks[1], (E,), 0, N, dtype=jnp.int32), 'dst': jax.random.randint(ks[2], (E,), 0, N, dtype=jnp.int32), 'Wq': jax.random.normal(ks[3], (D, D), dtype=jnp.float32) * s, 'Wk': jax.random.normal(ks[4], (D, D), dtype=jnp.float32) * s, 'Wv': jax.random.normal(ks[5], (D, D), dtype=jnp.float32) * s, 'ln1_g': jnp.ones((D,), jnp.float32), 'ln1_b': jnp.zeros((D,), jnp.float32), 'ln2_g': jnp.ones((D,), jnp.float32), 'ln2_b': jnp.zeros((D,), jnp.float32), 'W1': jax.random.normal(ks[6], (D, 4 * D), dtype=jnp.float32) * s, 'b1': jnp.zeros((4 * D,), jnp.float32), 'prelu_w': jnp.full((4 * D,), 0.25, jnp.float32), 'W2': jax.random.normal(ks[7], (4 * D, D), dtype=jnp.float32) * s, 'b2': jnp.zeros((D,), jnp.float32)}
    _L0_gnn_all = _L0_gnn_setup()
    _L0_gnn_in = {k: v for k, v in _L0_gnn_all.items() if k in ('Wq', 'Wk', 'Wv', 'ln1_g', 'ln1_b', 'ln2_g', 'ln2_b', 'W1', 'b1', 'prelu_w', 'W2', 'b2')}
    del _L0_gnn_all

    def _L1_gnn_setup():
        import jax, jax.numpy as jnp
        import numpy as np
        N_NODES = 3125
        EMB_DIM = 128
        N_EDGES = 50000
        key = jax.random.key(seed)
        k1, k2 = jax.random.split(key)
        edge_index = jax.random.randint(k1, (2, N_EDGES), 0, N_NODES, dtype=jnp.int64 if jax.config.read('jax_enable_x64') else jnp.int32)
        embedding = jax.random.normal(k2, (N_NODES, EMB_DIM), dtype=jnp.float32)
        return {'edge_index': edge_index, 'embedding': embedding}
    _L1_gnn_all = _L1_gnn_setup()
    _L1_gnn_in = {k: v for k, v in _L1_gnn_all.items() if k in ()}
    del _L1_gnn_all

    def _L2_gnn_setup():
        import jax, jax.numpy as jnp
        import numpy as np
        N, E = (50000, 25000)
        NUM_TYPES = 5
        NUM_HEADS = 4
        HIDDEN = 32
        IN_DIM = 128
        NEG_SLOPE = 0.2

        def typed_linear(x, types, W):
            out = jnp.zeros((x.shape[0], W.shape[2]), dtype=x.dtype)
            for t in range(W.shape[0]):
                out = out + jnp.where((types == t)[:, None], x @ W[t], jnp.zeros((), x.dtype))
            return out
        key = jax.random.key(seed)
        ks = jax.random.split(key, 10)
        x = jax.random.normal(ks[0], (N, IN_DIM), dtype=jnp.float32)
        ntype = jax.random.randint(ks[1], (N,), 0, NUM_TYPES)
        etype = jax.random.randint(ks[2], (E,), 0, NUM_TYPES)
        src = jax.random.randint(ks[3], (E,), 0, N)
        dst = jax.random.randint(ks[4], (E,), 0, N)
        sc = 1.0 / np.sqrt(IN_DIM)
        W_typed = jax.random.normal(ks[5], (NUM_TYPES, IN_DIM, HIDDEN * NUM_HEADS), dtype=jnp.float32) * sc
        al_w = jax.random.normal(ks[6], (NUM_TYPES, HIDDEN, HIDDEN), dtype=jnp.float32) * (1.0 / np.sqrt(HIDDEN))
        ar_w = jax.random.normal(ks[7], (NUM_TYPES, HIDDEN, HIDDEN), dtype=jnp.float32) * (1.0 / np.sqrt(HIDDEN))
        W_res = jax.random.normal(ks[8], (IN_DIM, HIDDEN * NUM_HEADS), dtype=jnp.float32) * sc
        b_res = jax.random.normal(ks[9], (HIDDEN * NUM_HEADS,), dtype=jnp.float32) * 0.01
        return {'x': x, 'ntype': ntype, 'etype': etype, 'src': src, 'dst': dst, 'W_typed': W_typed, 'al_w': al_w, 'ar_w': ar_w, 'W_res': W_res, 'b_res': b_res}
    _L2_gnn_all = _L2_gnn_setup()
    _L2_gnn_in = {k: v for k, v in _L2_gnn_all.items() if k in ('W_typed', 'al_w', 'ar_w', 'W_res', 'b_res')}
    del _L2_gnn_all

    def _L3_gnn_setup():
        import jax, jax.numpy as jnp
        import numpy as np
        N_NODES = 50000
        N_EDGES = 20000
        D_FEAT = 128
        HIDDEN = 128
        key = jax.random.key(seed)
        ks = jax.random.split(key, 6)
        x = jax.random.normal(ks[0], (N_NODES, D_FEAT), dtype=jnp.float32)
        edge_index = jax.random.randint(ks[1], (2, N_EDGES), 0, N_NODES, dtype=jnp.int64)
        W = jax.random.normal(ks[2], (D_FEAT, HIDDEN), dtype=jnp.float32) * (1.0 / np.sqrt(D_FEAT))
        b = jnp.zeros((HIDDEN,), dtype=jnp.float32)
        lin_W = jax.random.normal(ks[3], (D_FEAT, HIDDEN), dtype=jnp.float32) * (1.0 / np.sqrt(HIDDEN))
        lin_b = jnp.zeros((D_FEAT,), dtype=jnp.float32)
        return {'x': x, 'edge_index': edge_index, 'W': W, 'b': b, 'lin_W': lin_W, 'lin_b': lin_b}
    _L3_gnn_all = _L3_gnn_setup()
    _L3_gnn_in = {k: v for k, v in _L3_gnn_all.items() if k in ('W', 'b', 'lin_W', 'lin_b')}
    del _L3_gnn_all
    return {'x': x, 'src': src, 'dst': dst, 'edge_type_5': edge_type_5, 'node_type_5': node_type_5, 'L0_gnn_Wq': _L0_gnn_in['Wq'], 'L0_gnn_Wk': _L0_gnn_in['Wk'], 'L0_gnn_Wv': _L0_gnn_in['Wv'], 'L0_gnn_ln1_g': _L0_gnn_in['ln1_g'], 'L0_gnn_ln1_b': _L0_gnn_in['ln1_b'], 'L0_gnn_ln2_g': _L0_gnn_in['ln2_g'], 'L0_gnn_ln2_b': _L0_gnn_in['ln2_b'], 'L0_gnn_W1': _L0_gnn_in['W1'], 'L0_gnn_b1': _L0_gnn_in['b1'], 'L0_gnn_prelu_w': _L0_gnn_in['prelu_w'], 'L0_gnn_W2': _L0_gnn_in['W2'], 'L0_gnn_b2': _L0_gnn_in['b2'], 'L2_gnn_W_typed': _L2_gnn_in['W_typed'], 'L2_gnn_al_w': _L2_gnn_in['al_w'], 'L2_gnn_ar_w': _L2_gnn_in['ar_w'], 'L2_gnn_W_res': _L2_gnn_in['W_res'], 'L2_gnn_b_res': _L2_gnn_in['b_res'], 'L3_gnn_W': _L3_gnn_in['W'], 'L3_gnn_b': _L3_gnn_in['b'], 'L3_gnn_lin_W': _L3_gnn_in['lin_W'], 'L3_gnn_lin_b': _L3_gnn_in['lin_b']}

def reference(x, src, dst, edge_type_5, node_type_5, L0_gnn_Wq, L0_gnn_Wk, L0_gnn_Wv, L0_gnn_ln1_g, L0_gnn_ln1_b, L0_gnn_ln2_g, L0_gnn_ln2_b, L0_gnn_W1, L0_gnn_b1, L0_gnn_prelu_w, L0_gnn_W2, L0_gnn_b2, L2_gnn_W_typed, L2_gnn_al_w, L2_gnn_ar_w, L2_gnn_W_res, L2_gnn_b_res, L3_gnn_W, L3_gnn_b, L3_gnn_lin_W, L3_gnn_lin_b):
    import jax
    import jax.numpy as jnp

    def _L0_gnn_ref(feat, src, dst, Wq, Wk, Wv, ln1_g, ln1_b, ln2_g, ln2_b, W1, b1, prelu_w, W2, b2):
        import jax, jax.numpy as jnp
        import numpy as np
        N, E, D, H = (1250, 20000, 128, 8)
        DH = D // H
        EPS = 1e-05

        def _layernorm(x, g, b):
            mu = jnp.mean(x, axis=-1, keepdims=True)
            var = jnp.mean(jnp.square(x - mu), axis=-1, keepdims=True)
            return (x - mu) * jax.lax.rsqrt(var + EPS) * g + b
        n = feat.shape[0]
        feat_c = jax.lax.stop_gradient(feat)
        q = (feat @ Wq).reshape(n, H, DH)
        k = (feat_c @ Wk).reshape(n, H, DH)
        v = (feat_c @ Wv).reshape(n, H, DH)
        scores = jnp.einsum('ehd,ehd->eh', k[src], q[dst]) / np.float32(np.sqrt(DH * H))
        smax = jax.ops.segment_max(scores, dst, num_segments=n)
        sexp = jnp.exp(scores - smax[dst])
        ssum = jax.ops.segment_sum(sexp, dst, num_segments=n)
        a = sexp / ssum[dst]
        msgs = v[src] * a[:, :, None]
        ft2 = jax.ops.segment_sum(msgs, dst, num_segments=n).reshape(n, D)
        rst = _layernorm(ft2 + feat, ln1_g, ln1_b)
        h = rst @ W1 + b1
        h = jnp.where(h >= 0, h, prelu_w * h)
        ffn = h @ W2 + b2
        return _layernorm(rst + ffn, ln2_g, ln2_b)

    def _L1_gnn_ref(edge_index, embedding):
        import jax, jax.numpy as jnp
        import numpy as np
        N_NODES = 3125
        EMB_DIM = 128
        N_EDGES = 50000
        N = embedding.shape[0]
        loop = jnp.arange(N, dtype=edge_index.dtype)
        row = jnp.concatenate([edge_index[0], loop])
        col = jnp.concatenate([edge_index[1], loop])
        deg = jax.ops.segment_sum(jnp.ones_like(row, dtype=embedding.dtype), row, num_segments=N)
        deg_inv_sqrt = jnp.where(deg > 0, jax.lax.rsqrt(jnp.maximum(deg, 1.0)), 0.0)
        norm = deg_inv_sqrt[row] * deg_inv_sqrt[col]
        msgs = norm[:, None] * embedding[row]
        out = jax.ops.segment_sum(msgs, col, num_segments=N)
        return out

    def _L2_gnn_ref(x, ntype, etype, src, dst, W_typed, al_w, ar_w, W_res, b_res):
        import jax, jax.numpy as jnp
        import numpy as np
        N, E = (50000, 25000)
        NUM_TYPES = 5
        NUM_HEADS = 4
        HIDDEN = 32
        IN_DIM = 128
        NEG_SLOPE = 0.2

        def typed_linear(x, types, W):
            out = jnp.zeros((x.shape[0], W.shape[2]), dtype=x.dtype)
            for t in range(W.shape[0]):
                out = out + jnp.where((types == t)[:, None], x @ W[t], jnp.zeros((), x.dtype))
            return out
        n = x.shape[0]
        feat = typed_linear(x, ntype, W_typed)
        h = feat.reshape(n, NUM_HEADS, HIDDEN)
        ntype_rep = jnp.repeat(ntype, NUM_HEADS)
        h_flat = h.reshape(-1, HIDDEN)
        h_l = typed_linear(h_flat, ntype_rep, al_w).reshape(n, NUM_HEADS, HIDDEN).sum(-1)
        h_r = typed_linear(h_flat, ntype_rep, ar_w).reshape(n, NUM_HEADS, HIDDEN).sum(-1)
        e = jax.nn.leaky_relu(h_l[src] + h_r[dst], NEG_SLOPE)
        m = jax.ops.segment_max(e, dst, num_segments=n)
        ex = jnp.exp(e - m[dst])
        s = jax.ops.segment_sum(ex, dst, num_segments=n)
        alpha = ex / s[dst]
        msg = h[src] * alpha[:, :, None]
        agg = jax.ops.segment_sum(msg, dst, num_segments=n)
        out = agg.transpose(0, 2, 1).reshape(n, HIDDEN * NUM_HEADS)
        out = out + x @ W_res + b_res
        return jax.nn.relu(out)

    def _L3_gnn_ref(x, edge_index, W, b, lin_W, lin_b):
        import jax, jax.numpy as jnp
        import numpy as np
        N_NODES = 50000
        N_EDGES = 20000
        D_FEAT = 128
        HIDDEN = 128
        'HeteroGCN forward (eval mode -> dropout is identity).\n\n            GCNConv with default add_self_loops=True, normalize=True:\n              out_i = sum_{j->i} deg_j^{-1/2} deg_i^{-1/2} (x_j @ W) + b\n            then relu, then Linear(hidden -> d_feat).\n            '
        N = x.shape[0]
        loops = jnp.arange(N, dtype=edge_index.dtype)
        src = jnp.concatenate([edge_index[0], loops])
        dst = jnp.concatenate([edge_index[1], loops])
        deg = jax.ops.segment_sum(jnp.ones_like(dst, dtype=x.dtype), dst, num_segments=N)
        dis = jnp.where(deg > 0, jax.lax.rsqrt(jnp.maximum(deg, 1.0)), 0.0)
        norm = dis[src] * dis[dst]
        h = x @ W
        msg = h[src] * norm[:, None]
        agg = jax.ops.segment_sum(msg, dst, num_segments=N) + b
        h = jax.nn.relu(agg)
        out = h @ lin_W.T + lin_b
        return out
    edge_index = jnp.stack([src, dst])
    x = _layernorm(x + _L0_gnn_ref(x, src, dst, L0_gnn_Wq, L0_gnn_Wk, L0_gnn_Wv, L0_gnn_ln1_g, L0_gnn_ln1_b, L0_gnn_ln2_g, L0_gnn_ln2_b, L0_gnn_W1, L0_gnn_b1, L0_gnn_prelu_w, L0_gnn_W2, L0_gnn_b2), axis=-1)
    x = _layernorm(x + _L1_gnn_ref(edge_index, x), axis=-1)
    x = _layernorm(x + _L2_gnn_ref(x, node_type_5, edge_type_5, src, dst, L2_gnn_W_typed, L2_gnn_al_w, L2_gnn_ar_w, L2_gnn_W_res, L2_gnn_b_res), axis=-1)
    x = _layernorm(x + _L3_gnn_ref(x, edge_index, L3_gnn_W, L3_gnn_b, L3_gnn_lin_W, L3_gnn_lin_b), axis=-1)
    return x

_drawn_inputs = setup_inputs


def setup_inputs(seed=0):
    import zlib

    import numpy as np

    out = dict(_drawn_inputs(seed))
    spreads = {'L0_gnn_ln1_g': (1.0, 0.2),
     'L0_gnn_ln1_b': (0.0, 0.1),
     'L0_gnn_ln2_g': (1.0, 0.2),
     'L0_gnn_ln2_b': (0.0, 0.1),
     'L0_gnn_b1': (0.0, 0.1),
     'L0_gnn_prelu_w': (0.25, 0.6),
     'L0_gnn_b2': (0.0, 0.1),
     'L3_gnn_b': (0.0, 0.1),
     'L3_gnn_lin_b': (0.0, 0.1)}
    factors = {'L0_gnn_Wq': 8.0, 'L0_gnn_Wk': 8.0, 'L2_gnn_b_res': 8.0}
    for name, (base, spread) in spreads.items():
        noise = np.random.default_rng([zlib.crc32(name.encode()), seed]).standard_normal(out[name].shape)
        drawn = base * np.exp(spread * noise) if base else spread * noise
        out[name] = jnp.asarray(drawn.astype(out[name].dtype))
    for name, factor in factors.items():
        out[name] = (out[name] * factor).astype(out[name].dtype)
    return out
```

```python
from contextlib import ExitStack

import concourse.bass as bass
from concourse import mybir

ALU = mybir.AluOpType
ACT = mybir.ActivationFunctionType
AX = mybir.AxisListType
F32 = mybir.dt.float32
BF16 = mybir.dt.bfloat16
I32 = mybir.dt.int32

BIG = 1e30
ROUND = 12582912.0
EPS = 1e-5


class Signals(dict):

    def __init__(self, owner, sem):
        super().__init__()
        self.owner, self.sem = owner, sem

    def __missing__(self, name):
        self[name] = self.sem(f"{self.owner}_{name}")
        return self[name]


def gnn_kernel(nc, a, out):
    N, D = a["x"].shape
    E = a["src"].shape[0]
    LANES = 128
    NT = -(-N // LANES)
    LAST = N - (NT - 1) * LANES
    PAD = NT * LANES
    SLOTS = 8
    STEPS = -(-(PAD + E // SLOTS) // LANES)
    STEPS += STEPS % 2
    HALF = STEPS // 2
    ROWS = LANES * STEPS
    H0 = 8
    H2 = 4
    NTYPE = a["L2_gnn_W_typed"].shape[0]
    FF = a["L0_gnn_W1"].shape[1]
    FC = FF // 128
    EP = 125
    EC = E // EP
    BATCH = 55
    HA = (28, 27)
    NB = EC // BATCH
    assert EP * EC == E and NB * BATCH == EC
    LO = 64
    RB = -(-(SLOTS + E + SLOTS) // SLOTS)
    RBW = RB * SLOTS
    FS = 9
    FIT = STEPS // (2 * FS)
    assert FIT * 2 * FS == STEPS
    HXW = D + 2 * H2

    with ExitStack() as ctx:
        def sb(name, shape, dt=F32):
            return ctx.enter_context(nc.sbuf_tensor(name, shape, dt))

        def sem(name):
            return ctx.enter_context(nc.semaphore(name))

        def dram(name, shape, dt=F32):
            return nc.dram_tensor(name, shape, dt).ap()

        ps = [ctx.enter_context(nc.psum_tensor(f"ps{i}", [128, 512], F32)) for i in range(6)]

        shifted = dram("shifted_sources", [SLOTS * RB, SLOTS], I32)
        rowinfo_d = dram("rowinfo_d", [ROWS, 4])
        q_d = dram("q_d", [PAD, D])
        kv_d = dram("kv_d", [PAD, 2 * D])
        y_d = [dram(f"y{k}_d", [PAD, D]) for k in range(2)]
        h_d = dram("h_d", [PAD, D + H2])
        hr_d = dram("hr_d", [PAD, H2])
        W0 = D + 2 * H0
        W2_ = D + 2 * H2
        state_d = {"att0": dram("state0_d", [ROWS, W0]), "sum1": dram("state1_d", [ROWS, D]),
                   "att2": dram("state2_d", [ROWS, W2_]), "sum3": dram("state3_d", [ROWS, D])}
        carry_d = {"att0": dram("carry0_d", [LANES, W0]), "sum1": dram("carry1_d", [LANES, D]),
                   "att2": dram("carry2_d", [LANES, W2_]), "sum3": dram("carry3_d", [LANES, D])}

        X = sb("X", [128, NT, D])
        R = sb("R", [128, NT, D])
        T1 = sb("T1", [128, NT, D])
        finals = sb("finals", [128, 2 * NT * W0])
        final_state, final_carry = finals[:, 0:NT * W0], finals[:, NT * W0:]
        gathered = [sb(f"gathered{b}", [128, SLOTS * 2 * D]) for b in range(2)]
        dst_row = [sb(f"dst_row{b}", [128, D]) for b in range(2)]
        prod = sb("prod", [128, SLOTS, D])
        msg = sb("msg", [128, SLOTS * (D + H0)])
        state = [sb(f"state{b}", [128, W0]) for b in range(2)]
        index_cols = [sb(f"index_cols{b}", [128, SLOTS + 1], I32) for b in range(2)]
        IX = sb("IX", [128, STEPS + 2, SLOTS + 1])
        VALID = sb("VALID", [128, STEPS, SLOTS])
        BOUND = sb("BOUND", [128, STEPS, SLOTS])
        same = sb("same", [128, STEPS])
        same_bound = sb("same_bound", [128, STEPS])
        scores = sb("scores", [128, SLOTS, H0])
        top = sb("top", [128, H0])
        diff = sb("diff", [128, (SLOTS + 1) * H0])
        expd = sb("expd", [128, (SLOTS + 1) * H0])
        slot_sum = sb("slot_sum", [128, D + H0])
        scaled = sb("scaled", [128, D + H0])

        edge_i = sb("edge_i", [128, EC], I32)
        part_i = sb("part_i", [128, EC], I32)
        lo_b = sb("lo_b", [128, EC], BF16)
        hi_b = sb("hi_b", [128, EC], BF16)
        oh_lo = [sb(f"oh_lo{b}", [128, HA[b], LO], BF16) for b in range(2)]
        oh_hi = [sb(f"oh_hi{b}", [128, HA[b], 2 * NT], BF16) for b in range(2)]
        zero_b = sb("zero_b", [128, 128], BF16)
        iota_i = sb("iota_i", [128, 128], I32)
        iota_hi_i = sb("iota_hi_i", [128, 2 * NT], I32)
        node_i = sb("node_i", [128, NT], I32)
        row_i = sb("row_i", [128, STEPS], I32)
        part_id_i = sb("part_id_i", [128, 1], I32)
        iota_f = sb("iota_f", [128, 128])
        iota_lo_b = sb("iota_lo_b", [128, LO], BF16)
        iota_hi_b = sb("iota_hi_b", [128, 2 * NT], BF16)
        row_f = sb("row_f", [128, STEPS])
        part_id = sb("part_id", [128, 1])
        ident = sb("ident", [128, 128])
        before = sb("before", [128, 128])
        ones = sb("ones", [128, 128])
        zeros = sb("zeros", [128, 4 * STEPS])
        deg_rows = sb("deg_rows", [128, 2 * NT])
        tot = sb("tot", [128, 2 * NT])
        incl = sb("incl", [128, 2 * NT])
        starts = sb("starts", [128, 2 * NT])
        small_i = sb("small_i", [128, 2 * NT], I32)
        info = sb("info", [128, NT, 4])
        row0_i = sb("row0_i", [128, NT], I32)
        last_f = sb("last_f", [128, NT])
        last_i = sb("last_i", [128, NT], I32)
        lane_f = sb("lane_f", [128, NT])
        lane_i = sb("lane_i", [128, NT], I32)
        has = sb("has", [128, NT])
        has_bound = sb("has_bound", [128, NT])
        lane1_f = sb("lane1_f", [128, NT])
        rowinfo = sb("rowinfo", [128, STEPS, 4])
        RS = sb("RS", [128, 4, STEPS])
        lane_top = sb("lane_top", [4, 128])
        lane_excl = sb("lane_excl", [4, 128])
        lane_in = sb("lane_in", [4, 128])
        carry4 = sb("carry4", [128, 4])
        pos = sb("pos", [128, STEPS])
        pos_i = sb("pos_i", [128, STEPS], I32)
        low_i = sb("low_i", [128, STEPS], I32)
        high_i = sb("high_i", [128, STEPS], I32)
        low_f = sb("low_f", [128, STEPS])
        high_f = sb("high_f", [128, STEPS])
        table_row = sb("table_row", [128, STEPS])
        cont = sb("cont", [128, 1])
        cont2 = sb("cont2", [128, 1])
        wide = sb("wide", [128, 128])
        penalty = sb("penalty", [128, H0])
        penaltyT = sb("penaltyT", [H0, 128])
        contT = sb("contT", [128, 128])
        fetch_row = [sb(f"fetch_row{b}", [128, FS], I32) for b in range(2)]
        fetched = [sb(f"fetched{b}", [128, FS * SLOTS], I32) for b in range(2)]
        fetched_f = sb("fetched_f", [128, FS, SLOTS])
        dis = [sb(f"dis{k}", [128, NT]) for k in range(2)]
        outdeg = sb("outdeg", [128, NT])
        row_ok = sb("row_ok", [128, 1])

        xs = sb("xs", [128, 128])
        xT = sb("xT", [128, 128])
        hT = sb("hT", [128, FC * 128])
        hb = sb("hb", [128, FC, 128])
        hn = sb("hn", [128, FC, 128])
        proj = sb("proj", [128, 3 * D])

        Wqkv = sb("Wqkv", [128, 3 * D])
        W1 = sb("W1", [128, FF])
        W2 = sb("W2", [128, FC, D])
        b1 = sb("b1", [128, FC])
        pw = sb("pw", [128, FC])
        rows_in = {n: sb("row_" + n, [128, D]) for n in
                   ("L0_gnn_ln1_g", "L0_gnn_ln1_b", "L0_gnn_ln2_g", "L0_gnn_ln2_b", "L0_gnn_b2",
                    "L2_gnn_b_res", "L3_gnn_lin_b")}
        Wt_in = sb("Wt_in", [128, NTYPE, D])
        alr = sb("alr", [128, 2, NTYPE, 32])
        al_in = finals[:, 0:NTYPE * 32 * 32]
        Wcat = sb("Wcat", [128, NTYPE * HXW + D])
        Wprod = sb("Wprod", [128, D])
        ntype_i = sb("ntype_i", [128, NT], I32)
        ntype_f = sb("ntype_f", [128, NT])
        type_mask = sb("type_mask", [128, NT, NTYPE])
        hx = sb("hx", [128, HXW])
        hx2 = sb("hx2", [128, HXW])
        W3 = sb("W3", [128, D])
        b3 = sb("b3", [128, 1])
        lin_in = sb("lin_in", [128, D])
        linT = sb("linT", [128, D])
        eps_c = sb("eps_c", [128, 1])

        mean = sb("mean", [128, NT])
        var = sb("var", [128, NT])
        sd = sb("sd", [128, NT])
        rstd = sb("rstd", [128, NT])
        den = sb("den", [128, NT, H0])
        fm = sb("fm", [128, NT, H0])
        fmc = sb("fmc", [128, NT, H0])
        fd = sb("fd", [128, 2 * NT * H0])
        fe = sb("fe", [128, 2 * NT * H0])

        mT = sb("mT", [H0, 128])
        MT = sb("MT", [H0, 128])
        MprevT = sb("MprevT", [H0, 128])
        MM = sb("MM", [128, 2 * H0])
        md = sb("md", [128, 2 * H0])
        me = sb("me", [128, 2 * H0])
        Es = sb("Es", [128, D + H0])
        Gs = sb("Gs", [128, D + H0])
        EsT = sb("EsT", [128, 256])
        GsT = sb("GsT", [128, 256])
        CT = sb("CT", [128, 256])
        CTx = sb("CTx", [128, 256])
        carry_row = sb("carry_row", [128, W0])

        x_loaded, weights_loaded = sem("x_loaded"), sem("weights_loaded")
        al_loaded = [sem("al_loaded0"), sem("al_loaded1")]
        ends_loaded = [sem("dst_loaded"), sem("src_loaded")]
        shifted_ready, zeros_ready, rowinfo_zeroed = sem("shifted_ready"), sem("zeros_ready"), sem("rowinfo_zeroed")
        iotas_ready = sem("iotas_ready")
        dve_done = sem("dve_done")
        onehots_ready = [sem("onehots_ready0"), sem("onehots_ready1")]
        onehots_used = [sem("onehots_used0"), sem("onehots_used1")]
        rowinfo_scattered, rowinfo_loaded = sem("rowinfo_scattered"), sem("rowinfo_loaded")
        fetch_staged = [sem("fetch_staged0"), sem("fetch_staged1")]
        fetch_landed = [sem("fetch_landed0"), sem("fetch_landed1")]
        fetch_used = [sem("fetch_used0"), sem("fetch_used1")]
        fetch_chain = sem("fetch_chain")
        node_tables = sem("node_tables")
        stored_out = sem("stored_out")
        LS = {n: Signals(n, sem) for n in ("att0", "sum1", "att2", "sum3")}
        TS = {n: Signals(n, sem) for n in ("proj", "ffn", "typed", "gcn")}

        layers, attentions, sums = ("att0", "sum1", "att2", "sum3"), ("att0", "att2"), ("sum1", "sum3")
        norms = ("ln1", "ln2", "x0", "x1", "x2", "x3")
        turns = {"var": norms, "sd": norms, "steps": layers, "carry": layers, "CTx": layers, "C": layers,
                 "EG": layers, "table": sums, "m": attentions, "MM": attentions, "md": attentions,
                 "me": attentions, "fd": attentions, "fe": attentions, "MprevT": attentions}
        events = {}

        def event(name):
            family, _, turn = name.partition(" ")
            order = turns.get(family[2:])
            order = attentions if family == "V:EG" else order
            if order is None or turn not in order:
                family, turn, order = name.replace(" ", "_"), "", ("",)
            if family not in events:
                events[family] = sem("done_" + family.replace(":", "_"))
            return events[family], order.index(turn) + 1

        block = ctx.enter_context(nc.Block())

        def bc(ap, shape):
            return ap.to_broadcast(shape)

        def view(ap, spec, **kw):
            return ap.rearrange(spec, **kw)

        weight_loads = [(Wqkv[:, n * D:(n + 1) * D], a["L0_gnn_W" + "qkv"[n]]) for n in range(3)]
        weight_loads += [(W1[:, :], a["L0_gnn_W1"]), (W2[:, :, :], view(a["L0_gnn_W2"], "(c p) d -> p c d", p=128)),
                         (b1[:, :], view(a["L0_gnn_b1"], "(c p) -> p c", p=128)),
                         (pw[:, :], view(a["L0_gnn_prelu_w"], "(c p) -> p c", p=128)),
                         (b3[:, :], view(a["L3_gnn_b"], "(p o) -> p o", o=1)),
                         (ntype_i[:, 0:NT - 1], view(a["node_type_5"][0:(NT - 1) * 128], "(t p) -> p t", p=128)),
                         (ntype_i[0:LAST, NT - 1:NT], view(a["node_type_5"][(NT - 1) * 128:N], "(p o) -> p o", o=1)),
                         (Wt_in[:, :, :], view(a["L2_gnn_W_typed"], "t i o -> i t o")),
                         (Wcat[:, NTYPE * HXW:], a["L2_gnn_W_res"]), (W3[:, :], a["L3_gnn_W"]),
                         (lin_in[:, :], a["L3_gnn_lin_W"])]
        weight_loads += [(tile[:, :], a[n].partition_broadcast(128)) for n, tile in rows_in.items()]

        @block.sync
        def _(sp):
            sp.dma_start(view(edge_i[0:EP, :], "p c -> p c"), view(a["dst"], "(p c) -> p c", p=EP)).then_inc(ends_loaded[0], 16)
            sp.dma_start(X[:, 0:NT - 1, :], view(a["x"][0:(NT - 1) * 128, :], "(t p) d -> p t d", p=128)).then_inc(x_loaded, 16)
            sp.wait_ge(iotas_ready, 1)
            sp.dma_start(X[0:LAST, NT - 1, :], a["x"][(NT - 1) * 128:N, :]).then_inc(x_loaded, 16)
            flat = view(shifted, "a b -> (a b)")
            for s in range(SLOTS):
                at = s * RBW + SLOTS - s
                sp.dma_start(view(flat[at:at + E], "(p c) -> p c", p=EP), view(a["src"], "(p c) -> p c", p=EP)).then_inc(shifted_ready, 16)
                tail = flat[at + E:(s + 1) * RBW]
                sp.dma_start(view(tail, "(o c) -> o c", o=1), zeros[0:1, 0:tail.shape[0]].bitcast(I32)).then_inc(shifted_ready, 16)
            sp.dma_start(view(rowinfo_d, "(p i) c -> p (i c)", p=128), zeros[:, :]).then_inc(rowinfo_zeroed, 16)
            with nc.allow_non_contiguous_dma(reason="a few short parameter columns"):
                for tile, source in weight_loads:
                    sp.dma_start(tile, source).then_inc(weights_loaded, 16)
            sp.dma_start(al_in[:, :], view(a["L2_gnn_al_w"], "t i o -> (t i o)").partition_broadcast(128)).then_inc(al_loaded[0], 16)
            sp.wait_ge(rowinfo_scattered, 16 * NT)
            sp.dma_start(view(rowinfo[:, :, :], "p i c -> p (i c)"), view(rowinfo_d, "(p i) c -> p (i c)", p=128)).then_inc(rowinfo_loaded, 16)
            sp.wait_ge(*event("V:split0"))
            sp.dma_start(edge_i[0:EP, :], view(a["src"], "(p c) -> p c", p=EP)).then_inc(ends_loaded[1], 16)
            def tile_tables(S, parts):
                with sp.Fori(0, NT) as t:
                    sp.wait_ge(S["result"], t + 1)
                    for table, tile in parts:
                        sp.dma_start(table[bass.ds(t * 128, 128), :], tile).then_inc(S["written"], 16)
                sp.wait_ge(S["written"], 16 * NT * len(parts))

            def state_stores(name):
                S = LS[name]
                st = view(state_d[name], "(p i) w -> p i w", p=128)
                w = st.shape[2]
                with sp.Fori(0, HALF) as it:
                    for b in range(2):
                        sp.wait_ge(S["state_ready"], it * 2 + b + 1)
                        sp.dma_start(st[:, bass.ds(it * 2 + b, 1), :], state[b][:, 0:w]).then_inc(S[f"stored{b}"], 16)
                sp.wait_ge(*event("V:carry " + name))
                sp.dma_start(carry_d[name], carry_row[:, 0:w]).then_inc(S["carry_stored"], 16)

            def whole_table(name, k):
                sp.wait_ge(*event("V:table " + name))
                sp.dma_start(view(y_d[k], "(t p) d -> p t d", p=128), T1[:, :, :]).then_inc(LS[name]["table"], 16)

            tile_tables(TS["proj"], [(q_d, proj[:, 0:D]), (kv_d, proj[:, D:])])
            sp.wait_ge(*event("V:al0"))
            sp.dma_start(al_in[:, :], view(a["L2_gnn_ar_w"], "t i o -> (t i o)").partition_broadcast(128)).then_inc(al_loaded[1], 16)
            state_stores("att0")
            whole_table("sum1", 0)
            state_stores("sum1")
            tile_tables(TS["typed"], [(h_d, hx2[:, 0:D + H2]), (hr_d, hx2[:, D + H2:])])
            state_stores("att2")
            whole_table("sum3", 1)
            state_stores("sum3")
            sp.wait_ge(*event("V:x3"))
            sp.dma_start(view(out[0:(NT - 1) * 128, :], "(t p) d -> p t d", p=128), X[:, 0:NT - 1, :]).then_inc(stored_out, 16)
            sp.dma_start(out[(NT - 1) * 128:N, :], X[0:LAST, NT - 1, :]).then_inc(stored_out, 16)
            sp.wait_ge(stored_out, 32)

        @block.gpsimd
        def _(pool):
            nc.gpsimd.memset(X[:, NT - 1, :], 0.0)
            nc.gpsimd.memset(ntype_i[:, NT - 1:NT], 0)
            nc.gpsimd.memset(zeros[:, :], 0.0)
            nc.gpsimd.iota(iota_i[:, :], pattern=[[1, 128]], base=0, channel_multiplier=0)
            nc.gpsimd.iota(view(iota_hi_i[:, :], "p (a b) -> p a b", a=2), pattern=[[1, 2], [2, NT]], base=0, channel_multiplier=0)
            nc.gpsimd.iota(node_i[:, :], pattern=[[128, NT]], base=0, channel_multiplier=1)
            nc.gpsimd.iota(row_i[:, :], pattern=[[1, STEPS]], base=0, channel_multiplier=STEPS)
            nc.gpsimd.iota(part_id_i[:, :], pattern=[[0, 1]], base=0, channel_multiplier=1).then_inc(iotas_ready, 1)

            pool.wait_ge(rowinfo_zeroed, 16)
            pool.wait_ge(*event("V:info"))
            for t in range(NT):
                nc.gpsimd.indirect_dma_start(out=rowinfo_d, out_offset=bass.IndirectOffsetOnAxis(ap=row0_i[:, t:t + 1], axis=0),
                                             in_=info[:, t, :], in_offset=None).then_inc(rowinfo_scattered, 16)
            with pool.Fori(1, FIT + 1) as use:
                for b in range(2):
                    pool.wait_ge(shifted_ready, 32 * SLOTS)
                    pool.wait_ge(fetch_staged[b], use)
                    pool.wait_ge(fetch_used[b], use)
                    for k in range(FS):
                        nc.gpsimd.indirect_dma_start(out=fetched[b][:, k * SLOTS:(k + 1) * SLOTS], out_offset=None, in_=shifted,
                                                     in_offset=bass.IndirectOffsetOnAxis(ap=fetch_row[b][:, k:k + 1], axis=0)).then_inc(fetch_landed[b], 16)

            def steps(name, table, side, table_written):
                S = LS[name]
                w = table.shape[1]
                with pool.Fori(1, HALF + 1) as use:
                    for b in range(2):
                        pool.wait_ge(*table_written)
                        pool.wait_ge(S[f"index{b}"], use)
                        pool.wait_ge(S[f"free{b}"], use)
                        if side is not None:
                            nc.gpsimd.indirect_dma_start(out=dst_row[b][:, 0:side.shape[1]], out_offset=None, in_=side,
                                                         in_offset=bass.IndirectOffsetOnAxis(ap=index_cols[b][:, SLOTS:SLOTS + 1], axis=0)).then_inc(S[f"landed{b}"], 16)
                        for j in range(SLOTS):
                            nc.gpsimd.indirect_dma_start(out=gathered[b][:, j * w:(j + 1) * w], out_offset=None, in_=table,
                                                         in_offset=bass.IndirectOffsetOnAxis(ap=index_cols[b][:, j:j + 1], axis=0)).then_inc(S[f"landed{b}"], 16)
                w = state_d[name].shape[1]
                pool.wait_ge(S["stored0"], 16 * HALF)
                pool.wait_ge(S["stored1"], 16 * HALF)
                for t in range(NT):
                    nc.gpsimd.indirect_dma_start(out=final_state[:, t * w:(t + 1) * w], out_offset=None, in_=state_d[name],
                                                 in_offset=bass.IndirectOffsetOnAxis(ap=last_i[:, t:t + 1], axis=0)).then_inc(S["final_landed"], 16)
                pool.wait_ge(S["carry_stored"], 16)
                for t in range(NT):
                    nc.gpsimd.indirect_dma_start(out=final_carry[:, t * w:(t + 1) * w], out_offset=None, in_=carry_d[name],
                                                 in_offset=bass.IndirectOffsetOnAxis(ap=lane_i[:, t:t + 1], axis=0)).then_inc(S["final_landed"], 16)

            steps("att0", kv_d, q_d, (TS["proj"]["written"], 32 * NT))
            steps("sum1", y_d[0], None, (LS["sum1"]["table"], 16))
            steps("att2", h_d, hr_d, (TS["typed"]["written"], 32 * NT))
            steps("sum3", y_d[1], None, (LS["sum3"]["table"], 16))

        @block.scalar
        def _(act):
            def done(ins, name):
                ins.then_inc(event("A:" + name)[0], 1)

            def turn(S, source):
                def one(t):
                    act.wait_ge(S["turned"], t)
                    nc.scalar.copy(xs[:, :], source[:, bass.ds(t, 1), :]).then_inc(S["staged"], 1)
                    act.wait_ge(S["turned"], t + 1)
                    act.wait_ge(S["first"], t)
                    nc.scalar.copy(xT[:, :], ps[0][:, 0:128]).then_inc(S["xT"], 1)
                return one

            def sqrt_var(name):
                act.wait_ge(*event("V:var " + name))
                done(nc.scalar.activation(sd[:, :], var[:, :], ACT.Sqrt, bias=eps_c[:, 0:1]), "sd " + name)

            def steps(name, H, scale):
                S = LS[name]
                per = 16 * (SLOTS + (1 if H else 0))
                for b in range(2):
                    nc.scalar.copy(index_cols[b][:, :], IX[:, b, :]).then_inc(S[f"index{b}"], 1)
                with act.Fori(0, HALF) as it:
                    for b in range(2):
                        act.wait_ge(S[f"landed{b}"], (it + 1) * per)
                        nc.scalar.copy(index_cols[b][:, :], IX[:, bass.ds(it * 2 + (b + 2), 1), :]).then_inc(S[f"index{b}"], 1)
                        if H:
                            act.wait_ge(S["diffs"], it * 2 + b + 1)
                            nc.scalar.activation(expd[:, 0:(SLOTS + 1) * H], diff[:, 0:(SLOTS + 1) * H], ACT.Exp, scale=scale).then_inc(S["exps"], 1)
                if H:
                    act.wait_ge(*event("V:md " + name))
                    done(nc.scalar.activation(me[:, 0:2 * H], md[:, 0:2 * H], ACT.Exp, scale=scale), "me " + name)
                    act.wait_ge(*event("V:fd " + name))
                    done(nc.scalar.activation(fe[:, 0:2 * NT * H], fd[:, 0:2 * NT * H], ACT.Exp, scale=scale), "fe " + name)

            act.wait_ge(x_loaded, 32)
            one = turn(TS["proj"], X)
            with act.Fori(0, NT) as t:
                one(t)
            act.wait_ge(*event("V:table rows"))
            with act.Fori(0, FIT) as it:
                for b in range(2):
                    act.wait_ge(fetch_landed[b], it * (16 * FS))
                    nc.scalar.copy(fetch_row[b][:, :], table_row[:, bass.ds(it * (2 * FS) + b * FS, FS)]).then_inc(fetch_staged[b], 1)

            for k in (0, 1):
                act.wait_ge(*event(f"V:deg{k}"))
                done(nc.scalar.activation(sd[:, :], var[:, :], ACT.Sqrt), f"sqrt deg{k}")
            act.wait_ge(*event("V:IX"))
            steps("att0", H0, float(1.0 / (D ** 0.5)))
            sqrt_var("ln1")
            act.wait_ge(*event("V:ln1"))
            one = turn(TS["ffn"], R)
            with act.Fori(0, NT) as t:
                one(t)
            sqrt_var("ln2")
            sqrt_var("x0")
            steps("sum1", 0, 1.0)
            sqrt_var("x1")
            act.wait_ge(*event("V:x1"))
            one = turn(TS["typed"], X)
            with act.Fori(0, NT) as t:
                one(t)
                act.wait_ge(TS["typed"]["first"], t + 1)
                nc.scalar.copy(R[:, bass.ds(t, 1), :], ps[5][:, 0:D]).then_inc(TS["typed"]["second"], 1)
            steps("att2", H2, 1.0)
            sqrt_var("x2")
            steps("sum3", 0, 1.0)
            act.wait_ge(*event("V:agg3"))
            one = turn(TS["gcn"], R)
            with act.Fori(0, NT) as t:
                one(t)
                S = TS["gcn"]
                act.wait_ge(S["first"], t + 1)
                act.wait_ge(S["second"], t)
                nc.scalar.activation(hT[:, 0:128], ps[1][:, 0:128], ACT.Relu, bias=b3[:, 0:1]).then_inc(S["hidden"], 1)
            sqrt_var("x3")

        @block.tensor
        def _(pe):
            def done(ins, name):
                ins.then_inc(event("P:" + name)[0], 1)

            def histogram(k):
                pe.wait_ge(*event("V:consts" if k == 0 else "V:deg rows"))
                for u in range(2):
                    nc.tensor.matmul(ps[3 + k][LO * u:LO * (u + 1), 0:NT], zero_b[:, 0:LO], zero_b[:, 0:NT], start=True, stop=False)
                with pe.Fori(0, NB) as it:
                    for b in range(2):
                        pe.wait_ge(onehots_ready[b], it + (1 + k * NB))
                        for c in range(HA[b]):
                            for u in range(2):
                                mm = nc.tensor.matmul(ps[3 + k][LO * u:LO * (u + 1), 0:NT], oh_lo[b][0:EP, c, :],
                                                      oh_hi[b][0:EP, c, u * NT:(u + 1) * NT], start=False, stop=False)
                        mm.then_inc(onehots_used[b], 1)
                for u in range(2):
                    mm = nc.tensor.matmul(ps[3 + k][LO * u:LO * (u + 1), 0:NT], zero_b[:, 0:LO], zero_b[:, 0:NT], start=False, stop=True)
                done(mm, f"hist{k}")

            histogram(0)
            pe.wait_ge(*event("V:deg rows"))
            nc.tensor.matmul(ps[0][:, 0:2 * NT], before[:, :], deg_rows[:, :], start=True, stop=True)
            done(nc.tensor.matmul(ps[1][:, 0:2 * NT], ones[:, :], deg_rows[:, :], start=True, stop=True), "sums")
            def turn(S, t):
                pe.wait_ge(S["staged"], t + 1)
                pe.wait_ge(S["xT"], t)
                nc.tensor.transpose(ps[0][:, 0:128], xs[:, :], ident[:, :]).then_inc(S["turned"], 1)
                pe.wait_ge(S["xT"], t + 1)

            S = TS["proj"]
            pe.wait_ge(*event("V:info"))
            pe.wait_ge(weights_loaded, 16 * len(weight_loads))
            with pe.Fori(0, NT) as t:
                turn(S, t)
                pe.wait_ge(S["result"], t)
                nc.tensor.matmul(ps[1][:, 0:3 * D], xT[:, :], Wqkv[:, :], start=True, stop=True).then_inc(S["first"], 1)
            pe.wait_ge(*event("V:lane top"))
            done(nc.tensor.transpose(ps[0][0:4, 0:128], carry4[:, :], ident[:, :]), "lane top")
            pe.wait_ge(*event("V:lane excl"))
            done(nc.tensor.transpose(ps[0][:, 0:4], lane_excl[:, :], ident[0:4, 0:4]), "lane excl")
            pe.wait_ge(*event("V:cont"))
            nc.tensor.transpose(ps[0][0:H0, 0:128], penalty[:, :], ident[:, :])
            done(nc.tensor.transpose(ps[1][:, 0:128], wide[:, :], ident[:, :]), "cont")
            pe.wait_ge(*event("V:contT"))

            histogram(1)

            def carries(name, H):
                F = D + H
                if H:
                    pe.wait_ge(*event("V:steps " + name))
                    done(nc.tensor.transpose(ps[0][0:H, 0:128], state[1][:, F:F + H], ident[:, :]), "m " + name)
                    pe.wait_ge(*event("V:MprevT " + name))
                    nc.tensor.transpose(ps[0][:, 0:H], MT[0:H, :], ident[0:H, 0:H])
                    done(nc.tensor.transpose(ps[0][:, H:2 * H], MprevT[0:H, :], ident[0:H, 0:H]), "MM " + name)
                if H:
                    pe.wait_ge(*event("V:EG " + name))
                    nc.tensor.transpose(ps[1][:, 0:128], Es[:, 0:D], ident[:, :])
                    nc.tensor.transpose(ps[1][0:H, 128:256], Es[:, D:F], ident[:, :])
                    nc.tensor.transpose(ps[2][:, 0:128], Gs[:, 0:D], ident[:, :])
                    done(nc.tensor.transpose(ps[2][0:H, 128:256], Gs[:, D:F], ident[:, :]), "EG " + name)
                else:
                    pe.wait_ge(*event("V:steps " + name))
                    done(nc.tensor.transpose(ps[1][:, 0:128], state[1][:, 0:D], ident[:, :]), "EG " + name)
                pe.wait_ge(*event("V:CTx " + name))
                mm = nc.tensor.transpose(ps[0][:, 0:D], CTx[:, 0:128], ident[:, :])
                if H:
                    mm = nc.tensor.transpose(ps[0][:, D:F], CTx[0:H, 128:256], ident[0:H, 0:H])
                done(mm, "C " + name)

            carries("att0", H0)
            S = TS["ffn"]
            with pe.Fori(0, NT) as t:
                turn(S, t)
                pe.wait_ge(S["hidden"], t)
                for c in range(FC):
                    mm = nc.tensor.matmul(ps[1][:, c * 128:(c + 1) * 128], W1[:, c * 128:(c + 1) * 128], xT[:, :], start=True, stop=True)
                mm.then_inc(S["first"], 1)
                pe.wait_ge(S["hidden"], t + 1)
                pe.wait_ge(S["result"], t)
                for c in range(FC):
                    mm = nc.tensor.matmul(ps[2][:, 0:D], hT[:, c * 128:(c + 1) * 128], W2[:, c, :], start=(c == 0), stop=(c == FC - 1))
                mm.then_inc(S["second"], 1)
            carries("sum1", 0)
            S = TS["typed"]
            pe.wait_ge(*event("V:Wcat"))
            with pe.Fori(0, NT) as t:
                turn(S, t)
                pe.wait_ge(S["result"], t)
                pe.wait_ge(S["second"], t)
                nc.tensor.matmul(ps[1][:, 0:3 * HXW], xT[:, :], Wcat[:, 0:3 * HXW], start=True, stop=True)
                nc.tensor.matmul(ps[2][:, 0:2 * HXW], xT[:, :], Wcat[:, 3 * HXW:5 * HXW], start=True, stop=True)
                nc.tensor.matmul(ps[5][:, 0:D], xT[:, :], Wcat[:, 5 * HXW:], start=True, stop=True).then_inc(S["first"], 1)
            carries("att2", H2)
            pe.wait_ge(*event("V:x2"))
            done(nc.tensor.transpose(ps[0][:, 0:128], lin_in[:, :], ident[:, :]), "linT")
            carries("sum3", 0)
            S = TS["gcn"]
            with pe.Fori(0, NT) as t:
                turn(S, t)
                pe.wait_ge(S["hidden"], t)
                nc.tensor.matmul(ps[1][:, 0:128], W3[:, :], xT[:, :], start=True, stop=True).then_inc(S["first"], 1)
                pe.wait_ge(S["hidden"], t + 1)
                pe.wait_ge(S["result"], t)
                nc.tensor.matmul(ps[2][:, 0:D], hT[:, 0:128], linT[:, :], start=True, stop=True).then_inc(S["second"], 1)

        @block.vector
        def _(dve):
            v = nc.vector
            n_done = [0]

            def done(ins, name=None):
                if name:
                    ins.then_inc(event("V:" + name)[0], 1)
                    dve.wait_ge(*event("V:" + name))
                else:
                    n_done[0] += 1
                    ins.then_inc(dve_done, 1)
                    dve.wait_ge(dve_done, n_done[0])

            def after_pe(name):
                dve.wait_ge(*event("P:" + name))

            def after_act(name):
                dve.wait_ge(*event("A:" + name))

            dve.wait_ge(iotas_ready, 1)
            done(v.tensor_copy(iota_f[:, :], iota_i[:, :]))
            v.tensor_copy(iota_lo_b[:, :], iota_i[:, 0:LO])
            v.tensor_copy(iota_hi_b[:, :], iota_hi_i[:, :])
            v.tensor_copy(row_f[:, :], row_i[:, :])
            done(v.tensor_copy(part_id[:, :], part_id_i[:, :]))
            v.tensor_scalar(ident[:, :], iota_f[:, :], part_id[:, 0:1], None, ALU.is_equal)
            v.tensor_scalar(before[:, :], iota_f[:, :], part_id[:, 0:1], None, ALU.is_gt)
            v.tensor_scalar(row_ok[:, :], part_id[:, :], float(LAST), None, ALU.is_lt)
            v.memset(ones[:, :], 1.0)
            v.memset(eps_c[:, :], EPS)
            v.memset(IX[:, STEPS:STEPS + 2, :], 0.0)
            done(v.memset(zero_b[:, :], 0.0), "consts")

            def histogram(k):
                dve.wait_ge(ends_loaded[k], 16)
                done(v.tensor_scalar(part_i[0:EP, :], edge_i[0:EP, :], LO - 1, None, ALU.bitwise_and))
                done(v.tensor_copy(lo_b[0:EP, :], part_i[0:EP, :]))
                done(v.tensor_scalar(part_i[0:EP, :], edge_i[0:EP, :], LO.bit_length() - 1, None, ALU.arith_shift_right), f"split{k}")
                done(v.tensor_copy(hi_b[0:EP, :], part_i[0:EP, :]))
                with dve.Fori(0, NB) as it:
                    for b in range(2):
                        n = HA[b]
                        if k == 0:
                            dve.wait_ge(onehots_used[b], it)
                        else:
                            dve.wait_ge(onehots_used[b], it + NB)
                        at = it * BATCH + b * HA[0]
                        for oh, iota, part in ((oh_lo, iota_lo_b, lo_b), (oh_hi, iota_hi_b, hi_b)):
                            w = oh[b].shape[2]
                            ins = v.tensor_tensor(oh[b][0:EP, :, :], bc(iota[0:EP, :].unsqueeze(1), [EP, n, w]),
                                                  bc(part[0:EP, bass.ds(at, n)].unsqueeze(2), [EP, n, w]), ALU.is_equal)
                        ins.then_inc(onehots_ready[b], 1)
                dve.wait_ge(*event(f"P:hist{k}"))

            histogram(0)
            done(v.tensor_copy(deg_rows[:, 0:NT], ps[3][:, 0:NT]))
            done(v.tensor_scalar(deg_rows[:, NT:], deg_rows[:, 0:NT], float(SLOTS - 1), None, ALU.add))
            done(v.tensor_copy(small_i[:, 0:NT], deg_rows[:, NT:]))
            done(v.tensor_scalar(small_i[:, NT:], small_i[:, 0:NT], SLOTS.bit_length() - 1, None, ALU.arith_shift_right))
            done(v.tensor_copy(deg_rows[:, NT:], small_i[:, NT:]))
            done(v.tensor_scalar(deg_rows[:, NT:], deg_rows[:, NT:], 1.0, None, ALU.max), "deg rows")
            after_pe("sums")
            done(v.tensor_copy(tot[:, :], ps[1][:, 0:2 * NT]))
            for u in range(2):
                s = slice(u * NT, (u + 1) * NT)
                done(v.tensor_tensor_scan(incl[:, s], ones[:, 0:NT], tot[:, s], 0.0, ALU.mult, ALU.add))
            done(v.tensor_tensor(incl[:, :], incl[:, :], tot[:, :], ALU.subtract))
            done(v.tensor_tensor(starts[:, :], incl[:, :], ps[0][:, 0:2 * NT], ALU.add))
            v.tensor_copy(info[:, :, 0], node_i[:, :])
            v.tensor_copy(info[:, :, 1], starts[:, 0:NT])
            v.tensor_copy(info[:, :, 2], starts[:, NT:])
            v.tensor_tensor(info[:, :, 3], starts[:, 0:NT], deg_rows[:, 0:NT], ALU.add)
            done(v.tensor_copy(row0_i[:, :], starts[:, NT:]), "info")
            done(v.tensor_tensor(last_f[:, :], starts[:, NT:], deg_rows[:, NT:], ALU.add))
            done(v.tensor_scalar(last_f[:, :], last_f[:, :], -1.0, None, ALU.add))
            done(v.tensor_scalar(lane1_f[:, :], last_f[:, :], 0.5, 1.0 / STEPS, ALU.add, ALU.mult))
            done(v.tensor_scalar(lane1_f[:, :], lane1_f[:, :], -0.5, ROUND, ALU.add, ALU.add))
            done(v.tensor_scalar(lane_f[:, :], lane1_f[:, :], -ROUND, None, ALU.add))
            v.tensor_copy(last_i[:, :], last_f[:, :])
            v.tensor_copy(lane_i[:, :], lane_f[:, :])
            done(v.tensor_scalar(lane1_f[:, :], lane_f[:, :], float(STEPS), None, ALU.mult))
            done(v.tensor_tensor(has[:, :], starts[:, NT:], lane1_f[:, :], ALU.is_lt))
            done(v.tensor_scalar(has_bound[:, :], has[:, :], 0.5, 2 * BIG, ALU.subtract, ALU.mult))

            S = TS["proj"]
            with dve.Fori(0, NT) as t:
                dve.wait_ge(S["first"], t + 1)
                dve.wait_ge(S["written"], t * 32)
                v.tensor_copy(proj[:, 0:2 * D], ps[1][:, 0:2 * D])
                v.tensor_copy(view(proj[:, 2 * D:], "p (d h) -> p h d", h=H0),
                              view(ps[1][:, 2 * D:3 * D], "p (h d) -> p h d", h=H0)).then_inc(S["result"], 1)

            dve.wait_ge(rowinfo_loaded, 16)
            for c in range(4):
                last = v.tensor_tensor_scan(RS[:, c, :], rowinfo[:, :, c], rowinfo[:, :, c], 0.0, ALU.max, ALU.max)
            done(last)
            done(v.tensor_copy(carry4[:, :], RS[:, :, STEPS - 1]), "lane top")
            after_pe("lane top")
            done(v.tensor_copy(lane_in[:, :], ps[0][0:4, 0:128]))
            done(v.tensor_tensor_scan(lane_top[:, :], lane_in[:, :], lane_in[:, :], 0.0, ALU.max, ALU.max))
            v.memset(lane_excl[:, 0:1], 0.0)
            done(v.tensor_copy(lane_excl[:, 1:128], lane_top[:, 0:127]), "lane excl")
            after_pe("lane excl")
            done(v.tensor_copy(carry4[:, :], ps[0][:, 0:4]))
            for c in range(4):
                last = v.tensor_scalar(RS[:, c, :], RS[:, c, :], carry4[:, c:c + 1], None, ALU.max)
            done(last)
            row_node, row_start, row_first, row_end = (RS[:, c, :] for c in range(4))
            done(v.tensor_tensor(pos[:, :], row_f[:, :], row_first, ALU.subtract))
            done(v.tensor_scalar(pos[:, :], pos[:, :], float(SLOTS), None, ALU.mult))
            done(v.tensor_tensor(pos[:, :], pos[:, :], row_start, ALU.add))
            done(v.tensor_scalar(low_f[:, :], pos[:, :], float(E), None, ALU.min))
            done(v.tensor_copy(pos_i[:, :], low_f[:, :]))
            v.tensor_scalar(low_i[:, :], pos_i[:, :], SLOTS - 1, None, ALU.bitwise_and)
            done(v.tensor_scalar(high_i[:, :], pos_i[:, :], SLOTS.bit_length() - 1, None, ALU.arith_shift_right))
            v.tensor_copy(low_f[:, :], low_i[:, :])
            done(v.tensor_copy(high_f[:, :], high_i[:, :]))
            done(v.tensor_scalar(low_f[:, :], low_f[:, :], float(RB), 1.0, ALU.mult, ALU.add))
            done(v.tensor_tensor(table_row[:, :], low_f[:, :], high_f[:, :], ALU.add), "table rows")
            done(v.tensor_tensor(BOUND[:, :, :], bc(pos[:, :].unsqueeze(2), [128, STEPS, SLOTS]),
                                 bc(iota_f[:, 0:SLOTS].unsqueeze(1), [128, STEPS, SLOTS]), ALU.add))
            done(v.tensor_tensor(VALID[:, :, :], BOUND[:, :, :], bc(row_end.unsqueeze(2), [128, STEPS, SLOTS]), ALU.is_lt))
            done(v.tensor_scalar(BOUND[:, :, :], VALID[:, :, :], 0.5, 2 * BIG, ALU.subtract, ALU.mult))
            v.memset(same[:, 0:1], 0.0)
            done(v.tensor_tensor(same[:, 1:], RS[:, 0, 1:STEPS], RS[:, 0, 0:STEPS - 1], ALU.is_equal))
            v.tensor_scalar(same_bound[:, :], same[:, :], 0.5, 2 * BIG, ALU.subtract, ALU.mult)
            v.tensor_tensor(cont[:, :], RS[:, 0, 0:1], RS[:, 0, STEPS - 1:STEPS], ALU.is_equal)
            done(v.tensor_tensor(cont2[:, :], RS[:, 0, 0:1], carry4[:, 0:1], ALU.is_equal))
            done(v.tensor_tensor(cont[:, :], cont[:, :], cont2[:, :], ALU.mult))
            done(v.tensor_scalar(cont2[:, :], cont[:, :], 1.0, BIG, ALU.subtract, ALU.mult))
            v.tensor_copy(penalty[:, :], bc(cont2[:, 0:1], [128, H0]))
            done(v.tensor_copy(wide[:, :], bc(cont[:, 0:1], [128, 128])), "cont")
            after_pe("cont")
            v.tensor_copy(penaltyT[:, :], ps[0][0:H0, 0:128])
            done(v.tensor_copy(contT[:, :], ps[1][:, 0:128]), "contT")
            for b in range(2):
                v.memset(fetched_f[:, :, :], 0.0).then_inc(fetch_used[b], 1)
                dve.wait_ge(fetch_used[b], 1)

            with dve.Fori(0, FIT) as it:
                for b in range(2):
                    dve.wait_ge(fetch_landed[b], (it + 1) * (16 * FS))
                    at = it * (2 * FS) + b * FS
                    v.tensor_scalar(fetched_f[:, :, :], view(fetched[b][:, :], "p (k s) -> p k s", s=SLOTS), -float(N), None, ALU.add).then_inc(fetch_chain, 1)
                    dve.wait_ge(fetch_chain, it * 4 + (2 * b + 1))
                    v.tensor_tensor(fetched_f[:, :, :], fetched_f[:, :, :], VALID[:, bass.ds(at, FS), :], ALU.mult).then_inc(fetch_chain, 1)
                    dve.wait_ge(fetch_chain, it * 4 + (2 * b + 2))
                    v.tensor_scalar(IX[:, bass.ds(at, FS), 0:SLOTS], fetched_f[:, :, :], float(N), None, ALU.add).then_inc(fetch_used[b], 1)
                    dve.wait_ge(fetch_used[b], it + 2)
            done(v.tensor_copy(IX[:, 0:STEPS, SLOTS], row_node), "IX")

            histogram(1)
            done(v.tensor_copy(outdeg[:, :], ps[4][:, 0:NT]))
            for k, deg in ((0, outdeg[:, :]), (1, deg_rows[:, 0:NT])):
                if k:
                    after_act("sqrt deg0")
                done(v.tensor_scalar(var[:, :], deg, 1.0, None, ALU.add), f"deg{k}")
                after_act(f"sqrt deg{k}")
                done(v.reciprocal(dis[k][:, :], sd[:, :]))
            dve.wait_ge(weights_loaded, 16 * len(weight_loads))
            for g in range(2):
                dve.wait_ge(al_loaded[g], 16)
                done(v.tensor_reduce(alr[:, g, :, :], view(al_in[:, :], "p (t i o) -> p t i o", t=NTYPE, i=32), AX.X, ALU.add), f"al{g}")
            for t in range(NTYPE):
                v.tensor_copy(view(Wcat[:, t * HXW:t * HXW + D], "p (k h) -> p h k", h=H2), view(Wt_in[:, t, :], "p (h k) -> p h k", h=H2))
                for g in range(2):
                    done(v.tensor_tensor(view(Wprod[:, :], "p (h k) -> p h k", h=H2), view(Wt_in[:, t, :], "p (h k) -> p h k", h=H2),
                                         bc(alr[:, g, t, :].unsqueeze(1), [128, H2, 32]), ALU.mult))
                    done(v.tensor_reduce(Wcat[:, t * HXW + D + g * H2:t * HXW + D + (g + 1) * H2],
                                         view(Wprod[:, :], "p (h k) -> p h k", h=H2), AX.X, ALU.add), "Wcat" if (t, g) == (NTYPE - 1, 1) else None)
            done(v.tensor_copy(ntype_f[:, :], ntype_i[:, :]))
            for t in range(NTYPE):
                last = v.tensor_scalar(type_mask[:, :, t], ntype_f[:, :], float(t), None, ALU.is_equal)
            done(last)

            def attention_steps(name, H, U, dot):
                S = LS[name]
                F = D + H
                rw = 2 * D if dot else D + H
                n_chain = [0]
                per = 7 if dot else 8
                for b in range(2):
                    v.memset(state[b][:, 0:F + H], 0.0).then_inc(S[f"free{b}"], 1)
                    dve.wait_ge(S[f"free{b}"], 1)
                with dve.Fori(0, HALF) as it:
                    def link(ins):
                        n_chain[0] += 1
                        ins.then_inc(S["chain"], 1)
                        dve.wait_ge(S["chain"], it * (2 * per) + n_chain[0])

                    for b in range(2):
                        new, old = state[b], state[1 - b]
                        g = view(gathered[b][:, 0:SLOTS * rw], "p (j w) -> p j w", w=rw)
                        sc = scores[:, :, 0:H]
                        i = it * 2 + b
                        dve.wait_ge(S[f"landed{b}"], (it + 1) * (16 * (SLOTS + 1)))
                        if dot:
                            link(v.tensor_tensor(prod[:, :, :], g[:, :, 0:D], bc(dst_row[b][:, :].unsqueeze(1), [128, SLOTS, D]), ALU.mult))
                            link(v.tensor_reduce(sc, view(prod[:, :, :], "p j (h u) -> p j h u", h=H), AX.X, ALU.add))
                            value = g[:, :, D:]
                        else:
                            link(v.tensor_tensor(sc, g[:, :, D:], bc(dst_row[b][:, 0:H].unsqueeze(1), [128, SLOTS, H]), ALU.add))
                            link(v.tensor_scalar(prod[:, :, 0:H], sc, 0.2, None, ALU.mult))
                            link(v.tensor_tensor(sc, sc, prod[:, :, 0:H], ALU.max))
                            value = g[:, :, 0:D]
                        link(v.tensor_tensor(sc, sc, bc(BOUND[:, bass.ds(i, 1), :].rearrange("p o j -> p (o j)").unsqueeze(2), [128, SLOTS, H]), ALU.min))
                        link(v.tensor_reduce(top[:, 0:H], view(sc, "p j h -> p h j"), AX.X, ALU.max))
                        dve.wait_ge(S[f"stored{b}"], it * 16)
                        link(v.scalar_tensor_tensor(new[:, F:F + H], old[:, F:F + H], same_bound[:, bass.ds(i, 1)], top[:, 0:H], ALU.min, ALU.max))
                        v.scalar_tensor_tensor(diff[:, 0:H], old[:, F:F + H], same_bound[:, bass.ds(i, 1)], new[:, F:F + H], ALU.min, ALU.subtract)
                        v.tensor_tensor(view(diff[:, H:(SLOTS + 1) * H], "p (j h) -> p j h", h=H), sc,
                                        bc(new[:, F:F + H].unsqueeze(1), [128, SLOTS, H]), ALU.subtract).then_inc(S["diffs"], 1)
                        dve.wait_ge(S["exps"], i + 1)
                        m = view(msg[:, 0:SLOTS * F], "p (j f) -> p j f", f=F)
                        link(v.tensor_tensor(m[:, :, D:], view(expd[:, H:(SLOTS + 1) * H], "p (j h) -> p j h", h=H),
                                             bc(VALID[:, bass.ds(i, 1), :].rearrange("p o j -> p (o j)").unsqueeze(2), [128, SLOTS, H]), ALU.mult))
                        v.tensor_tensor(view(m[:, :, 0:D], "p j (u h) -> p j u h", h=H), view(value, "p j (u h) -> p j u h", h=H),
                                        bc(m[:, :, D:].unsqueeze(2), [128, SLOTS, U, H]), ALU.mult).then_inc(S[f"free{b}"], 1)
                        dve.wait_ge(S[f"free{b}"], it + 2)
                        v.tensor_reduce(slot_sum[:, 0:F], view(m, "p j f -> p f j"), AX.X, ALU.add)
                        link(v.scalar_tensor_tensor(view(scaled[:, 0:F], "p (u h) -> p u h", h=H), view(old[:, 0:F], "p (u h) -> p u h", h=H),
                                                    same[:, bass.ds(i, 1)], bc(expd[:, 0:H].unsqueeze(1), [128, U + 1, H]), ALU.mult, ALU.mult))
                        v.tensor_tensor(new[:, 0:F], scaled[:, 0:F], slot_sum[:, 0:F], ALU.add).then_inc(S["state_ready"], 1)
                        dve.wait_ge(S["state_ready"], i + 1)
                assert n_chain[0] == 2 * per

            def sum_steps(name):
                S = LS[name]
                for b in range(2):
                    v.memset(state[b][:, 0:D], 0.0).then_inc(S[f"free{b}"], 1)
                    dve.wait_ge(S[f"free{b}"], 1)
                with dve.Fori(0, HALF) as it:
                    for b in range(2):
                        i = it * 2 + b
                        g = view(gathered[b][:, 0:SLOTS * D], "p (j w) -> p w j", w=D)
                        dve.wait_ge(S[f"landed{b}"], (it + 1) * (16 * SLOTS))
                        v.tensor_reduce(slot_sum[:, 0:D], g, AX.X, ALU.add).then_inc(S[f"free{b}"], 1)
                        dve.wait_ge(S[f"free{b}"], it + 2)
                        dve.wait_ge(S[f"stored{b}"], it * 16)
                        v.scalar_tensor_tensor(state[b][:, 0:D], state[1 - b][:, 0:D], same[:, bass.ds(i, 1)], slot_sum[:, 0:D], ALU.mult, ALU.add).then_inc(S["state_ready"], 1)
                        dve.wait_ge(S["state_ready"], i + 1)

            def carries(name, H, U):
                F = D + H
                end = state[1]
                done(v.memset(CTx[:, :], 0.0), "steps " + name)
                if H:
                    after_pe("m " + name)
                    done(v.tensor_copy(mT[0:H, :], ps[0][0:H, 0:128]))
                    done(v.tensor_tensor_scan(MT[0:H, :], penaltyT[0:H, :], mT[0:H, :], -BIG, ALU.add, ALU.max))
                    v.memset(MprevT[0:H, 0:1], -BIG)
                    done(v.tensor_copy(MprevT[0:H, 1:128], MT[0:H, 0:127]), "MprevT " + name)
                    after_pe("MM " + name)
                    done(v.tensor_copy(MM[:, 0:2 * H], ps[0][:, 0:2 * H]))
                    v.tensor_tensor(md[:, 0:H], end[:, F:F + H], MM[:, 0:H], ALU.subtract)
                    done(v.scalar_tensor_tensor(md[:, H:2 * H], MM[:, H:2 * H], cont2[:, 0:1], MM[:, 0:H], ALU.add, ALU.subtract), "md " + name)
                    after_act("me " + name)
                    done(v.tensor_scalar(me[:, H:2 * H], me[:, H:2 * H], cont[:, 0:1], None, ALU.mult))
                    v.tensor_tensor(view(Es[:, 0:F], "p (u h) -> p u h", h=H), view(end[:, 0:F], "p (u h) -> p u h", h=H),
                                    bc(me[:, 0:H].unsqueeze(1), [128, U + 1, H]), ALU.mult)
                    done(v.tensor_copy(view(Gs[:, 0:F], "p (u h) -> p u h", h=H), bc(me[:, H:2 * H].unsqueeze(1), [128, U + 1, H])), "EG " + name)
                after_pe("EG " + name)
                done(v.tensor_copy(EsT[:, 0:128], ps[1][:, 0:128]))
                if H:
                    v.tensor_copy(EsT[0:H, 128:256], ps[1][0:H, 128:256])
                    v.tensor_copy(GsT[:, 0:128], ps[2][:, 0:128])
                    done(v.tensor_copy(GsT[0:H, 128:256], ps[2][0:H, 128:256]))
                    v.tensor_tensor_scan(CT[:, 0:128], GsT[:, 0:128], EsT[:, 0:128], 0.0, ALU.mult, ALU.add)
                    done(v.tensor_tensor_scan(CT[0:H, 128:256], GsT[0:H, 128:256], EsT[0:H, 128:256], 0.0, ALU.mult, ALU.add))
                    v.tensor_copy(CTx[0:H, 129:256], CT[0:H, 128:255])
                else:
                    done(v.tensor_tensor_scan(CT[:, 0:128], contT[:, :], EsT[:, 0:128], 0.0, ALU.mult, ALU.add))
                done(v.tensor_copy(CTx[:, 1:128], CT[:, 0:127]), "CTx " + name)
                after_pe("C " + name)
                if H:
                    v.tensor_copy(carry_row[:, F:F + H], MM[:, H:2 * H])
                done(v.tensor_copy(carry_row[:, 0:F], ps[0][:, 0:F]), "carry " + name)

            def merge_softmax(name, H, U, target):
                F = D + H
                w = F + H
                fs = view(final_state[:, 0:NT * w], "p (t w) -> p t w", w=w)
                fc = view(final_carry[:, 0:NT * w], "p (t w) -> p t w", w=w)
                m, mc = fm[:, :, 0:H], fmc[:, :, 0:H]
                dve.wait_ge(LS[name]["final_landed"], 16 * 2 * NT)
                done(v.tensor_tensor(mc, fc[:, :, F:], bc(has_bound[:, :].unsqueeze(2), [128, NT, H]), ALU.min))
                done(v.tensor_tensor(m, fs[:, :, F:], mc, ALU.max))
                d = view(fd[:, 0:2 * NT * H], "p (g t h) -> p g t h", g=2, h=H)
                e = view(fe[:, 0:2 * NT * H], "p (g t h) -> p g t h", g=2, h=H)
                v.tensor_tensor(d[:, 0], fs[:, :, F:], m, ALU.subtract)
                done(v.tensor_tensor(d[:, 1], mc, m, ALU.subtract), "fd " + name)
                after_act("fe " + name)
                done(v.tensor_tensor(e[:, 1], e[:, 1], bc(has[:, :].unsqueeze(2), [128, NT, H]), ALU.mult))
                for part, f in ((fs, 0), (fc, 1)):
                    p4 = view(part[:, :, 0:F], "p t (u h) -> p t u h", h=H)
                    last = v.tensor_tensor(p4, p4, bc(e[:, f].unsqueeze(2), [128, NT, U + 1, H]), ALU.mult)
                done(last)
                done(v.tensor_tensor(fs[:, :, 0:F], fs[:, :, 0:F], fc[:, :, 0:F], ALU.add))
                done(v.tensor_scalar(den[:, :, 0:H], fs[:, :, D:F], 1e-30, None, ALU.max))
                done(v.reciprocal(den[:, :, 0:H], den[:, :, 0:H]))
                done(v.tensor_tensor(target, view(fs[:, :, 0:D], "p t (u h) -> p t u h", h=H), bc(den[:, :, 0:H].unsqueeze(2), [128, NT, U, H]), ALU.mult))

            def over_nodes(col):
                return bc(col[:, :].unsqueeze(2), [128, NT, D])

            def over_tiles(row):
                return bc(row[:, :].unsqueeze(1), [128, NT, D])

            def layernorm(Y, name, g=None, b=None, masked=False):
                done(v.tensor_reduce(mean[:, :], Y[:, :, :], AX.X, ALU.add))
                done(v.tensor_scalar(mean[:, :], mean[:, :], 1.0 / D, None, ALU.mult))
                done(v.tensor_tensor(Y[:, :, :], Y[:, :, :], over_nodes(mean), ALU.subtract))
                done(v.tensor_tensor(final_carry_sq, Y[:, :, :], Y[:, :, :], ALU.mult))
                done(v.tensor_reduce(var[:, :], final_carry_sq, AX.X, ALU.add))
                done(v.tensor_scalar(var[:, :], var[:, :], 1.0 / D, None, ALU.mult), "var " + name)
                after_act("sd " + name)
                done(v.reciprocal(rstd[:, :], sd[:, :]))
                done(v.tensor_tensor(Y[:, :, :], Y[:, :, :], over_nodes(rstd), ALU.mult), None if g is not None or masked else name)
                if g is not None:
                    done(v.tensor_tensor(Y[:, :, :], Y[:, :, :], over_tiles(g), ALU.mult))
                    done(v.tensor_tensor(Y[:, :, :], Y[:, :, :], over_tiles(b), ALU.add), name)

            def next_x(name):
                layernorm(X, name, masked=True)
                done(v.tensor_scalar(X[:, NT - 1, :], X[:, NT - 1, :], row_ok[:, 0:1], None, ALU.mult), name)

            final_carry_sq = view(final_carry[:, 0:NT * D], "p (t d) -> p t d", d=D)

            attention_steps("att0", H0, D // H0, True)
            carries("att0", H0, D // H0)
            merge_softmax("att0", H0, D // H0, view(R[:, :, :], "p t (h u) -> p t u h", h=H0))
            done(v.tensor_tensor(R[:, :, :], R[:, :, :], X[:, :, :], ALU.add))
            layernorm(R, "ln1", rows_in["L0_gnn_ln1_g"], rows_in["L0_gnn_ln1_b"])
            S = TS["ffn"]
            with dve.Fori(0, NT) as t:
                dve.wait_ge(S["first"], t + 1)
                p1 = view(ps[1][:, :], "p (c n) -> p c n", c=FC)
                v.tensor_tensor(hb[:, :, :], p1, bc(b1[:, :].unsqueeze(2), [128, FC, 128]), ALU.add).then_inc(S["chain"], 1)
                dve.wait_ge(S["chain"], t * 2 + 1)
                v.scalar_tensor_tensor(hn[:, :, :], hb[:, :, :], 0.0, bc(pw[:, :].unsqueeze(2), [128, FC, 128]), ALU.min, ALU.mult).then_inc(S["chain"], 1)
                dve.wait_ge(S["chain"], t * 2 + 2)
                dve.wait_ge(S["second"], t)
                v.scalar_tensor_tensor(view(hT[:, :], "p (c n) -> p c n", c=FC), hb[:, :, :], 0.0, hn[:, :, :], ALU.max, ALU.add).then_inc(S["hidden"], 1)
                dve.wait_ge(S["second"], t + 1)
                v.tensor_copy(T1[:, bass.ds(t, 1), :], ps[2][:, 0:D]).then_inc(S["result"], 1)
            dve.wait_ge(S["result"], NT)
            done(v.tensor_tensor(R[:, :, :], R[:, :, :], T1[:, :, :], ALU.add))
            done(v.tensor_tensor(R[:, :, :], R[:, :, :], over_tiles(rows_in["L0_gnn_b2"]), ALU.add))
            layernorm(R, "ln2", rows_in["L0_gnn_ln2_g"], rows_in["L0_gnn_ln2_b"])
            done(v.tensor_tensor(X[:, :, :], X[:, :, :], R[:, :, :], ALU.add))
            next_x("x0")

            def gcn_sum(name, k):
                done(v.tensor_tensor(T1[:, :, :], X[:, :, :], over_nodes(dis[k]), ALU.mult), "table " + name)
                sum_steps(name)
                carries(name, 0, D)
                fs = view(final_state[:, 0:NT * D], "p (t w) -> p t w", w=D)
                fc = final_carry_sq
                dve.wait_ge(LS[name]["final_landed"], 16 * 2 * NT)
                done(v.tensor_tensor(fc, fc, over_nodes(has), ALU.mult))
                done(v.tensor_tensor(fs, fs, fc, ALU.add))
                done(v.tensor_tensor(fs, fs, T1[:, :, :], ALU.add))
                done(v.tensor_tensor(R[:, :, :], fs, over_nodes(dis[k]), ALU.mult), "agg3" if k else "agg1")

            gcn_sum("sum1", 0)
            done(v.tensor_tensor(X[:, :, :], X[:, :, :], R[:, :, :], ALU.add))
            next_x("x1")

            S = TS["typed"]
            with dve.Fori(0, NT) as t:
                dve.wait_ge(S["first"], t + 1)
                for k in range(NTYPE):
                    bank, at = (ps[1], k * HXW) if k < 3 else (ps[2], (k - 3) * HXW)
                    mask = view(type_mask[:, :, :], "p t k -> p (t k)")[:, bass.ds(t * NTYPE + k, 1)]
                    dest = hx2 if k == NTYPE - 1 else hx
                    if k == NTYPE - 1:
                        dve.wait_ge(S["written"], t * 32)
                    if k == 0:
                        ins = v.tensor_scalar(dest[:, :], bank[:, at:at + HXW], mask, None, ALU.mult)
                    else:
                        ins = v.scalar_tensor_tensor(dest[:, :], bank[:, at:at + HXW], mask, hx[:, :], ALU.mult, ALU.add)
                    if k < NTYPE - 1:
                        ins.then_inc(S["chain"], 1)
                        dve.wait_ge(S["chain"], t * (NTYPE - 1) + (k + 1))
                ins.then_inc(S["result"], 1)
            attention_steps("att2", H2, D // H2, False)
            carries("att2", H2, D // H2)
            merge_softmax("att2", H2, D // H2, view(T1[:, :, :], "p t (u h) -> p t u h", h=H2))
            dve.wait_ge(S["second"], NT)
            done(v.tensor_tensor(R[:, :, :], R[:, :, :], T1[:, :, :], ALU.add))
            done(v.tensor_tensor(R[:, :, :], R[:, :, :], over_tiles(rows_in["L2_gnn_b_res"]), ALU.add))
            done(v.tensor_scalar(R[:, :, :], R[:, :, :], 0.0, None, ALU.max))
            done(v.tensor_tensor(X[:, :, :], X[:, :, :], R[:, :, :], ALU.add))
            next_x("x2")
            after_pe("linT")
            done(v.tensor_copy(linT[:, :], ps[0][:, 0:128]))

            gcn_sum("sum3", 1)
            S = TS["gcn"]
            with dve.Fori(0, NT) as t:
                dve.wait_ge(S["second"], t + 1)
                v.tensor_tensor(X[:, bass.ds(t, 1), :], X[:, bass.ds(t, 1), :], ps[2][:, 0:D].unsqueeze(1), ALU.add).then_inc(S["result"], 1)
            dve.wait_ge(S["result"], NT)
            done(v.tensor_tensor(X[:, :, :], X[:, :, :], over_tiles(rows_in["L3_gnn_lin_b"]), ALU.add))
            layernorm(X, "x3")


NAMES = ("x", "src", "dst", "node_type_5", "L0_gnn_Wq", "L0_gnn_Wk", "L0_gnn_Wv", "L0_gnn_ln1_g",
         "L0_gnn_ln1_b", "L0_gnn_ln2_g", "L0_gnn_ln2_b", "L0_gnn_W1", "L0_gnn_b1", "L0_gnn_prelu_w",
         "L0_gnn_W2", "L0_gnn_b2", "L2_gnn_W_typed", "L2_gnn_al_w", "L2_gnn_ar_w", "L2_gnn_W_res",
         "L2_gnn_b_res", "L3_gnn_W", "L3_gnn_b", "L3_gnn_lin_W", "L3_gnn_lin_b")


def kernel(**inputs):
    import numpy as np
    import concourse.bacc as bacc
    from concourse.bass_utils import run_bass_kernel_spmd as run

    nc = bacc.Bacc("TRN2", target_bir_lowering=False, num_devices=1)
    arrays, aps = {}, {}
    for name in NAMES:
        array = np.ascontiguousarray(inputs[name])
        arrays["in_" + name] = array
        aps[name] = nc.dram_tensor("in_" + name, array.shape, mybir.dt.from_np(array.dtype), kind="ExternalInput").ap()
    out = nc.dram_tensor("out_x", tuple(inputs["x"].shape), F32, kind="ExternalOutput").ap()
    gnn_kernel(nc, aps, out)
    return run(nc, [arrays], core_ids=[0]).results[0]["out_x"]
```

```python
from contextlib import ExitStack

import concourse.bass as bass
from concourse import mybir

ALU = mybir.AluOpType
ACT = mybir.ActivationFunctionType
AX = mybir.AxisListType
F32 = mybir.dt.float32
BF16 = mybir.dt.bfloat16
I32 = mybir.dt.int32

BIG = 1e30
ROUND = 12582912.0
EPS = 1e-5


class Signals(dict):

    def __init__(self, owner, sem):
        super().__init__()
        self.owner, self.sem = owner, sem

    def __missing__(self, name):
        self[name] = self.sem(f"{self.owner}_{name}")
        return self[name]


def gnn_kernel(nc, a, out):
    N, D = a["x"].shape
    E = a["src"].shape[0]
    LANES = 128
    NT = -(-N // LANES)
    LAST = N - (NT - 1) * LANES
    PAD = NT * LANES
    SLOTS = 6
    RUN = 8
    STEPS = -(-((E + N * (SLOTS - 1)) // SLOTS) // LANES)
    STEPS += STEPS % 2
    HALF = STEPS // 2
    ROWS = LANES * STEPS
    H0 = 8
    H2 = 4
    NTYPE = a["L2_gnn_W_typed"].shape[0]
    FF = a["L0_gnn_W1"].shape[1]
    FC = FF // 128
    EP = 125
    EC = E // EP
    NB = NT
    BATCH = EC // NB
    HA = (BATCH - BATCH // 2, BATCH // 2)
    assert EP * EC == E and NB * BATCH == EC
    LO = 64
    RB = -(-(RUN + E + RUN) // RUN)
    RBW = RB * RUN
    FS = 13
    FIT = STEPS // (2 * FS)
    BF = NB // FIT
    assert FIT * 2 * FS == STEPS
    HXW = D + 2 * H2

    with ExitStack() as ctx:
        def sb(name, shape, dt=F32):
            return ctx.enter_context(nc.sbuf_tensor(name, shape, dt))

        def sem(name):
            return ctx.enter_context(nc.semaphore(name))

        def dram(name, shape, dt=F32):
            return nc.dram_tensor(name, shape, dt).ap()

        ps = [ctx.enter_context(nc.psum_tensor(f"ps{i}", [128, 512], F32)) for i in range(6)]

        shifted = dram("shifted_sources", [RUN * RB, RUN], I32)
        rowinfo_d = dram("rowinfo_d", [ROWS + PAD, 4])
        q_d = dram("q_d", [PAD, D])
        kv_d = dram("kv_d", [PAD, 2 * D])
        y_d = [dram(f"y{k}_d", [PAD, D]) for k in range(2)]
        h_d = dram("h_d", [PAD, D + H2])
        hr_d = dram("hr_d", [PAD, H2])
        W0 = D + 2 * H0
        W2_ = D + 2 * H2
        width = {"att0": W0, "sum1": D, "att2": W2_, "sum3": D}
        state_d = {n: dram(f"state_{n}", [ROWS + 1, w]) for n, w in width.items()}
        carry_d = {n: dram(f"carry_{n}", [PAD + LANES, w]) for n, w in width.items()}

        X = sb("X", [128, NT, D])
        R = sb("R", [128, NT, D])
        T1 = sb("T1", [128, NT, D])
        finals = sb("finals", [128, 2 * NT * W0])
        final_state, final_carry = finals[:, 0:NT * W0], finals[:, NT * W0:]
        gathered = [sb(f"gathered{b}", [128, SLOTS * 2 * D]) for b in range(2)]
        dst_row = [sb(f"dst_row{b}", [128, D]) for b in range(2)]
        prod = sb("prod", [128, SLOTS, D])
        msg = sb("msg", [128, SLOTS * (D + H0)])
        state = [sb(f"state{b}", [128, W0]) for b in range(2)]
        index_cols = [sb(f"index_cols{b}", [128, SLOTS + 1], I32) for b in range(2)]
        IX = sb("IX", [128, STEPS + 2, SLOTS + 1])
        VALID = sb("VALID", [128, STEPS, SLOTS])
        BOUND = sb("BOUND", [128, STEPS, SLOTS])
        same = sb("same", [128, STEPS])
        same_bound = sb("same_bound", [128, STEPS])
        scores = sb("scores", [128, SLOTS, H0])
        top = sb("top", [128, H0])
        diff = sb("diff", [128, (SLOTS + 1) * H0])
        expd = sb("expd", [128, (SLOTS + 1) * H0])
        slot_sum = sb("slot_sum", [128, D + H0])
        scaled = sb("scaled", [128, D + H0])

        edge_i = sb("edge_i", [128, EC], I32)
        part_i = sb("part_i", [128, EC], I32)
        lo_b = sb("lo_b", [128, EC], BF16)
        hi_b = sb("hi_b", [128, EC], BF16)
        oh_lo = [sb(f"oh_lo{b}", [128, HA[b], LO], BF16) for b in range(2)]
        oh_hi = [sb(f"oh_hi{b}", [128, HA[b], 2 * NT], BF16) for b in range(2)]
        zero_b = sb("zero_b", [128, 128], BF16)
        iota_i = sb("iota_i", [128, 128], I32)
        iota_hi_i = sb("iota_hi_i", [128, 2 * NT], I32)
        node_i = sb("node_i", [128, NT], I32)
        row_i = sb("row_i", [128, STEPS], I32)
        part_id_i = sb("part_id_i", [128, 1], I32)
        iota_f = sb("iota_f", [128, 128])
        iota_lo_b = sb("iota_lo_b", [128, LO], BF16)
        iota_hi_b = sb("iota_hi_b", [128, 2 * NT], BF16)
        row_f = sb("row_f", [128, STEPS])
        part_id = sb("part_id", [128, 1])
        ident = sb("ident", [128, 128])
        before = sb("before", [128, 128])
        ones = sb("ones", [128, 128])
        zeros = sb("zeros", [128, 4 * STEPS])
        deg_rows = sb("deg_rows", [128, 2 * NT])
        tot = sb("tot", [128, 2 * NT])
        incl = sb("incl", [128, 2 * NT])
        starts = sb("starts", [128, 2 * NT])
        small_i = sb("small_i", [128, 2 * NT], I32)
        info = sb("info", [128, NT, 4])
        row0_i = sb("row0_i", [128, NT], I32)
        last_f = sb("last_f", [128, NT])
        last_i = sb("last_i", [128, NT], I32)
        empty = sb("empty", [128, NT])
        target_f = sb("target_f", [128, NT])
        neutral = [sb("neutral0", [128, W0]), sb("neutral2", [128, W2_])]
        lane_cols = sb("lane_cols", [128, 8])
        carry_to_i = sb("carry_to_i", [128, 1], I32)
        rowinfo = sb("rowinfo", [128, STEPS, 4])
        RS = sb("RS", [128, 4, STEPS])
        lane_top = sb("lane_top", [4, 128])
        lane_excl = sb("lane_excl", [4, 128])
        lane_in = sb("lane_in", [4, 128])
        carry4 = sb("carry4", [128, 4])
        pos = sb("pos", [128, STEPS])
        pos_i = sb("pos_i", [128, STEPS], I32)
        low_i = sb("low_i", [128, STEPS], I32)
        high_i = sb("high_i", [128, STEPS], I32)
        low_f = sb("low_f", [128, STEPS])
        high_f = sb("high_f", [128, STEPS])
        table_row = sb("table_row", [128, STEPS])
        cont = sb("cont", [128, 1])
        cont2 = sb("cont2", [128, 1])
        wide = sb("wide", [128, 128])
        penalty = sb("penalty", [128, H0])
        penaltyT = sb("penaltyT", [H0, 128])
        contT = sb("contT", [128, 128])
        fetch_row = [sb(f"fetch_row{b}", [128, FS], I32) for b in range(2)]
        fetched = [sb(f"fetched{b}", [128, FS * RUN], I32) for b in range(2)]
        fetched_f = sb("fetched_f", [128, FS, SLOTS])
        dis = [sb(f"dis{k}", [128, NT]) for k in range(2)]
        outdeg = sb("outdeg", [128, NT])
        row_ok = sb("row_ok", [128, 1])

        xs = sb("xs", [128, 128])
        xT = sb("xT", [128, 128])
        hT = sb("hT", [128, FC * 128])
        hb = sb("hb", [128, FC, 128])
        hn = sb("hn", [128, FC, 128])
        proj = sb("proj", [128, 3 * D])

        Wqkv = sb("Wqkv", [128, 3 * D])
        W1 = sb("W1", [128, FF])
        W2 = sb("W2", [128, FC, D])
        b1 = sb("b1", [128, FC])
        pw = sb("pw", [128, FC])
        rows_in = {n: sb("row_" + n, [128, D]) for n in
                   ("L0_gnn_ln1_g", "L0_gnn_ln1_b", "L0_gnn_ln2_g", "L0_gnn_ln2_b", "L0_gnn_b2",
                    "L2_gnn_b_res", "L3_gnn_lin_b")}
        Wt_in = sb("Wt_in", [128, NTYPE, D])
        alr = sb("alr", [128, 2, NTYPE, 32])
        al_in = finals[:, 0:NTYPE * 32 * 32]
        Wcat = sb("Wcat", [128, NTYPE * HXW + D])
        Wprod = sb("Wprod", [128, D])
        ntype_i = sb("ntype_i", [128, NT], I32)
        ntype_f = sb("ntype_f", [128, NT])
        type_mask = sb("type_mask", [128, NT, NTYPE])
        hx = sb("hx", [128, HXW])
        hx2 = sb("hx2", [128, HXW])
        W3 = sb("W3", [128, D])
        b3 = sb("b3", [128, 1])
        lin_in = sb("lin_in", [128, D])
        linT = sb("linT", [128, D])
        eps_c = sb("eps_c", [128, 1])

        mean = sb("mean", [128, NT])
        var = sb("var", [128, NT])
        sd = sb("sd", [128, NT])
        rstd = sb("rstd", [128, NT])
        den = sb("den", [128, NT, H0])
        fm = sb("fm", [128, NT, H0])
        fd = sb("fd", [128, 2 * NT * H0])
        fe = sb("fe", [128, 2 * NT * H0])

        mT = sb("mT", [H0, 128])
        MT = sb("MT", [H0, 128])
        MprevT = sb("MprevT", [H0, 128])
        MM = sb("MM", [128, 2 * H0])
        md = sb("md", [128, 2 * H0])
        me = sb("me", [128, 2 * H0])
        Es = sb("Es", [128, D + H0])
        Gs = sb("Gs", [128, D + H0])
        EsT = sb("EsT", [128, 256])
        GsT = sb("GsT", [128, 256])
        CT = sb("CT", [128, 256])
        CTx = sb("CTx", [128, 256])
        carry_row = sb("carry_row", [128, W0])

        assert ROWS * 1.0 < 2 ** 23

        def wait(eng, signal, value):
            if not (isinstance(value, int) and value == 0):
                eng.wait_ge(signal, value)

        def loop(eng, n, turn):
            turn(0)
            with eng.Fori(1, n) as i:
                turn(i)

        x_loaded, weights_loaded = sem("x_loaded"), sem("weights_loaded")
        al_loaded = [sem("al_loaded0"), sem("al_loaded1")]
        ends_loaded = [sem("dst_loaded"), sem("src_loaded")]
        shifted_ready, zeros_ready, rowinfo_zeroed = sem("shifted_ready"), sem("zeros_ready"), sem("rowinfo_zeroed")
        iotas_ready = sem("iotas_ready")
        neutral_written = sem("neutral_written")
        dve_done = sem("dve_done")
        onehots_ready = [sem("onehots_ready0"), sem("onehots_ready1")]
        onehots_used = [sem("onehots_used0"), sem("onehots_used1")]
        rowinfo_scattered, rowinfo_loaded = sem("rowinfo_scattered"), sem("rowinfo_loaded")
        fetch_staged = [sem("fetch_staged0"), sem("fetch_staged1")]
        fetch_landed = [sem("fetch_landed0"), sem("fetch_landed1")]
        fetch_used = [sem("fetch_used0"), sem("fetch_used1")]
        fetch_chain = sem("fetch_chain")
        node_tables = sem("node_tables")
        stored_out = sem("stored_out")
        carries_landed = sem("carries_landed")
        LS = {n: Signals(n, sem) for n in ("att0", "sum1", "att2", "sum3")}
        TS = {n: Signals(n, sem) for n in ("proj", "ffn", "typed", "gcn")}

        layers, attentions, sums = ("att0", "sum1", "att2", "sum3"), ("att0", "att2"), ("sum1", "sum3")
        norms = ("ln1", "ln2", "x0", "x1", "x2", "x3")
        turns = {"var": norms, "sd": norms, "steps": layers, "carry": layers, "CTx": layers, "C": layers,
                 "EG": layers, "table": sums, "m": attentions, "MM": attentions, "md": attentions,
                 "me": attentions, "fd": attentions, "fe": attentions, "MprevT": attentions}
        numbered = {"x": "0123", "ln": "12", "deg": "01", "sqrt deg": "01", "hist": "01", "split": "01", "agg": "13"}
        events = {}

        def event(name):
            family, _, turn = name.partition(" ")
            order = turns.get(family[2:])
            order = attentions if family == "V:EG" else order
            if name[-1] in numbered.get(name[2:-1], ""):
                family, turn, order = name[:-1].replace(" ", "_"), name[-1], numbered[name[2:-1]]
            elif order is None or turn not in order:
                family, turn, order = name.replace(" ", "_"), "", ("",)
            if family not in events:
                events[family] = sem("done_" + family.replace(":", "_"))
            return events[family], order.index(turn) + 1

        block = ctx.enter_context(nc.Block())

        def bc(ap, shape):
            return ap.to_broadcast(shape)

        def view(ap, spec, **kw):
            return ap.rearrange(spec, **kw)

        weight_loads = [(Wqkv[:, n * D:(n + 1) * D], a["L0_gnn_W" + "qkv"[n]]) for n in range(3)]
        weight_loads += [(W1[:, :], a["L0_gnn_W1"]), (W2[:, :, :], view(a["L0_gnn_W2"], "(c p) d -> p c d", p=128)),
                         (b1[:, :], view(a["L0_gnn_b1"], "(c p) -> p c", p=128)),
                         (pw[:, :], view(a["L0_gnn_prelu_w"], "(c p) -> p c", p=128)),
                         (b3[:, :], view(a["L3_gnn_b"], "(p o) -> p o", o=1)),
                         (ntype_i[:, 0:NT - 1], view(a["node_type_5"][0:(NT - 1) * 128], "(t p) -> p t", p=128)),
                         (ntype_i[0:LAST, NT - 1:NT], view(a["node_type_5"][(NT - 1) * 128:N], "(p o) -> p o", o=1)),
                         (Wt_in[:, :, :], view(a["L2_gnn_W_typed"], "t i o -> i t o")),
                         (Wcat[:, NTYPE * HXW:], a["L2_gnn_W_res"]), (W3[:, :], a["L3_gnn_W"]),
                         (lin_in[:, :], a["L3_gnn_lin_W"])]
        weight_loads += [(tile[:, :], a[n].partition_broadcast(128)) for n, tile in rows_in.items()]

        @block.sync
        def _(sp):
            sp.dma_start(view(edge_i[0:EP, :], "p c -> p c"), view(a["dst"], "(p c) -> p c", p=EP)).then_inc(ends_loaded[0], 16)
            sp.dma_start(X[:, 0:NT - 1, :], view(a["x"][0:(NT - 1) * 128, :], "(t p) d -> p t d", p=128)).then_inc(x_loaded, 16)
            sp.wait_ge(iotas_ready, 1)
            sp.dma_start(X[0:LAST, NT - 1, :], a["x"][(NT - 1) * 128:N, :]).then_inc(x_loaded, 16)
            flat = view(shifted, "a b -> (a b)")
            for s in range(RUN):
                at = s * RBW + RUN - s
                sp.dma_start(view(flat[at:at + E], "(p c) -> p c", p=EP), view(a["src"], "(p c) -> p c", p=EP)).then_inc(shifted_ready, 16)
                tail = flat[at + E:(s + 1) * RBW]
                sp.dma_start(view(tail, "(o c) -> o c", o=1), zeros[0:1, 0:tail.shape[0]].bitcast(I32)).then_inc(shifted_ready, 16)
            sp.dma_start(view(rowinfo_d[0:ROWS, :], "(p i) c -> p (i c)", p=128), zeros[:, :]).then_inc(rowinfo_zeroed, 16)
            with nc.allow_non_contiguous_dma(reason="a few short parameter columns"):
                for tile, source in weight_loads:
                    sp.dma_start(tile, source).then_inc(weights_loaded, 16)
            sp.dma_start(al_in[:, :], view(a["L2_gnn_al_w"], "t i o -> (t i o)").partition_broadcast(128)).then_inc(al_loaded[0], 16)
            sp.wait_ge(*event("V:consts"))
            for n, w in width.items():
                nothing = {W0: neutral[0], W2_: neutral[1], D: zeros}[w]
                sp.dma_start(state_d[n][ROWS:ROWS + 1, :], zeros[0:1, 0:w]).then_inc(neutral_written, 16)
                sp.dma_start(view(carry_d[n], "(k p) w -> p k w", p=128),
                             nothing[:, 0:w].unsqueeze(1).to_broadcast([128, NT + 1, w])).then_inc(neutral_written, 16)
            def tile_tables(S, parts):
                with sp.Fori(0, NT) as t:
                    sp.wait_ge(S["result"], t + 1)
                    for table, tile in parts:
                        sp.dma_start(table[bass.ds(t * 128, 128), :], tile).then_inc(S["written"], 16)
                sp.wait_ge(S["written"], 16 * NT * len(parts))

            def state_stores(name):
                S = LS[name]
                st = view(state_d[name][0:ROWS, :], "(p i) w -> p i w", p=128)
                w = st.shape[2]
                with sp.Fori(0, HALF) as it:
                    for b in range(2):
                        sp.wait_ge(S["state_ready"], it * 2 + b + 1)
                        sp.dma_start(st[:, bass.ds(it * 2 + b, 1), :], state[b][:, 0:w]).then_inc(S[f"stored{b}"], 16)
                sp.wait_ge(S["carry_scattered"], 16)
                sp.dma_start(view(final_carry[:, 0:NT * w], "p (t w) -> p t w", w=w),
                             view(carry_d[name][0:PAD, :], "(t p) w -> p t w", p=128)).then_inc(carries_landed, 16)

            def whole_table(name, k):
                sp.wait_ge(*event("V:table " + name))
                sp.dma_start(view(y_d[k], "(t p) d -> p t d", p=128), T1[:, :, :]).then_inc(LS[name]["table"], 16)

            tile_tables(TS["proj"], [(q_d, proj[:, 0:D]), (kv_d, proj[:, D:])])
            sp.wait_ge(rowinfo_scattered, 16 * NT)
            sp.dma_start(view(rowinfo[:, :, :], "p i c -> p (i c)"), view(rowinfo_d[0:ROWS, :], "(p i) c -> p (i c)", p=128)).then_inc(rowinfo_loaded, 16)
            sp.wait_ge(*event("V:split0"))
            sp.dma_start(edge_i[0:EP, :], view(a["src"], "(p c) -> p c", p=EP)).then_inc(ends_loaded[1], 16)
            sp.wait_ge(*event("V:al0"))
            sp.dma_start(al_in[:, :], view(a["L2_gnn_ar_w"], "t i o -> (t i o)").partition_broadcast(128)).then_inc(al_loaded[1], 16)
            state_stores("att0")
            whole_table("sum1", 0)
            state_stores("sum1")
            tile_tables(TS["typed"], [(h_d, hx2[:, 0:D + H2]), (hr_d, hx2[:, D + H2:])])
            state_stores("att2")
            whole_table("sum3", 1)
            state_stores("sum3")
            sp.wait_ge(*event("V:x3"))
            sp.dma_start(view(out[0:(NT - 1) * 128, :], "(t p) d -> p t d", p=128), X[:, 0:NT - 1, :]).then_inc(stored_out, 16)
            sp.dma_start(out[(NT - 1) * 128:N, :], X[0:LAST, NT - 1, :]).then_inc(stored_out, 16)
            sp.wait_ge(stored_out, 32)

        @block.gpsimd
        def _(pool):
            nc.gpsimd.memset(X[:, NT - 1, :], 0.0)
            nc.gpsimd.memset(ntype_i[:, NT - 1:NT], 0)
            nc.gpsimd.memset(zeros[:, :], 0.0)
            nc.gpsimd.iota(iota_i[:, :], pattern=[[1, 128]], base=0, channel_multiplier=0)
            nc.gpsimd.iota(view(iota_hi_i[:, :], "p (a b) -> p a b", a=2), pattern=[[1, 2], [2, NT]], base=0, channel_multiplier=0)
            nc.gpsimd.iota(node_i[:, :], pattern=[[128, NT]], base=0, channel_multiplier=1)
            nc.gpsimd.iota(row_i[:, :], pattern=[[1, STEPS]], base=0, channel_multiplier=STEPS)
            nc.gpsimd.iota(part_id_i[:, :], pattern=[[0, 1]], base=0, channel_multiplier=1).then_inc(iotas_ready, 1)

            pool.wait_ge(rowinfo_zeroed, 16)
            pool.wait_ge(*event("V:info"))
            for t in range(NT):
                nc.gpsimd.indirect_dma_start(out=rowinfo_d, out_offset=bass.IndirectOffsetOnAxis(ap=row0_i[:, t:t + 1], axis=0),
                                             in_=info[:, t, :], in_offset=None).then_inc(rowinfo_scattered, 16)
            with pool.Fori(1, FIT + 1) as use:
                for b in range(2):
                    pool.wait_ge(shifted_ready, 32 * RUN)
                    pool.wait_ge(fetch_staged[b], use)
                    pool.wait_ge(fetch_used[b], use)
                    for k in range(FS):
                        nc.gpsimd.indirect_dma_start(out=fetched[b][:, k * RUN:(k + 1) * RUN], out_offset=None, in_=shifted,
                                                     in_offset=bass.IndirectOffsetOnAxis(ap=fetch_row[b][:, k:k + 1], axis=0)).then_inc(fetch_landed[b], 16)

            def steps(name, table, side, table_written):
                S = LS[name]
                w = table.shape[1]
                with pool.Fori(1, HALF + 1) as use:
                    for b in range(2):
                        pool.wait_ge(*table_written)
                        pool.wait_ge(S[f"index{b}"], use)
                        pool.wait_ge(S[f"free{b}"], use)
                        if side is not None:
                            nc.gpsimd.indirect_dma_start(out=dst_row[b][:, 0:side.shape[1]], out_offset=None, in_=side,
                                                         in_offset=bass.IndirectOffsetOnAxis(ap=index_cols[b][:, SLOTS:SLOTS + 1], axis=0)).then_inc(S[f"landed{b}"], 16)
                        for j in range(SLOTS):
                            nc.gpsimd.indirect_dma_start(out=gathered[b][:, j * w:(j + 1) * w], out_offset=None, in_=table,
                                                         in_offset=bass.IndirectOffsetOnAxis(ap=index_cols[b][:, j:j + 1], axis=0)).then_inc(S[f"landed{b}"], 16)
                w = state_d[name].shape[1]
                pool.wait_ge(neutral_written, 16 * 2 * len(width))
                pool.wait_ge(S["stored0"], 16 * HALF)
                pool.wait_ge(S["stored1"], 16 * HALF)
                for t in range(NT):
                    nc.gpsimd.indirect_dma_start(out=final_state[:, t * w:(t + 1) * w], out_offset=None, in_=state_d[name],
                                                 in_offset=bass.IndirectOffsetOnAxis(ap=last_i[:, t:t + 1], axis=0)).then_inc(S["final_landed"], 16)
                pool.wait_ge(*event("V:carry " + name))
                pool.wait_ge(neutral_written, 16 * 2 * len(width))
                nc.gpsimd.indirect_dma_start(out=carry_d[name], out_offset=bass.IndirectOffsetOnAxis(ap=carry_to_i[:, 0:1], axis=0),
                                             in_=carry_row[:, 0:w], in_offset=None).then_inc(S["carry_scattered"], 16)

            steps("att0", kv_d, q_d, (TS["proj"]["written"], 32 * NT))
            steps("sum1", y_d[0], None, (LS["sum1"]["table"], 16))
            steps("att2", h_d, hr_d, (TS["typed"]["written"], 32 * NT))
            steps("sum3", y_d[1], None, (LS["sum3"]["table"], 16))

        @block.scalar
        def _(act):
            def done(ins, name):
                ins.then_inc(event("A:" + name)[0], 1)

            def turn(S, source):
                def one(t):
                    nc.scalar.copy(xs[:, :], source[:, bass.ds(t, 1), :]).then_inc(S["staged"], 1)
                    act.wait_ge(S["turned"], t + 1)
                    wait(act, S["first"], t)
                    nc.scalar.copy(xT[:, :], ps[0][:, 0:128]).then_inc(S["xT"], 1)
                return one

            def sqrt_var(name):
                act.wait_ge(*event("V:var " + name))
                done(nc.scalar.activation(sd[:, :], var[:, :], ACT.Sqrt, bias=eps_c[:, 0:1]), "sd " + name)

            def steps(name, H, scale):
                S = LS[name]
                per = 16 * (SLOTS + (1 if H else 0))
                for b in range(2):
                    nc.scalar.copy(index_cols[b][:, :], IX[:, b, :]).then_inc(S[f"index{b}"], 1)

                def pair(it):
                    for b in range(2):
                        act.wait_ge(S[f"landed{b}"], (it + 1) * per)
                        nc.scalar.copy(index_cols[b][:, :], IX[:, bass.ds(it * 2 + (b + 2), 1), :]).then_inc(S[f"index{b}"], 1)
                        if H:
                            act.wait_ge(S["diffs"], it * 2 + b + 1)
                            nc.scalar.activation(expd[:, 0:(SLOTS + 1) * H], diff[:, 0:(SLOTS + 1) * H], ACT.Exp, scale=scale).then_inc(S["exps"], 1)

                loop(act, HALF, pair)
                if H:
                    act.wait_ge(*event("V:md " + name))
                    done(nc.scalar.activation(me[:, 0:2 * H], md[:, 0:2 * H], ACT.Exp, scale=scale), "me " + name)
                    act.wait_ge(*event("V:fd " + name))
                    done(nc.scalar.activation(fe[:, 0:2 * NT * H], fd[:, 0:2 * NT * H], ACT.Exp, scale=scale), "fe " + name)

            act.wait_ge(x_loaded, 32)
            loop(act, NT, turn(TS["proj"], X))
            act.wait_ge(*event("V:table rows"))

            def fetch(it):
                for b in range(2):
                    act.wait_ge(fetch_used[b], it + 1)
                    nc.scalar.copy(fetch_row[b][:, :], table_row[:, bass.ds(it * (2 * FS) + b * FS, FS)]).then_inc(fetch_staged[b], 1)

            loop(act, FIT, fetch)

            for k in (0, 1):
                act.wait_ge(*event(f"V:deg{k}"))
                done(nc.scalar.activation(sd[:, :], var[:, :], ACT.Sqrt), f"sqrt deg{k}")
            act.wait_ge(*event("V:IX"))
            steps("att0", H0, float(1.0 / (D ** 0.5)))
            sqrt_var("ln1")
            act.wait_ge(*event("V:ln1"))
            loop(act, NT, turn(TS["ffn"], R))
            sqrt_var("ln2")
            sqrt_var("x0")
            steps("sum1", 0, 1.0)
            sqrt_var("x1")
            act.wait_ge(*event("V:x1"))
            one = turn(TS["typed"], X)

            def typed(t):
                one(t)
                act.wait_ge(TS["typed"]["first"], t + 1)
                nc.scalar.copy(R[:, bass.ds(t, 1), :], ps[5][:, 0:D]).then_inc(TS["typed"]["second"], 1)

            loop(act, NT, typed)
            steps("att2", H2, 1.0)
            sqrt_var("x2")
            steps("sum3", 0, 1.0)
            act.wait_ge(*event("V:agg3"))
            one = turn(TS["gcn"], R)
            S = TS["gcn"]

            def gcn(t):
                one(t)
                act.wait_ge(S["first"], t + 1)
                wait(act, S["second"], t)
                nc.scalar.activation(hT[:, 0:128], ps[1][:, 0:128], ACT.Relu, bias=b3[:, 0:1]).then_inc(S["hidden"], 1)

            loop(act, NT, gcn)
            sqrt_var("x3")

        @block.tensor
        def _(pe):
            def done(ins, name):
                ins.then_inc(event("P:" + name)[0], 1)

            def open_counts(k):
                for u in range(2):
                    mm = nc.tensor.matmul(ps[3 + k][LO * u:LO * (u + 1), 0:NT], zero_b[:, 0:LO], zero_b[:, 0:NT], start=True, stop=False)
                    if k == 0:
                        mm.then_inc(onehots_used[u], 1)

            def batch(k, n):
                for b in range(2):
                    pe.wait_ge(onehots_ready[b], n + (1 + k * NB))
                    for c in range(HA[b]):
                        for u in range(2):
                            mm = nc.tensor.matmul(ps[3 + k][LO * u:LO * (u + 1), 0:NT], oh_lo[b][0:EP, c, :],
                                                  oh_hi[b][0:EP, c, u * NT:(u + 1) * NT], start=False, stop=False)
                    mm.then_inc(onehots_used[b], 1)

            def close_counts(k):
                for u in range(2):
                    mm = nc.tensor.matmul(ps[3 + k][LO * u:LO * (u + 1), 0:NT], zero_b[:, 0:LO], zero_b[:, 0:NT], start=False, stop=True)
                done(mm, f"hist{k}")

            def turn(S, t):
                pe.wait_ge(S["staged"], t + 1)
                wait(pe, S["xT"], t)
                nc.tensor.transpose(ps[0][:, 0:128], xs[:, :], ident[:, :]).then_inc(S["turned"], 1)
                pe.wait_ge(S["xT"], t + 1)

            pe.wait_ge(*event("V:consts"))
            open_counts(0)
            pe.wait_ge(weights_loaded, 16 * len(weight_loads))

            def project(t):
                S = TS["proj"]
                turn(S, t)
                wait(pe, S["result"], t)
                nc.tensor.matmul(ps[1][:, 0:3 * D], xT[:, :], Wqkv[:, :], start=True, stop=True).then_inc(S["first"], 1)
                batch(0, t)

            loop(pe, NT, project)
            close_counts(0)
            pe.wait_ge(*event("V:deg rows"))
            pe.wait_ge(TS["proj"]["result"], NT)
            nc.tensor.matmul(ps[0][:, 0:2 * NT], before[:, :], deg_rows[:, :], start=True, stop=True)
            done(nc.tensor.matmul(ps[1][:, 0:2 * NT], ones[:, :], deg_rows[:, :], start=True, stop=True), "sums")
            pe.wait_ge(*event("V:lane top"))
            done(nc.tensor.transpose(ps[0][0:4, 0:128], carry4[:, :], ident[:, :]), "lane top")
            pe.wait_ge(*event("V:lane excl"))
            done(nc.tensor.transpose(ps[0][:, 0:4], lane_excl[:, :], ident[0:4, 0:4]), "lane excl")
            pe.wait_ge(*event("V:cont"))
            nc.tensor.transpose(ps[0][0:H0, 0:128], penalty[:, :], ident[:, :])
            done(nc.tensor.transpose(ps[1][:, 0:128], wide[:, :], ident[:, :]), "cont")
            pe.wait_ge(*event("V:contT"))

            open_counts(1)

            def batches(it):
                for c in range(BF):
                    batch(1, it * BF + c)

            loop(pe, FIT, batches)
            for n in range(FIT * BF, NB):
                batch(1, n)
            close_counts(1)

            def carries(name, H):
                F = D + H
                if H:
                    pe.wait_ge(*event("V:steps " + name))
                    done(nc.tensor.transpose(ps[0][0:H, 0:128], state[1][:, F:F + H], ident[:, :]), "m " + name)
                    pe.wait_ge(*event("V:MprevT " + name))
                    nc.tensor.transpose(ps[0][:, 0:H], MT[0:H, :], ident[0:H, 0:H])
                    done(nc.tensor.transpose(ps[0][:, H:2 * H], MprevT[0:H, :], ident[0:H, 0:H]), "MM " + name)
                if H:
                    pe.wait_ge(*event("V:EG " + name))
                    nc.tensor.transpose(ps[1][:, 0:128], Es[:, 0:D], ident[:, :])
                    nc.tensor.transpose(ps[1][0:H, 128:256], Es[:, D:F], ident[:, :])
                    nc.tensor.transpose(ps[2][:, 0:128], Gs[:, 0:D], ident[:, :])
                    done(nc.tensor.transpose(ps[2][0:H, 128:256], Gs[:, D:F], ident[:, :]), "EG " + name)
                else:
                    pe.wait_ge(*event("V:steps " + name))
                    done(nc.tensor.transpose(ps[1][:, 0:128], state[1][:, 0:D], ident[:, :]), "EG " + name)
                pe.wait_ge(*event("V:CTx " + name))
                mm = nc.tensor.transpose(ps[0][:, 0:D], CTx[:, 0:128], ident[:, :])
                if H:
                    mm = nc.tensor.transpose(ps[0][:, D:F], CTx[0:H, 128:256], ident[0:H, 0:H])
                done(mm, "C " + name)

            carries("att0", H0)
            S = TS["ffn"]

            def ffn_first(t):
                turn(S, t)
                wait(pe, S["read"], t)
                for c in range(FC):
                    mm = nc.tensor.matmul(ps[1][:, c * 128:(c + 1) * 128], W1[:, c * 128:(c + 1) * 128], xT[:, :], start=True, stop=True)
                mm.then_inc(S["first"], 1)

            def ffn_second(t):
                pe.wait_ge(S["hidden"], t + 1)
                wait(pe, S["result"], t)
                for c in range(FC):
                    mm = nc.tensor.matmul(ps[2][:, 0:D], hT[:, c * 128:(c + 1) * 128], W2[:, c, :], start=(c == 0), stop=(c == FC - 1))
                mm.then_inc(S["second"], 1)

            ffn_first(0)
            ffn_first(1)
            ffn_second(0)
            with pe.Fori(2, NT) as t:
                ffn_first(t)
                ffn_second(t - 1)
            ffn_second(NT - 1)
            carries("sum1", 0)
            S = TS["typed"]
            pe.wait_ge(*event("V:Wcat"))

            def typed(t):
                S = TS["typed"]
                turn(S, t)
                wait(pe, S["result"], t)
                wait(pe, S["second"], t)
                nc.tensor.matmul(ps[1][:, 0:3 * HXW], xT[:, :], Wcat[:, 0:3 * HXW], start=True, stop=True)
                nc.tensor.matmul(ps[2][:, 0:2 * HXW], xT[:, :], Wcat[:, 3 * HXW:5 * HXW], start=True, stop=True)
                nc.tensor.matmul(ps[5][:, 0:D], xT[:, :], Wcat[:, 5 * HXW:], start=True, stop=True).then_inc(S["first"], 1)

            loop(pe, NT, typed)
            carries("att2", H2)
            pe.wait_ge(*event("V:x2"))
            done(nc.tensor.transpose(ps[0][:, 0:128], lin_in[:, :], ident[:, :]), "linT")
            carries("sum3", 0)

            def gcn(t):
                S = TS["gcn"]
                turn(S, t)
                wait(pe, S["hidden"], t)
                nc.tensor.matmul(ps[1][:, 0:128], W3[:, :], xT[:, :], start=True, stop=True).then_inc(S["first"], 1)
                pe.wait_ge(S["hidden"], t + 1)
                wait(pe, S["result"], t)
                nc.tensor.matmul(ps[2][:, 0:D], hT[:, 0:128], linT[:, :], start=True, stop=True).then_inc(S["second"], 1)

            loop(pe, NT, gcn)

        @block.vector
        def _(dve):
            v = nc.vector
            n_done = [0]

            def done(ins, name=None):
                if name:
                    ins.then_inc(event("V:" + name)[0], 1)
                    dve.wait_ge(*event("V:" + name))
                else:
                    n_done[0] += 1
                    ins.then_inc(dve_done, 1)
                    dve.wait_ge(dve_done, n_done[0])

            def after_pe(name):
                dve.wait_ge(*event("P:" + name))

            def after_act(name):
                dve.wait_ge(*event("A:" + name))

            dve.wait_ge(iotas_ready, 1)
            done(v.tensor_copy(iota_f[:, :], iota_i[:, :]))
            v.tensor_copy(iota_lo_b[:, :], iota_i[:, 0:LO])
            v.tensor_copy(iota_hi_b[:, :], iota_hi_i[:, :])
            v.tensor_copy(row_f[:, :], row_i[:, :])
            done(v.tensor_copy(part_id[:, :], part_id_i[:, :]))
            v.tensor_scalar(ident[:, :], iota_f[:, :], part_id[:, 0:1], None, ALU.is_equal)
            v.tensor_scalar(before[:, :], iota_f[:, :], part_id[:, 0:1], None, ALU.is_gt)
            v.tensor_scalar(row_ok[:, :], part_id[:, :], float(LAST), None, ALU.is_lt)
            v.memset(ones[:, :], 1.0)
            v.memset(eps_c[:, :], EPS)
            v.memset(IX[:, STEPS:STEPS + 2, :], 0.0)
            for tile, H in zip(neutral, (H0, H2)):
                v.memset(tile[:, 0:D + H], 0.0)
                v.memset(tile[:, D + H:], -BIG)
            done(v.memset(zero_b[:, :], 0.0), "consts")

            def split(k):
                dve.wait_ge(ends_loaded[k], 16)
                done(v.tensor_scalar(part_i[0:EP, :], edge_i[0:EP, :], LO - 1, None, ALU.bitwise_and))
                done(v.tensor_copy(lo_b[0:EP, :], part_i[0:EP, :]))
                done(v.tensor_scalar(part_i[0:EP, :], edge_i[0:EP, :], LO.bit_length() - 1, None, ALU.arith_shift_right), f"split{k}")
                done(v.tensor_copy(hi_b[0:EP, :], part_i[0:EP, :]))

            def batch(k, n):
                for b in range(2):
                    dve.wait_ge(onehots_used[b], n + (1 + k * NB))
                    for oh, iota, part in ((oh_lo, iota_lo_b, lo_b), (oh_hi, iota_hi_b, hi_b)):
                        w = oh[b].shape[2]
                        ins = v.tensor_tensor(oh[b][0:EP, :, :], bc(iota[0:EP, :].unsqueeze(1), [EP, HA[b], w]),
                                              bc(part[0:EP, bass.ds(n * BATCH + b * HA[0], HA[b])].unsqueeze(2), [EP, HA[b], w]), ALU.is_equal)
                    ins.then_inc(onehots_ready[b], 1)

            split(0)

            def project(t):
                S = TS["proj"]
                batch(0, t)
                dve.wait_ge(S["first"], t + 1)
                wait(dve, S["written"], t * 32)
                v.tensor_copy(proj[:, 0:2 * D], ps[1][:, 0:2 * D])
                v.tensor_copy(view(proj[:, 2 * D:], "p (d h) -> p h d", h=H0),
                              view(ps[1][:, 2 * D:3 * D], "p (h d) -> p h d", h=H0)).then_inc(S["result"], 1)

            loop(dve, NT, project)
            after_pe("hist0")
            done(v.tensor_copy(deg_rows[:, 0:NT], ps[3][:, 0:NT]))
            done(v.tensor_scalar(starts[:, 0:NT], deg_rows[:, 0:NT], 0.5 * (SLOTS - 1), 1.0 / SLOTS, ALU.add, ALU.mult))
            done(v.tensor_scalar(deg_rows[:, NT:], starts[:, 0:NT], ROUND, -ROUND, ALU.add, ALU.add), "deg rows")
            after_pe("sums")
            done(v.tensor_copy(tot[:, :], ps[1][:, 0:2 * NT]))
            for u in range(2):
                s = slice(u * NT, (u + 1) * NT)
                done(v.tensor_tensor_scan(incl[:, s], ones[:, 0:NT], tot[:, s], 0.0, ALU.mult, ALU.add))
            done(v.tensor_tensor(incl[:, :], incl[:, :], tot[:, :], ALU.subtract))
            done(v.tensor_tensor(starts[:, :], incl[:, :], ps[0][:, 0:2 * NT], ALU.add))
            v.tensor_copy(info[:, :, 0], node_i[:, :])
            v.tensor_copy(info[:, :, 1], starts[:, 0:NT])
            v.tensor_copy(info[:, :, 2], starts[:, NT:])
            v.tensor_tensor(info[:, :, 3], starts[:, 0:NT], deg_rows[:, 0:NT], ALU.add)
            v.tensor_copy(target_f[:, :], node_i[:, :])
            done(v.tensor_scalar(empty[:, :], deg_rows[:, NT:], 0.0, None, ALU.is_equal))
            done(v.tensor_scalar(target_f[:, :], target_f[:, :], float(ROWS), None, ALU.add))
            done(v.tensor_tensor(target_f[:, :], target_f[:, :], starts[:, NT:], ALU.subtract))
            done(v.tensor_tensor(target_f[:, :], target_f[:, :], empty[:, :], ALU.mult))
            done(v.tensor_tensor(target_f[:, :], target_f[:, :], starts[:, NT:], ALU.add))
            done(v.tensor_copy(row0_i[:, :], target_f[:, :]), "info")
            done(v.tensor_tensor(last_f[:, :], starts[:, NT:], deg_rows[:, NT:], ALU.add))
            done(v.tensor_scalar(last_f[:, :], last_f[:, :], -1.0 - ROWS, None, ALU.add))
            done(v.tensor_scalar(target_f[:, :], empty[:, :], -1.0, 1.0, ALU.mult, ALU.add))
            done(v.tensor_tensor(last_f[:, :], last_f[:, :], target_f[:, :], ALU.mult))
            done(v.tensor_scalar(last_i[:, :], last_f[:, :], float(ROWS), None, ALU.add))

            dve.wait_ge(rowinfo_loaded, 16)
            for c in range(4):
                last = v.tensor_tensor_scan(RS[:, c, :], rowinfo[:, :, c], rowinfo[:, :, c], 0.0, ALU.max, ALU.max)
            done(last)
            done(v.tensor_copy(carry4[:, :], RS[:, :, STEPS - 1]), "lane top")
            after_pe("lane top")
            done(v.tensor_copy(lane_in[:, :], ps[0][0:4, 0:128]))
            done(v.tensor_tensor_scan(lane_top[:, :], lane_in[:, :], lane_in[:, :], 0.0, ALU.max, ALU.max))
            v.memset(lane_excl[:, 0:1], 0.0)
            done(v.tensor_copy(lane_excl[:, 1:128], lane_top[:, 0:127]), "lane excl")
            after_pe("lane excl")
            done(v.tensor_copy(carry4[:, :], ps[0][:, 0:4]))
            for c in range(4):
                last = v.tensor_scalar(RS[:, c, :], RS[:, c, :], carry4[:, c:c + 1], None, ALU.max)
            done(last)
            row_node, row_start, row_first, row_end = (RS[:, c, :] for c in range(4))
            done(v.tensor_tensor(pos[:, :], row_f[:, :], row_first, ALU.subtract))
            done(v.tensor_scalar(pos[:, :], pos[:, :], float(SLOTS), None, ALU.mult))
            done(v.tensor_tensor(pos[:, :], pos[:, :], row_start, ALU.add))
            done(v.tensor_scalar(low_f[:, :], pos[:, :], float(E), None, ALU.min))
            done(v.tensor_copy(pos_i[:, :], low_f[:, :]))
            v.tensor_scalar(low_i[:, :], pos_i[:, :], RUN - 1, None, ALU.bitwise_and)
            done(v.tensor_scalar(high_i[:, :], pos_i[:, :], RUN.bit_length() - 1, None, ALU.arith_shift_right))
            v.tensor_copy(low_f[:, :], low_i[:, :])
            done(v.tensor_copy(high_f[:, :], high_i[:, :]))
            done(v.tensor_scalar(low_f[:, :], low_f[:, :], float(RB), 1.0, ALU.mult, ALU.add))
            done(v.tensor_tensor(table_row[:, :], low_f[:, :], high_f[:, :], ALU.add), "table rows")
            done(v.tensor_tensor(BOUND[:, :, :], bc(pos[:, :].unsqueeze(2), [128, STEPS, SLOTS]),
                                 bc(iota_f[:, 0:SLOTS].unsqueeze(1), [128, STEPS, SLOTS]), ALU.add))
            done(v.tensor_tensor(VALID[:, :, :], BOUND[:, :, :], bc(row_end.unsqueeze(2), [128, STEPS, SLOTS]), ALU.is_lt))
            done(v.tensor_scalar(BOUND[:, :, :], VALID[:, :, :], 0.5, 2 * BIG, ALU.subtract, ALU.mult))
            v.memset(same[:, 0:1], 0.0)
            done(v.tensor_tensor(same[:, 1:], RS[:, 0, 1:STEPS], RS[:, 0, 0:STEPS - 1], ALU.is_equal))
            v.tensor_scalar(same_bound[:, :], same[:, :], 0.5, 2 * BIG, ALU.subtract, ALU.mult)
            v.tensor_tensor(cont[:, :], RS[:, 0, 0:1], RS[:, 0, STEPS - 1:STEPS], ALU.is_equal)
            done(v.tensor_tensor(cont2[:, :], RS[:, 0, 0:1], carry4[:, 0:1], ALU.is_equal))
            done(v.tensor_tensor(cont[:, :], cont[:, :], cont2[:, :], ALU.mult))
            done(v.tensor_scalar(cont2[:, :], cont[:, :], 1.0, BIG, ALU.subtract, ALU.mult))
            def col(k):
                return lane_cols[:, k:k + 1]

            v.tensor_tensor(col(0), RS[:, 0, 0:1], carry4[:, 0:1], ALU.is_equal)
            v.tensor_tensor(col(1), pos[:, 0:1], RS[:, 3, 0:1], ALU.is_lt)
            v.tensor_scalar(col(3), part_id[:, :], float(PAD), None, ALU.add)
            done(v.tensor_scalar(col(2), pos[:, 0:1], float(SLOTS * STEPS), None, ALU.add))
            done(v.tensor_tensor(col(5), col(2), RS[:, 3, 0:1], ALU.is_ge))
            done(v.tensor_tensor(col(6), col(0), col(1), ALU.mult))
            done(v.tensor_tensor(col(7), col(6), col(5), ALU.mult))
            done(v.tensor_tensor(col(4), RS[:, 0, 0:1], col(3), ALU.subtract))
            done(v.tensor_tensor(col(4), col(4), col(7), ALU.mult))
            done(v.tensor_tensor(carry_to_i[:, :], col(4), col(3), ALU.add))
            v.tensor_copy(penalty[:, :], bc(cont2[:, 0:1], [128, H0]))
            done(v.tensor_copy(wide[:, :], bc(cont[:, 0:1], [128, 128])), "cont")
            after_pe("cont")
            v.tensor_copy(penaltyT[:, :], ps[0][0:H0, 0:128])
            done(v.tensor_copy(contT[:, :], ps[1][:, 0:128]), "contT")
            for b in range(2):
                v.memset(fetched_f[:, :, :], 0.0).then_inc(fetch_used[b], 1)
                dve.wait_ge(fetch_used[b], 1)

            dve.wait_ge(weights_loaded, 16 * len(weight_loads))
            for g in range(2):
                dve.wait_ge(al_loaded[g], 16)
                done(v.tensor_reduce(alr[:, g, :, :], view(al_in[:, :], "p (t i o) -> p t i o", t=NTYPE, i=32), AX.X, ALU.add), f"al{g}")
            for t in range(NTYPE):
                v.tensor_copy(view(Wcat[:, t * HXW:t * HXW + D], "p (k h) -> p h k", h=H2), view(Wt_in[:, t, :], "p (h k) -> p h k", h=H2))
                for g in range(2):
                    done(v.tensor_tensor(view(Wprod[:, :], "p (h k) -> p h k", h=H2), view(Wt_in[:, t, :], "p (h k) -> p h k", h=H2),
                                         bc(alr[:, g, t, :].unsqueeze(1), [128, H2, 32]), ALU.mult))
                    done(v.tensor_reduce(Wcat[:, t * HXW + D + g * H2:t * HXW + D + (g + 1) * H2],
                                         view(Wprod[:, :], "p (h k) -> p h k", h=H2), AX.X, ALU.add), "Wcat" if (t, g) == (NTYPE - 1, 1) else None)
            done(v.tensor_copy(ntype_f[:, :], ntype_i[:, :]))
            for t in range(NTYPE):
                last = v.tensor_scalar(type_mask[:, :, t], ntype_f[:, :], float(t), None, ALU.is_equal)
            done(last)

            split(1)

            def fetch(it):
                for b in range(2):
                    for c in range(BF // 2):
                        batch(1, it * BF + (b * (BF // 2) + c))
                    dve.wait_ge(fetch_landed[b], (it + 1) * (16 * FS))
                    at = it * (2 * FS) + b * FS
                    v.tensor_scalar(fetched_f[:, :, :], view(fetched[b][:, :], "p (k s) -> p k s", s=RUN)[:, :, 0:SLOTS], -float(N), None, ALU.add).then_inc(fetch_chain, 1)
                    dve.wait_ge(fetch_chain, it * 4 + (2 * b + 1))
                    v.tensor_tensor(fetched_f[:, :, :], fetched_f[:, :, :], VALID[:, bass.ds(at, FS), :], ALU.mult).then_inc(fetch_chain, 1)
                    dve.wait_ge(fetch_chain, it * 4 + (2 * b + 2))
                    v.tensor_scalar(IX[:, bass.ds(at, FS), 0:SLOTS], fetched_f[:, :, :], float(N), None, ALU.add).then_inc(fetch_used[b], 1)
                    dve.wait_ge(fetch_used[b], it + 2)

            loop(dve, FIT, fetch)
            done(v.tensor_copy(IX[:, 0:STEPS, SLOTS], row_node), "IX")
            for n in range(FIT * BF, NB):
                batch(1, n)
            after_pe("hist1")
            done(v.tensor_copy(outdeg[:, :], ps[4][:, 0:NT]))
            for k, deg in ((0, outdeg[:, :]), (1, deg_rows[:, 0:NT])):
                if k:
                    after_act("sqrt deg0")
                done(v.tensor_scalar(var[:, :], deg, 1.0, None, ALU.add), f"deg{k}")
                after_act(f"sqrt deg{k}")
                done(v.reciprocal(dis[k][:, :], sd[:, :]))

            def attention_steps(name, H, U, dot):
                S = LS[name]
                F = D + H
                rw = 2 * D if dot else D + H
                n_chain = [0]
                per = 7 if dot else 8

                for b in range(2):
                    v.memset(state[b][:, 0:F + H], 0.0).then_inc(S[f"free{b}"], 1)
                    dve.wait_ge(S[f"free{b}"], 1)
                def pair(it):
                    n_chain[0] = 0

                    def link(ins):
                        n_chain[0] += 1
                        ins.then_inc(S["chain"], 1)
                        dve.wait_ge(S["chain"], it * (2 * per) + n_chain[0])

                    for b in range(2):
                        new, old = state[b], state[1 - b]
                        g = view(gathered[b][:, 0:SLOTS * rw], "p (j w) -> p j w", w=rw)
                        sc = scores[:, :, 0:H]
                        i = it * 2 + b
                        dve.wait_ge(S[f"landed{b}"], (it + 1) * (16 * (SLOTS + 1)))
                        if dot:
                            link(v.tensor_tensor(prod[:, :, :], g[:, :, 0:D], bc(dst_row[b][:, :].unsqueeze(1), [128, SLOTS, D]), ALU.mult))
                            link(v.tensor_reduce(sc, view(prod[:, :, :], "p j (h u) -> p j h u", h=H), AX.X, ALU.add))
                            value = g[:, :, D:]
                        else:
                            link(v.tensor_tensor(sc, g[:, :, D:], bc(dst_row[b][:, 0:H].unsqueeze(1), [128, SLOTS, H]), ALU.add))
                            link(v.tensor_scalar(prod[:, :, 0:H], sc, 0.2, None, ALU.mult))
                            link(v.tensor_tensor(sc, sc, prod[:, :, 0:H], ALU.max))
                            value = g[:, :, 0:D]
                        link(v.tensor_tensor(sc, sc, bc(BOUND[:, bass.ds(i, 1), :].rearrange("p o j -> p (o j)").unsqueeze(2), [128, SLOTS, H]), ALU.min))
                        link(v.tensor_reduce(top[:, 0:H], view(sc, "p j h -> p h j"), AX.X, ALU.max))
                        wait(dve, S[f"stored{b}"], it * 16)
                        link(v.scalar_tensor_tensor(new[:, F:F + H], old[:, F:F + H], same_bound[:, bass.ds(i, 1)], top[:, 0:H], ALU.min, ALU.max))
                        v.scalar_tensor_tensor(diff[:, 0:H], old[:, F:F + H], same_bound[:, bass.ds(i, 1)], new[:, F:F + H], ALU.min, ALU.subtract)
                        v.tensor_tensor(view(diff[:, H:(SLOTS + 1) * H], "p (j h) -> p j h", h=H), sc,
                                        bc(new[:, F:F + H].unsqueeze(1), [128, SLOTS, H]), ALU.subtract).then_inc(S["diffs"], 1)
                        dve.wait_ge(S["exps"], i + 1)
                        m = view(msg[:, 0:SLOTS * F], "p (j f) -> p j f", f=F)
                        link(v.tensor_tensor(m[:, :, D:], view(expd[:, H:(SLOTS + 1) * H], "p (j h) -> p j h", h=H),
                                             bc(VALID[:, bass.ds(i, 1), :].rearrange("p o j -> p (o j)").unsqueeze(2), [128, SLOTS, H]), ALU.mult))
                        v.tensor_tensor(view(m[:, :, 0:D], "p j (u h) -> p j u h", h=H), view(value, "p j (u h) -> p j u h", h=H),
                                        bc(m[:, :, D:].unsqueeze(2), [128, SLOTS, U, H]), ALU.mult).then_inc(S[f"free{b}"], 1)
                        dve.wait_ge(S[f"free{b}"], it + 2)
                        v.tensor_reduce(slot_sum[:, 0:F], view(m, "p j f -> p f j"), AX.X, ALU.add)
                        link(v.scalar_tensor_tensor(view(scaled[:, 0:F], "p (u h) -> p u h", h=H), view(old[:, 0:F], "p (u h) -> p u h", h=H),
                                                    same[:, bass.ds(i, 1)], bc(expd[:, 0:H].unsqueeze(1), [128, U + 1, H]), ALU.mult, ALU.mult))
                        v.tensor_tensor(new[:, 0:F], scaled[:, 0:F], slot_sum[:, 0:F], ALU.add).then_inc(S["state_ready"], 1)
                        dve.wait_ge(S["state_ready"], i + 1)
                    assert n_chain[0] == 2 * per

                loop(dve, HALF, pair)

            def sum_steps(name):
                S = LS[name]
                for b in range(2):
                    v.memset(state[b][:, 0:D], 0.0).then_inc(S[f"free{b}"], 1)
                    dve.wait_ge(S[f"free{b}"], 1)
                def pair(it):
                    for b in range(2):
                        i = it * 2 + b
                        g = view(gathered[b][:, 0:SLOTS * D], "p (j w) -> p w j", w=D)
                        dve.wait_ge(S[f"landed{b}"], (it + 1) * (16 * SLOTS))
                        v.tensor_reduce(slot_sum[:, 0:D], g, AX.X, ALU.add).then_inc(S[f"free{b}"], 1)
                        dve.wait_ge(S[f"free{b}"], it + 2)
                        wait(dve, S[f"stored{b}"], it * 16)
                        v.scalar_tensor_tensor(state[b][:, 0:D], state[1 - b][:, 0:D], same[:, bass.ds(i, 1)], slot_sum[:, 0:D], ALU.mult, ALU.add).then_inc(S["state_ready"], 1)
                        dve.wait_ge(S["state_ready"], i + 1)

                loop(dve, HALF, pair)

            def carries(name, H, U):
                F = D + H
                end = state[1]
                done(v.memset(CTx[:, :], 0.0), "steps " + name)
                if H:
                    after_pe("m " + name)
                    done(v.tensor_copy(mT[0:H, :], ps[0][0:H, 0:128]))
                    done(v.tensor_tensor_scan(MT[0:H, :], penaltyT[0:H, :], mT[0:H, :], -BIG, ALU.add, ALU.max))
                    v.memset(MprevT[0:H, 0:1], -BIG)
                    done(v.tensor_copy(MprevT[0:H, 1:128], MT[0:H, 0:127]), "MprevT " + name)
                    after_pe("MM " + name)
                    done(v.tensor_copy(MM[:, 0:2 * H], ps[0][:, 0:2 * H]))
                    v.tensor_tensor(md[:, 0:H], end[:, F:F + H], MM[:, 0:H], ALU.subtract)
                    done(v.scalar_tensor_tensor(md[:, H:2 * H], MM[:, H:2 * H], cont2[:, 0:1], MM[:, 0:H], ALU.add, ALU.subtract), "md " + name)
                    after_act("me " + name)
                    done(v.tensor_scalar(me[:, H:2 * H], me[:, H:2 * H], cont[:, 0:1], None, ALU.mult))
                    v.tensor_tensor(view(Es[:, 0:F], "p (u h) -> p u h", h=H), view(end[:, 0:F], "p (u h) -> p u h", h=H),
                                    bc(me[:, 0:H].unsqueeze(1), [128, U + 1, H]), ALU.mult)
                    done(v.tensor_copy(view(Gs[:, 0:F], "p (u h) -> p u h", h=H), bc(me[:, H:2 * H].unsqueeze(1), [128, U + 1, H])), "EG " + name)
                after_pe("EG " + name)
                done(v.tensor_copy(EsT[:, 0:128], ps[1][:, 0:128]))
                if H:
                    v.tensor_copy(EsT[0:H, 128:256], ps[1][0:H, 128:256])
                    v.tensor_copy(GsT[:, 0:128], ps[2][:, 0:128])
                    done(v.tensor_copy(GsT[0:H, 128:256], ps[2][0:H, 128:256]))
                    v.tensor_tensor_scan(CT[:, 0:128], GsT[:, 0:128], EsT[:, 0:128], 0.0, ALU.mult, ALU.add)
                    done(v.tensor_tensor_scan(CT[0:H, 128:256], GsT[0:H, 128:256], EsT[0:H, 128:256], 0.0, ALU.mult, ALU.add))
                    v.tensor_copy(CTx[0:H, 129:256], CT[0:H, 128:255])
                else:
                    done(v.tensor_tensor_scan(CT[:, 0:128], contT[:, :], EsT[:, 0:128], 0.0, ALU.mult, ALU.add))
                done(v.tensor_copy(CTx[:, 1:128], CT[:, 0:127]), "CTx " + name)
                after_pe("C " + name)
                if H:
                    v.tensor_copy(carry_row[:, F:F + H], MM[:, H:2 * H])
                done(v.tensor_copy(carry_row[:, 0:F], ps[0][:, 0:F]), "carry " + name)

            def merge_softmax(name, H, U, target):
                F = D + H
                w = F + H
                fs = view(final_state[:, 0:NT * w], "p (t w) -> p t w", w=w)
                fc = view(final_carry[:, 0:NT * w], "p (t w) -> p t w", w=w)
                m, mc = fm[:, :, 0:H], fc[:, :, F:]
                dve.wait_ge(LS[name]["final_landed"], 16 * NT)
                dve.wait_ge(carries_landed, 16 * (layers.index(name) + 1))
                done(v.tensor_tensor(m, fs[:, :, F:], mc, ALU.max))
                d = view(fd[:, 0:2 * NT * H], "p (g t h) -> p g t h", g=2, h=H)
                e = view(fe[:, 0:2 * NT * H], "p (g t h) -> p g t h", g=2, h=H)
                v.tensor_tensor(d[:, 0], fs[:, :, F:], m, ALU.subtract)
                done(v.tensor_tensor(d[:, 1], mc, m, ALU.subtract), "fd " + name)
                after_act("fe " + name)
                for part, f in ((fs, 0), (fc, 1)):
                    p4 = view(part[:, :, 0:F], "p t (u h) -> p t u h", h=H)
                    last = v.tensor_tensor(p4, p4, bc(e[:, f].unsqueeze(2), [128, NT, U + 1, H]), ALU.mult)
                done(last)
                done(v.tensor_tensor(fs[:, :, 0:F], fs[:, :, 0:F], fc[:, :, 0:F], ALU.add))
                done(v.tensor_scalar(den[:, :, 0:H], fs[:, :, D:F], 1e-30, None, ALU.max))
                done(v.reciprocal(den[:, :, 0:H], den[:, :, 0:H]))
                done(v.tensor_tensor(target, view(fs[:, :, 0:D], "p t (u h) -> p t u h", h=H), bc(den[:, :, 0:H].unsqueeze(2), [128, NT, U, H]), ALU.mult))

            def over_nodes(col):
                return bc(col[:, :].unsqueeze(2), [128, NT, D])

            def over_tiles(row):
                return bc(row[:, :].unsqueeze(1), [128, NT, D])

            def layernorm(Y, name, g=None, b=None, masked=False):
                done(v.tensor_reduce(mean[:, :], Y[:, :, :], AX.X, ALU.add))
                done(v.tensor_scalar(mean[:, :], mean[:, :], 1.0 / D, None, ALU.mult))
                done(v.tensor_tensor(Y[:, :, :], Y[:, :, :], over_nodes(mean), ALU.subtract))
                done(v.tensor_tensor(final_carry_sq, Y[:, :, :], Y[:, :, :], ALU.mult))
                done(v.tensor_reduce(var[:, :], final_carry_sq, AX.X, ALU.add))
                done(v.tensor_scalar(var[:, :], var[:, :], 1.0 / D, None, ALU.mult), "var " + name)
                after_act("sd " + name)
                done(v.reciprocal(rstd[:, :], sd[:, :]))
                done(v.tensor_tensor(Y[:, :, :], Y[:, :, :], over_nodes(rstd), ALU.mult), None if g is not None or masked else name)
                if g is not None:
                    done(v.tensor_tensor(Y[:, :, :], Y[:, :, :], over_tiles(g), ALU.mult))
                    done(v.tensor_tensor(Y[:, :, :], Y[:, :, :], over_tiles(b), ALU.add), name)

            def next_x(name):
                layernorm(X, name, masked=True)
                done(v.tensor_scalar(X[:, NT - 1, :], X[:, NT - 1, :], row_ok[:, 0:1], None, ALU.mult), name)

            final_carry_sq = view(final_carry[:, 0:NT * D], "p (t d) -> p t d", d=D)

            attention_steps("att0", H0, D // H0, True)
            carries("att0", H0, D // H0)
            merge_softmax("att0", H0, D // H0, view(R[:, :, :], "p t (h u) -> p t u h", h=H0))
            done(v.tensor_tensor(R[:, :, :], R[:, :, :], X[:, :, :], ALU.add))
            layernorm(R, "ln1", rows_in["L0_gnn_ln1_g"], rows_in["L0_gnn_ln1_b"])
            S = TS["ffn"]

            def ffn_hidden(t, second_of):
                dve.wait_ge(S["first"], t + 1)
                p1 = view(ps[1][:, :], "p (c n) -> p c n", c=FC)
                v.tensor_tensor(hb[:, :, :], p1, bc(b1[:, :].unsqueeze(2), [128, FC, 128]), ALU.add).then_inc(S["read"], 1)
                dve.wait_ge(S["read"], t + 1)
                v.scalar_tensor_tensor(hn[:, :, :], hb[:, :, :], 0.0, bc(pw[:, :].unsqueeze(2), [128, FC, 128]), ALU.min, ALU.mult).then_inc(S["chain"], 1)
                dve.wait_ge(S["chain"], t + 1)
                if second_of is not None:
                    ffn_result(second_of)
                v.scalar_tensor_tensor(view(hT[:, :], "p (c n) -> p c n", c=FC), hb[:, :, :], 0.0, hn[:, :, :], ALU.max, ALU.add).then_inc(S["hidden"], 1)
                dve.wait_ge(S["hidden"], t + 1)

            def ffn_result(t):
                dve.wait_ge(S["second"], t + 1)
                v.tensor_tensor(R[:, bass.ds(t, 1), :], R[:, bass.ds(t, 1), :], ps[2][:, 0:D].unsqueeze(1), ALU.add).then_inc(S["result"], 1)

            ffn_hidden(0, None)
            ffn_hidden(1, 0)
            with dve.Fori(2, NT) as t:
                ffn_hidden(t, t - 1)
            ffn_result(NT - 1)
            dve.wait_ge(S["result"], NT)
            done(v.tensor_tensor(R[:, :, :], R[:, :, :], over_tiles(rows_in["L0_gnn_b2"]), ALU.add))
            layernorm(R, "ln2", rows_in["L0_gnn_ln2_g"], rows_in["L0_gnn_ln2_b"])
            done(v.tensor_tensor(X[:, :, :], X[:, :, :], R[:, :, :], ALU.add))
            next_x("x0")

            def gcn_sum(name, k):
                done(v.tensor_tensor(T1[:, :, :], X[:, :, :], over_nodes(dis[k]), ALU.mult), "table " + name)
                sum_steps(name)
                carries(name, 0, D)
                fs = view(final_state[:, 0:NT * D], "p (t w) -> p t w", w=D)
                fc = final_carry_sq
                dve.wait_ge(LS[name]["final_landed"], 16 * NT)
                dve.wait_ge(carries_landed, 16 * (layers.index(name) + 1))
                done(v.tensor_tensor(fs, fs, fc, ALU.add))
                done(v.tensor_tensor(fs, fs, T1[:, :, :], ALU.add))
                done(v.tensor_tensor(R[:, :, :], fs, over_nodes(dis[k]), ALU.mult), "agg3" if k else "agg1")

            gcn_sum("sum1", 0)
            done(v.tensor_tensor(X[:, :, :], X[:, :, :], R[:, :, :], ALU.add))
            next_x("x1")

            S = TS["typed"]

            def typed(t):
                S = TS["typed"]
                dve.wait_ge(S["first"], t + 1)
                for k in range(NTYPE):
                    bank, at = (ps[1], k * HXW) if k < 3 else (ps[2], (k - 3) * HXW)
                    mask = view(type_mask[:, :, :], "p t k -> p (t k)")[:, bass.ds(t * NTYPE + k, 1)]
                    dest = hx2 if k == NTYPE - 1 else hx
                    if k == NTYPE - 1:
                        wait(dve, S["written"], t * 32)
                    if k == 0:
                        ins = v.tensor_scalar(dest[:, :], bank[:, at:at + HXW], mask, None, ALU.mult)
                    else:
                        ins = v.scalar_tensor_tensor(dest[:, :], bank[:, at:at + HXW], mask, hx[:, :], ALU.mult, ALU.add)
                    if k < NTYPE - 1:
                        ins.then_inc(S["chain"], 1)
                        dve.wait_ge(S["chain"], t * (NTYPE - 1) + (k + 1))
                ins.then_inc(S["result"], 1)

            loop(dve, NT, typed)
            attention_steps("att2", H2, D // H2, False)
            carries("att2", H2, D // H2)
            merge_softmax("att2", H2, D // H2, view(T1[:, :, :], "p t (u h) -> p t u h", h=H2))
            dve.wait_ge(S["second"], NT)
            done(v.tensor_tensor(R[:, :, :], R[:, :, :], T1[:, :, :], ALU.add))
            done(v.tensor_tensor(R[:, :, :], R[:, :, :], over_tiles(rows_in["L2_gnn_b_res"]), ALU.add))
            done(v.tensor_scalar(R[:, :, :], R[:, :, :], 0.0, None, ALU.max))
            done(v.tensor_tensor(X[:, :, :], X[:, :, :], R[:, :, :], ALU.add))
            next_x("x2")
            after_pe("linT")
            done(v.tensor_copy(linT[:, :], ps[0][:, 0:128]))

            gcn_sum("sum3", 1)
            S = TS["gcn"]
            with dve.Fori(0, NT) as t:
                dve.wait_ge(S["second"], t + 1)
                v.tensor_tensor(X[:, bass.ds(t, 1), :], X[:, bass.ds(t, 1), :], ps[2][:, 0:D].unsqueeze(1), ALU.add).then_inc(S["result"], 1)
            dve.wait_ge(S["result"], NT)
            done(v.tensor_tensor(X[:, :, :], X[:, :, :], over_tiles(rows_in["L3_gnn_lin_b"]), ALU.add))
            layernorm(X, "x3")


NAMES = ("x", "src", "dst", "node_type_5", "L0_gnn_Wq", "L0_gnn_Wk", "L0_gnn_Wv", "L0_gnn_ln1_g",
         "L0_gnn_ln1_b", "L0_gnn_ln2_g", "L0_gnn_ln2_b", "L0_gnn_W1", "L0_gnn_b1", "L0_gnn_prelu_w",
         "L0_gnn_W2", "L0_gnn_b2", "L2_gnn_W_typed", "L2_gnn_al_w", "L2_gnn_ar_w", "L2_gnn_W_res",
         "L2_gnn_b_res", "L3_gnn_W", "L3_gnn_b", "L3_gnn_lin_W", "L3_gnn_lin_b")


def kernel(**inputs):
    import numpy as np
    import concourse.bacc as bacc
    from concourse.bass_utils import run_bass_kernel_spmd as run

    nc = bacc.Bacc("TRN2", target_bir_lowering=False, num_devices=1)
    arrays, aps = {}, {}
    for name in NAMES:
        array = np.ascontiguousarray(inputs[name])
        arrays["in_" + name] = array
        aps[name] = nc.dram_tensor("in_" + name, array.shape, mybir.dt.from_np(array.dtype), kind="ExternalInput").ap()
    out = nc.dram_tensor("out_x", tuple(inputs["x"].shape), F32, kind="ExternalOutput").ap()
    gnn_kernel(nc, aps, out)
    return run(nc, [arrays], core_ids=[0]).results[0]["out_x"]
```

```python
from contextlib import ExitStack

import concourse.bass as bass
from concourse import mybir

ALU = mybir.AluOpType
ACT = mybir.ActivationFunctionType
AX = mybir.AxisListType
F32 = mybir.dt.float32
BF16 = mybir.dt.bfloat16
I32 = mybir.dt.int32

BIG = 1e30
NEG_SLOPE = 0.2
ROUND = 12582912.0
EPS = 1e-5


class Signals(dict):

    def __init__(self, owner, sem):
        super().__init__()
        self.owner, self.sem = owner, sem

    def __missing__(self, name):
        self[name] = self.sem(f"{self.owner}_{name}")
        return self[name]


def gnn_kernel(nc, a, out):
    N, D = a["x"].shape
    E = a["src"].shape[0]
    LANES = 128
    NT = -(-N // LANES)
    LAST = N - (NT - 1) * LANES
    PAD = NT * LANES
    SLOTS = 6
    GROUP = 4
    RUN = 32
    assert GROUP * SLOTS <= RUN
    STEPS = -(-((E + N * (SLOTS - 1)) // SLOTS) // LANES)
    STEPS += STEPS % 2
    BUFFERS = 3
    TURNS = STEPS // BUFFERS
    assert TURNS * BUFFERS == STEPS
    ROWS = LANES * STEPS
    H0 = 8
    H2 = 4
    NTYPE = a["L2_gnn_W_typed"].shape[0]
    FF = a["L0_gnn_W1"].shape[1]
    FC = FF // 128
    EP = 125
    EC = E // EP
    NB = 25
    assert NB == NT
    BUFS = 4
    BATCH = EC // NB
    HA = (BATCH - BATCH // 2, BATCH // 2)
    assert EP * EC == E and NB * BATCH == EC
    LO = 64
    RB = -(-(RUN + E + RUN) // RUN)
    RBW = RB * RUN
    GROUPS = STEPS // GROUP
    CHUNKS = 3
    CHUNK = GROUPS // CHUNKS
    assert CHUNKS == 3
    assert CHUNKS * CHUNK * GROUP == STEPS
    HXW = D + 2 * H2
    J = 13
    ESTEPS = -(-(-(-E // LANES)) // J)
    ESTEPS += ESTEPS % 2
    EHALF = ESTEPS // 2
    EL = ESTEPS * J
    EDGES = LANES * EL
    assert EDGES - EL < E

    with ExitStack() as ctx:
        def sb(name, shape, dt=F32):
            return ctx.enter_context(nc.sbuf_tensor(name, shape, dt))

        def sem(name):
            return ctx.enter_context(nc.semaphore(name))

        def dram(name, shape, dt=F32):
            return nc.dram_tensor(name, shape, dt).ap()

        ps = [ctx.enter_context(nc.psum_tensor(f"ps{i}", [128, 512], F32)) for i in range(8)]

        turned_in = (ps[0], ps[7])
        product_in = ((ps[1], ps[2], ps[5]), (ps[3], ps[4], ps[6]))

        shifted = dram("shifted_sources", [RUN * RB, RUN], I32)
        rowinfo_d = dram("rowinfo_d", [ROWS + PAD, 4])
        q_d = dram("q_d", [PAD, D])
        kv_d = dram("kv_d", [PAD, 2 * D])
        y_d = [dram(f"y{k}_d", [PAD, D]) for k in range(2)]
        h_d = dram("h_d", [PAD, D + H2])
        hr_d = dram("hr_d", [PAD, H2])
        hre_d = dram("hre_d", [EDGES + PAD, H2])
        W0 = D + 2 * H0
        W2_ = D + 2 * H2
        width = {"att0": W0, "sum1": D, "att2": W2_, "sum3": D}
        stored_rows = {"att0": ROWS, "sum1": EDGES, "att2": EDGES, "sum3": EDGES}
        state_d = {n: dram(f"state_{n}", [stored_rows[n] + 1, w]) for n, w in width.items()}
        carry_d = {n: dram(f"carry_{n}", [PAD + LANES, w]) for n, w in width.items()}

        X = sb("X", [128, NT, D])
        R = sb("R", [128, NT, D])
        T1_ends = sb("T1_ends", [128, max(NT * D, EL * H2)])
        T1 = T1_ends[:, 0:NT * D].rearrange("p (t d) -> p t d", d=D)
        score_ends = T1_ends[:, 0:EL * H2].rearrange("p (e h) -> p e h", h=H2)
        finals = sb("finals", [128, 2 * NT * W0])
        final_state, final_carry = finals[:, 0:NT * W0], finals[:, NT * W0:]
        run = [finals[:, b * (J + 1) * W2_:(b + 1) * (J + 1) * W2_] for b in range(2)]
        gathered = [sb(f"gathered{b}", [128, max(SLOTS * 2 * D, J * (D + H2))]) for b in range(2)]
        src_lanes = sb("src_lanes", [128, (ESTEPS + 2) * J], I32)
        dst_lanes = sb("dst_lanes", [128, EL + 2], I32)
        dst_lanes_f = sb("dst_lanes_f", [128, EL + 2])
        same_edge = sb("same_edge", [128, EL])
        penalty_edge = sb("penalty_edge", [128, ESTEPS, J + 1])
        edge_scores = sb("edge_scores", [128, J + 1, H2])
        last_maximum = sb("last_maximum", [128, J, H2])
        hr_enter = sb("hr_enter", [128, H2])
        enters = sb("enters", [128, 1])
        weighted = finals[:, 2 * (J + 1) * W2_:2 * (J + 1) * W2_ + J * (D + H2)]
        gathered.append(finals[:, 0:SLOTS * 2 * D])
        dst_row = [sb(f"dst_row{b}", [128, D]) for b in range(2)] + [finals[:, SLOTS * 2 * D:SLOTS * 2 * D + D]]
        prod = sb("prod", [128, SLOTS, D])
        msg = sb("msg", [128, SLOTS * (D + H0)])
        state = [sb(f"state{b}", [128, W0]) for b in range(2)] + [final_carry[:, 0:W0]]
        lane_end = {"att0": state[(STEPS - 1) % BUFFERS], "sum1": state[1], "att2": state[1], "sum3": state[1]}
        index_cols = [sb(f"index_cols{b}", [128, max(SLOTS + 1, J)], I32) for b in range(BUFFERS)]
        IX = sb("IX", [128, STEPS + BUFFERS, SLOTS + 1])
        VALID = sb("VALID", [128, STEPS, SLOTS])
        BOUND = sb("BOUND", [128, STEPS, SLOTS])
        same = sb("same", [128, STEPS])
        same_bound = sb("same_bound", [128, STEPS])
        scores = sb("scores", [128, SLOTS, H0])
        top = sb("top", [128, H0])
        diff = sb("diff", [128, max((SLOTS + 1) * H0, 2 * J * H2)])
        expd = sb("expd", [128, max((SLOTS + 1) * H0, 2 * J * H2)])
        slot_sum = sb("slot_sum", [128, D + H0])
        scaled = sb("scaled", [128, D + H0])

        edge_i = sb("edge_i", [128, EC], I32)
        part_i = sb("part_i", [128, EC], I32)
        assert 2 * EC <= gathered[0].shape[1]
        lo_b = sb("lo_b", [128, EC], BF16)
        hi_b = sb("hi_b", [128, EC], BF16)
        oh_lo = [sb(f"oh_lo{b}", [128, HA[b], LO], BF16) for b in range(2)]
        oh_hi = [sb(f"oh_hi{b}", [128, HA[b], 2 * NT], BF16) for b in range(2)]
        zero_b = sb("zero_b", [128, 128], BF16)
        iota_i = sb("iota_i", [128, 128], I32)
        iota_hi_i = sb("iota_hi_i", [128, 2 * NT], I32)
        node_i = sb("node_i", [128, NT], I32)
        row_i = sb("row_i", [128, STEPS], I32)
        part_id_i = sb("part_id_i", [128, 1], I32)
        iota_f = sb("iota_f", [128, 128])
        iota_lo_b = sb("iota_lo_b", [128, LO], BF16)
        iota_hi_b = sb("iota_hi_b", [128, 2 * NT], BF16)
        row_f = sb("row_f", [128, STEPS])
        part_id = sb("part_id", [128, 1])
        ident = sb("ident", [128, 128])
        before = sb("before", [128, 128])
        ones = sb("ones", [128, 128])
        zeros = sb("zeros", [128, 4 * STEPS])
        deg_rows = sb("deg_rows", [128, 2 * NT])
        tot = sb("tot", [128, 2 * NT])
        incl = sb("incl", [128, 2 * NT])
        starts = sb("starts", [128, 2 * NT])
        first_f = sb("first_f", [128, 1])
        line_f = sb("line_f", [128, NT])
        line_i = sb("line_i", [128, NT], I32)
        counts = sb("counts", [128, NT])
        node_f = sb("node_f", [128, NT])
        edge_starts = sb("edge_starts", [128, NT + 1])
        ones_b = sb("ones_b", [128, 1], BF16)
        is_first = sb("is_first", [128, 1])
        lines = [gathered[k // 2][:, (k % 2) * EC:(k % 2 + 1) * EC].bitcast(I32) for k in range(BUFS)]
        smaller = lo_b
        node_along = R[:, :, :].rearrange("p t d -> p (t d)").bitcast(I32)
        past_first = T1_ends[:, 0:PAD // 2].bitcast(BF16)
        info = sb("info", [128, NT, 4])
        row0_i = sb("row0_i", [128, NT], I32)
        last_f = sb("last_f", [128, NT])
        last_i = sb("last_i", [128, NT], I32)
        last_edge_i = sb("last_edge_i", [128, NT], I32)
        first_edge_i = sb("first_edge_i", [128, NT], I32)
        empty = sb("empty", [128, NT])
        target_f = sb("target_f", [128, NT])
        neutral = [sb("neutral0", [128, W0]), sb("neutral2", [128, W2_])]
        lane_cols = sb("lane_cols", [128, 8])
        carry_to_i = sb("carry_to_i", [128, 1], I32)
        carry_to_edge_i = sb("carry_to_edge_i", [128, 1], I32)
        rowinfo = sb("rowinfo", [128, STEPS, 4])
        RS = sb("RS", [128, 4, STEPS])
        lane_top = sb("lane_top", [4, 128])
        lane_excl = sb("lane_excl", [4, 128])
        lane_in = sb("lane_in", [4, 128])
        carry4 = sb("carry4", [128, 4])
        pos = sb("pos", [128, STEPS])
        pos_i = sb("pos_i", [128, STEPS], I32)
        low_i = sb("low_i", [128, STEPS], I32)
        high_i = sb("high_i", [128, STEPS], I32)
        low_f = sb("low_f", [128, STEPS])
        high_f = sb("high_f", [128, STEPS])
        table_row = sb("table_row", [128, STEPS])
        cont = sb("cont", [128, 1])
        cont2 = sb("cont2", [128, 1])
        penalty = sb("penalty", [128, H0])
        penaltyT = sb("penaltyT", [H0, 128])
        contT = sb("contT", [128, 128])
        penaltyT_edge = sb("penaltyT_edge", [H0, 128])
        contT_edge = sb("contT_edge", [128, 128])
        cont2_edge = sb("cont2_edge", [128, 1])
        cont_edge = sb("cont_edge", [128, 1])
        fetch_row_i = sb("fetch_row_i", [128, GROUPS], I32)
        most = SLOTS * (GROUP - 1) - (GROUP - 1) + 1
        assert most * CHUNK * SLOTS <= GROUPS * RUN
        place = [SLOTS * 2 * D + D, NT * W0 + W0, NT * W0 + W0 + GROUPS * RUN]
        assert place[0] + GROUPS * RUN <= NT * W0 and place[2] + GROUPS * RUN <= 2 * NT * W0
        fetched_f, fetched, picked_parts = (finals[:, at:at + GROUPS * RUN] for at in place)
        fetched_f, fetched = (x.rearrange("p (k s) -> p k s", s=RUN) for x in (fetched_f, fetched))
        fetched = fetched.bitcast(I32)
        picked = sb("picked", [128, CHUNK, SLOTS])
        dis = [sb(f"dis{k}", [128, NT]) for k in range(2)]
        outdeg = sb("outdeg", [128, NT])
        row_ok = sb("row_ok", [128, 1])

        xs = [sb(f"xs{b}", [128, 128]) for b in range(2)]
        xT = [sb(f"xT{b}", [128, 128]) for b in range(2)]
        hT = sb("hT", [128, FC * 128])
        hidden = (hT[:, :], msg[:, 0:FC * 128])
        hb = sb("hb", [128, FC, 128])
        hn = sb("hn", [128, FC, 128])
        wide, Wprod, following, corner = (hn[:, c, :] for c in range(4))
        proj = [sb(f"proj{b}", [128, 3 * D]) for b in range(2)]

        Wqkv = sb("Wqkv", [128, 3 * D])
        W1 = sb("W1", [128, FF])
        W2 = sb("W2", [128, FC, D])
        b1 = sb("b1", [128, FC])
        pw = sb("pw", [128, FC])
        rows_in = {n: sb("row_" + n, [128, D]) for n in
                   ("L0_gnn_ln1_g", "L0_gnn_ln1_b", "L0_gnn_ln2_g", "L0_gnn_ln2_b", "L0_gnn_b2",
                    "L2_gnn_b_res", "L3_gnn_lin_b")}
        Wt_in = sb("Wt_in", [128, NTYPE, D])
        alr = sb("alr", [128, 2, NTYPE, 32])
        al_rows = sb("al_rows", [128, 2, 2, 32])
        al_sums = sb("al_sums", [128, 2, 2])
        al_pieces = [(c, min(128, NTYPE * 32 - c * 128)) for c in range(-(-NTYPE * 32 // 128))]
        Wcat = sb("Wcat", [128, NTYPE * HXW + D])
        ntype_i = sb("ntype_i", [128, NT], I32)
        ntype_f = sb("ntype_f", [128, NT])
        type_mask = sb("type_mask", [128, NT, NTYPE])
        hx = sb("hx", [128, HXW])
        hx2 = [sb(f"hx2{b}", [128, HXW]) for b in range(2)]
        W3 = sb("W3", [128, D])
        b3 = sb("b3", [128, 1])
        lin_in = sb("lin_in", [128, D])
        linT = sb("linT", [128, D])
        eps_c = sb("eps_c", [128, 1])

        stats = sb("stats", [128, NT, 6])
        apart = sb("apart", [128, NT])
        mean = sb("mean", [128, NT])
        var = sb("var", [128, NT])
        sd = sb("sd", [128, NT])
        rstd = sb("rstd", [128, NT])
        den = sb("den", [128, NT, H0])
        fm = sb("fm", [128, NT, H0])
        fd = sb("fd", [128, 2 * NT * H0])
        fe = sb("fe", [128, 2 * NT * H0])

        mT = sb("mT", [H0, 128])
        MT = sb("MT", [H0, 128])
        MprevT = sb("MprevT", [H0, 128])
        MM = sb("MM", [128, 2 * H0])
        md = sb("md", [128, 2 * H0])
        me = sb("me", [128, 2 * H0])
        Es = sb("Es", [128, D + H0])
        Gs = sb("Gs", [128, D + H0])
        EsT = sb("EsT", [128, 256])
        GsT = sb("GsT", [128, 256])
        CT = sb("CT", [128, 256])
        CTx = sb("CTx", [128, 256])
        carry_row = sb("carry_row", [128, W0])

        assert ROWS * 1.0 < 2 ** 23

        halves = (range(0, -(-NT // 2)), range(-(-NT // 2), NT))

        def wait(eng, signal, value):
            if not (isinstance(value, int) and value <= 0):
                eng.wait_ge(signal, value)

        def loop(eng, n, turn):
            turn(0)
            with eng.Fori(1, n) as i:
                turn(i)

        def tiles(eng, turn):
            turn(0, 0)
            turn(1, 1)
            with eng.Fori(1, NT // 2) as it:
                for b in range(2):
                    turn(it * 2 + b, b)
            if NT % 2:
                turn(NT - 1, 0)

        x_loaded, weights_loaded = sem("x_loaded"), sem("weights_loaded")
        ends_loaded = [sem("dst_loaded"), sem("src_loaded")]
        shifted_ready, zeros_ready, rowinfo_zeroed = sem("shifted_ready"), sem("zeros_ready"), sem("rowinfo_zeroed")
        iotas_ready = sem("iotas_ready")
        neutral_written = sem("neutral_written")
        lanes_loaded = sem("lanes_loaded")
        types_loaded = sem("types_loaded")
        hr_scattered = [sem(f"hr_scattered{b}") for b in range(2)]
        hr_entered, score_ends_loaded = sem("hr_entered"), sem("score_ends_loaded")
        dve_done = sem("dve_done")
        onehots_ready = [sem("onehots_ready0"), sem("onehots_ready1")]
        onehots_used = [sem("onehots_used0"), sem("onehots_used1")]
        rowinfo_scattered, rowinfo_loaded = sem("rowinfo_scattered"), sem("rowinfo_loaded")
        fetch_landed = [sem(f"fetch_landed{c}") for c in range(CHUNKS)]
        line_landed = [sem(f"line_landed{k}") for k in range(BUFS)]
        line_counted = sem("line_counted")
        stored_out = sem("stored_out")
        carries_landed = sem("carries_landed")
        LS = {n: Signals(n, sem) for n in ("att0", "sum1", "att2", "sum3")}
        TS = {n: Signals(n, sem) for n in ("proj", "ffn", "typed", "gcn")}

        layers, attentions, sums = ("att0", "sum1", "att2", "sum3"), ("att0", "att2"), ("sum1", "sum3")
        parts = ("att0 0", "att0 1", "att2 0", "att2 1")
        norms = ("ln1", "ln2", "x0", "x1", "x2", "x3")
        turns = {"var": norms, "sd": norms, "steps": layers, "carry": layers, "CTx": layers, "C": layers,
                 "EG": layers, "table": sums, "m": attentions, "MM": attentions, "md": attentions,
                 "me": attentions, "fd": parts, "fe": parts, "MprevT": attentions}
        numbered = {"x": "0123", "ln": "12", "deg": "01", "sqrt deg": "01", "IX": "012"}
        prepared = {"V:": ("first ends", "past first", "lines", "consts", "edge starts", "deg rows", "info",
                           "al sums", "cont edges", "contT edges", "lane top", "lane excl", "table rows", "cont", "contT"),
                    "P:": ("lines", "edge ends", "sums", "al rows", "cont edges", "lane top", "lane excl", "cont", "hist")}
        events = {}

        def event(name):
            family, _, turn = name.partition(" ")
            order = turns.get(family[2:])
            order = attentions if family == "V:EG" else order
            if name[2:] in prepared.get(name[:2], ()):
                family, turn, order = name[:2] + "prepared", name[2:], prepared[name[:2]]
            elif name[-1] in numbered.get(name[2:-1], ""):
                family, turn, order = name[:-1].replace(" ", "_"), name[-1], numbered[name[2:-1]]
            elif order is None or turn not in order:
                family, turn, order = name.replace(" ", "_"), "", ("",)
            if family not in events:
                events[family] = sem("done_" + family.replace(":", "_"))
            return events[family], order.index(turn) + 1

        block = ctx.enter_context(nc.Block())

        def bc(ap, shape):
            return ap.to_broadcast(shape)

        def view(ap, spec, **kw):
            return ap.rearrange(spec, **kw)

        weight_loads = [(Wqkv[:, n * D:(n + 1) * D], a["L0_gnn_W" + "qkv"[n]]) for n in range(3)]
        weight_loads += [(W1[:, :], a["L0_gnn_W1"]), (W2[:, :, :], view(a["L0_gnn_W2"], "(c p) d -> p c d", p=128)),
                         (b1[:, :], view(a["L0_gnn_b1"], "(c p) -> p c", p=128)),
                         (pw[:, :], view(a["L0_gnn_prelu_w"], "(c p) -> p c", p=128)),
                         (b3[:, :], view(a["L3_gnn_b"], "(p o) -> p o", o=1)),
                         (Wcat[:, NTYPE * HXW:], a["L2_gnn_W_res"]), (W3[:, :], a["L3_gnn_W"]),
                         (lin_in[:, :], a["L3_gnn_lin_W"]), (Wt_in[:, :, :], view(a["L2_gnn_W_typed"], "t i o -> i t o"))]
        weight_loads += [(tile[:, :], a[n].partition_broadcast(128)) for n, tile in rows_in.items()]
        weight_loads += [(al_rows[0:rows, g, c, :], view(a[f"L2_gnn_a{'lr'[g]}_w"], "t i o -> (t i) o")[c * 128:c * 128 + rows, :])
                         for g in range(2) for c, rows in al_pieces]
        type_loads = [(ntype_i[:, 0:NT - 1], view(a["node_type_5"][0:(NT - 1) * 128], "(t p) -> p t", p=128)),
                         (ntype_i[0:LAST, NT - 1:NT], view(a["node_type_5"][(NT - 1) * 128:N], "(p o) -> p o", o=1))]

        @block.sync
        def _(sp):
            sp.dma_start(view(edge_i[0:EP, :], "p c -> p c"), view(a["dst"], "(p c) -> p c", p=EP)).then_inc(ends_loaded[0], 16)
            sp.dma_start(X[:, 0:NT - 1, :], view(a["x"][0:(NT - 1) * 128, :], "(t p) d -> p t d", p=128)).then_inc(x_loaded, 16)
            with nc.allow_non_contiguous_dma(reason="a few short parameter columns"):
                for tile, source in weight_loads:
                    sp.dma_start(tile, source).then_inc(weights_loaded, 16)
            sp.wait_ge(iotas_ready, 1)
            sp.dma_start(X[0:LAST, NT - 1, :], a["x"][(NT - 1) * 128:N, :]).then_inc(x_loaded, 16)
            sp.dma_start(view(rowinfo_d[0:ROWS, :], "(p i) c -> p (i c)", p=128), zeros[:, :]).then_inc(rowinfo_zeroed, 16)
            with nc.allow_non_contiguous_dma(reason="a column a tile"):
                for tile, source in type_loads:
                    sp.dma_start(tile, source).then_inc(types_loaded, 16)
            full = EL * (LANES - 1)
            with nc.allow_non_contiguous_dma(reason="one neighbour per lane"):
                for lanes, at, ends in ((src_lanes, 0, a["src"]), (dst_lanes, 1, a["dst"])):
                    sp.dma_start(lanes[0:LANES - 1, at:at + EL], view(ends[0:full], "(p c) -> p c", c=EL)).then_inc(lanes_loaded, 16)
                    sp.dma_start(lanes[LANES - 1:LANES, at:at + E - full], view(ends[full:E], "(o c) -> o c", o=1)).then_inc(lanes_loaded, 16)
                sp.dma_start(dst_lanes[1:LANES, 0:1], view(a["dst"][0:full], "(p c) -> p c", c=EL)[:, EL - 1:EL]).then_inc(lanes_loaded, 16)
                sp.dma_start(dst_lanes[0:LANES - 2, EL + 1:EL + 2], view(a["dst"][EL:full], "(p c) -> p c", c=EL)[:, 0:1]).then_inc(lanes_loaded, 16)
                sp.dma_start(dst_lanes[LANES - 2:LANES - 1, EL + 1:EL + 2], view(a["dst"][full:full + 1], "(o c) -> o c", o=1)).then_inc(lanes_loaded, 16)
            def tile_tables(S, parts):
                def write(t, b):
                    sp.wait_ge(S["result"], t + 1)
                    for table, tile in parts[b]:
                        sp.dma_start(table[bass.ds(t * 128, 128), :], tile).then_inc(S[f"written{b}"], 16)

                tiles(sp, write)
                for b in range(2):
                    sp.wait_ge(S[f"written{b}"], 32 * ((NT + 1 - b) // 2))

            def bring_carries(name):
                w = width[name]
                sp.wait_ge(LS[name]["carry_scattered"], 16)
                sp.dma_start(view(final_carry[:, 0:NT * w], "p (t w) -> p t w", w=w),
                             view(carry_d[name][0:PAD, :], "(t p) w -> p t w", p=128)).then_inc(carries_landed, 16)

            def edge_state_stores(name):
                S = LS[name]
                w = width[name]
                st = view(state_d[name][0:EDGES, :], "(p s j) w -> p s (j w)", p=128, j=J)
                at = w if name == "att2" else 0
                with sp.Fori(0, EHALF) as it:
                    for b in range(2):
                        sp.wait_ge(S[f"ready{b}"], it + 2)
                        sp.dma_start(st[:, bass.ds(it * 2 + b, 1), :], run[b][:, at:at + J * w]).then_inc(S[f"stored{b}"], 16)
                bring_carries(name)

            def state_stores(name):
                S = LS[name]
                st = view(state_d[name][0:ROWS, :], "(p i) w -> p i w", p=128)
                w = st.shape[2]
                with sp.Fori(0, TURNS) as it:
                    for b in range(BUFFERS):
                        sp.wait_ge(S["state_ready"], it * BUFFERS + b + 1)
                        sp.dma_start(st[:, bass.ds(it * BUFFERS + b, 1), :], state[b][:, 0:w]).then_inc(S[f"stored{b}"], 16)
                bring_carries(name)

            def whole_table(name, k):
                sp.wait_ge(*event("V:table " + name))
                sp.dma_start(view(y_d[k], "(t p) d -> p t d", p=128), T1[:, :, :]).then_inc(LS[name]["table"], 16)

            tile_tables(TS["proj"], [((q_d, proj[b][:, 0:D]), (kv_d, proj[b][:, D:])) for b in range(2)])
            sp.wait_ge(rowinfo_scattered, 16 * NT)
            sp.dma_start(view(rowinfo[:, :, :], "p i c -> p (i c)"), view(rowinfo_d[0:ROWS, :], "(p i) c -> p (i c)", p=128)).then_inc(rowinfo_loaded, 16)
            sp.wait_ge(*event("V:first ends"))
            sp.dma_start(edge_i[0:EP, :], view(a["src"], "(p c) -> p c", p=EP)).then_inc(ends_loaded[1], 16)
            sp.wait_ge(*event("V:consts"))
            for n, w in width.items():
                nothing = {W0: neutral[0], W2_: neutral[1], D: zeros}[w]
                sp.dma_start(state_d[n][stored_rows[n]:, :], zeros[0:1, 0:w]).then_inc(neutral_written, 16)
                sp.dma_start(view(carry_d[n], "(k p) w -> p k w", p=128),
                             nothing[:, 0:w].unsqueeze(1).to_broadcast([128, NT + 1, w])).then_inc(neutral_written, 16)
            pieces = next(r for r in range(1, EL) if EL % r == 0 and EL * H2 // r <= 4 * STEPS)
            sp.dma_start(view(hre_d[0:EDGES, :], "(p r c) w -> p r (c w)", p=128, r=pieces),
                         zeros[:, 0:EL * H2 // pieces].unsqueeze(1).to_broadcast([128, pieces, EL * H2 // pieces])).then_inc(neutral_written, 16)
            state_stores("att0")
            whole_table("sum1", 0)
            edge_state_stores("sum1")
            tile_tables(TS["typed"], [((h_d, hx2[b][:, 0:D + H2]), (hr_d, hx2[b][:, D + H2:])) for b in range(2)])
            for b in range(2):
                sp.wait_ge(hr_scattered[b], 16 * ((NT + 1 - b) // 2))
            sp.dma_start(score_ends, view(hre_d[0:EDGES, :], "(p e) h -> p e h", p=128)).then_inc(score_ends_loaded, 16)
            edge_state_stores("att2")
            whole_table("sum3", 1)
            edge_state_stores("sum3")
            sp.wait_ge(*event("V:x3"))
            sp.dma_start(view(out[0:(NT - 1) * 128, :], "(t p) d -> p t d", p=128), X[:, 0:NT - 1, :]).then_inc(stored_out, 16)
            sp.dma_start(out[(NT - 1) * 128:N, :], X[0:LAST, NT - 1, :]).then_inc(stored_out, 16)
            sp.wait_ge(stored_out, 32)

        @block.gpsimd
        def _(pool):
            nc.gpsimd.memset(X[:, NT - 1, :], 0.0)
            nc.gpsimd.memset(ntype_i[:, NT - 1:NT], 0)
            nc.gpsimd.memset(zeros[:, :], 0.0)
            nc.gpsimd.iota(node_along, pattern=[[1, PAD]], base=0, channel_multiplier=0)
            nc.gpsimd.iota(iota_i[:, :], pattern=[[1, 128]], base=0, channel_multiplier=0)
            nc.gpsimd.iota(view(iota_hi_i[:, :], "p (a b) -> p a b", a=2), pattern=[[1, 2], [2, NT]], base=0, channel_multiplier=0)
            nc.gpsimd.iota(node_i[:, :], pattern=[[128, NT]], base=0, channel_multiplier=1)
            nc.gpsimd.iota(row_i[:, :], pattern=[[1, STEPS]], base=0, channel_multiplier=STEPS)
            nc.gpsimd.iota(src_lanes[:, :], pattern=[[0, (ESTEPS + 2) * J]], base=N, channel_multiplier=0)
            nc.gpsimd.iota(dst_lanes[:, :], pattern=[[0, EL + 2]], base=N, channel_multiplier=0)
            nc.gpsimd.iota(part_id_i[:, :], pattern=[[0, 1]], base=0, channel_multiplier=1).then_inc(iotas_ready, 1)

            pool.wait_ge(*event("V:lines"))
            for t in range(NT):
                if t >= BUFS:
                    pool.wait_ge(line_counted, t - BUFS + 1)
                nc.gpsimd.indirect_dma_start(out=lines[t % BUFS], out_offset=None, in_=view(a["dst"], "(p c) -> p c", p=EP),
                                             in_offset=bass.IndirectOffsetOnAxis(ap=line_i[:, t:t + 1], axis=0)).then_inc(line_landed[t % BUFS], 16)
            pool.wait_ge(rowinfo_zeroed, 16)
            pool.wait_ge(*event("V:info"))
            for t in range(NT):
                nc.gpsimd.indirect_dma_start(out=rowinfo_d, out_offset=bass.IndirectOffsetOnAxis(ap=row0_i[:, t:t + 1], axis=0),
                                             in_=info[:, t, :], in_offset=None).then_inc(rowinfo_scattered, 16)
            pool.wait_ge(shifted_ready, 32 * RUN)
            pool.wait_ge(*event("V:table rows"))
            for k in range(GROUPS):
                nc.gpsimd.indirect_dma_start(out=fetched[:, k, :], out_offset=None, in_=shifted,
                                             in_offset=bass.IndirectOffsetOnAxis(ap=fetch_row_i[:, k:k + 1], axis=0)).then_inc(fetch_landed[k // CHUNK], 16)

            def tables_written(S):
                for b in range(2):
                    pool.wait_ge(S[f"written{b}"], 32 * ((NT + 1 - b) // 2))

            def steps(name, table, side, table_written):
                S = LS[name]
                w = table.shape[1]
                with pool.Fori(1, TURNS + 1) as use:
                    for b in range(BUFFERS):
                        pool.wait_ge(*table_written)
                        pool.wait_ge(S[f"index{b}"], use)
                        pool.wait_ge(S[f"free{b}"], use)
                        if side is not None:
                            nc.gpsimd.indirect_dma_start(out=dst_row[b][:, 0:side.shape[1]], out_offset=None, in_=side,
                                                         in_offset=bass.IndirectOffsetOnAxis(ap=index_cols[b][:, SLOTS:SLOTS + 1], axis=0)).then_inc(S[f"landed{b}"], 16)
                        for j in range(SLOTS):
                            nc.gpsimd.indirect_dma_start(out=gathered[b][:, j * w:(j + 1) * w], out_offset=None, in_=table,
                                                         in_offset=bass.IndirectOffsetOnAxis(ap=index_cols[b][:, j:j + 1], axis=0)).then_inc(S[f"landed{b}"], 16)
                finish(name, TURNS, BUFFERS, last_i, carry_to_i)

            def edge_steps(name, table, table_written, used):
                S = LS[name]
                w = table.shape[1]
                with pool.Fori(1, EHALF + 1) as use:
                    for b in range(2):
                        pool.wait_ge(*table_written)
                        pool.wait_ge(S[f"index{b}"], use)
                        pool.wait_ge(S[f"{used}{b}"], use)
                        for j in range(J):
                            nc.gpsimd.indirect_dma_start(out=gathered[b][:, j * w:(j + 1) * w], out_offset=None, in_=table,
                                                         in_offset=bass.IndirectOffsetOnAxis(ap=index_cols[b][:, j:j + 1], axis=0)).then_inc(S[f"landed{b}"], 16)
                finish(name, EHALF, 2, last_edge_i, carry_to_edge_i)

            def finish(name, turns, buffers, last_i, carry_to_i):
                S = LS[name]
                w = state_d[name].shape[1]
                pool.wait_ge(neutral_written, 16 * (2 * len(width) + 1))
                for b in range(buffers):
                    pool.wait_ge(S[f"stored{b}"], 16 * turns)
                pool.wait_ge(*event("V:steps " + name))
                for t in range(NT):
                    nc.gpsimd.indirect_dma_start(out=final_state[:, t * w:(t + 1) * w], out_offset=None, in_=state_d[name],
                                                 in_offset=bass.IndirectOffsetOnAxis(ap=last_i[:, t:t + 1], axis=0)).then_inc(S[f"final_landed{int(t in halves[1])}"], 16)
                    if t == (NT // 3 if name in attentions else 0):
                        pool.wait_ge(*event("V:carry " + name))
                        nc.gpsimd.indirect_dma_start(out=carry_d[name], out_offset=bass.IndirectOffsetOnAxis(ap=carry_to_i[:, 0:1], axis=0),
                                                     in_=carry_row[:, 0:w], in_offset=None).then_inc(S["carry_scattered"], 16)

            tables_written(TS["proj"])
            steps("att0", kv_d, q_d, (TS["proj"]["written0"], 32 * ((NT + 1) // 2)))
            edge_steps("sum1", y_d[0], (LS["sum1"]["table"], 16), "ready")
            pool.wait_ge(neutral_written, 16 * (2 * len(width) + 1))
            for t in range(NT):
                pool.wait_ge(TS["typed"]["result"], t + 1)
                nc.gpsimd.indirect_dma_start(out=hre_d, out_offset=bass.IndirectOffsetOnAxis(ap=first_edge_i[:, t:t + 1], axis=0),
                                             in_=hx2[t % 2][:, D + H2:], in_offset=None).then_inc(hr_scattered[t % 2], 16)
            tables_written(TS["typed"])
            nc.gpsimd.indirect_dma_start(out=hr_enter[:, :], out_offset=None, in_=hr_d,
                                         in_offset=bass.IndirectOffsetOnAxis(ap=dst_lanes[:, 1:2], axis=0)).then_inc(hr_entered, 16)
            edge_steps("att2", h_d, (TS["typed"]["written0"], 32 * ((NT + 1) // 2)), "free")
            edge_steps("sum3", y_d[1], (LS["sum3"]["table"], 16), "ready")

        @block.scalar
        def _(act):
            def done(ins, name):
                ins.then_inc(event("A:" + name)[0], 1)

            def turned_tiles(S, source, use):
                def stage(t, b):
                    nc.scalar.copy(xs[b][:, :], source[:, bass.ds(t, 1), :]).then_inc(S["staged"], 1)

                def one(t, b):
                    if not (isinstance(t, int) and t == NT - 1):
                        stage(t + 1, 1 - b)
                    act.wait_ge(S["turned"], t + 1)
                    wait(act, S["first"], t - 1)
                    nc.scalar.copy(xT[b][:, :], turned_in[b][:, 0:128]).then_inc(S["xT"], 1)
                    if not (isinstance(t, int) and t == 0):
                        use(t - 1, 1 - b)

                stage(0, 0)
                tiles(act, one)
                use(NT - 1, (NT - 1) % 2)

            def sqrt_var(name):
                act.wait_ge(*event("V:var " + name))
                done(nc.scalar.activation(sd[:, :], var[:, :], ACT.Sqrt, bias=eps_c[:, 0:1]), "sd " + name)

            def steps(name, H, scale):
                S = LS[name]
                per = 16 * (SLOTS + (1 if H else 0))
                for b in range(BUFFERS):
                    nc.scalar.copy(index_cols[b][:, 0:SLOTS + 1], IX[:, b, :]).then_inc(S[f"index{b}"], 1)
                act.wait_ge(*event("V:IX2"))

                def pair(it):
                    for b in range(BUFFERS):
                        act.wait_ge(S[f"landed{b}"], (it + 1) * per)
                        nc.scalar.copy(index_cols[b][:, 0:SLOTS + 1], IX[:, bass.ds(it * BUFFERS + (b + BUFFERS), 1), :]).then_inc(S[f"index{b}"], 1)
                        if H:
                            act.wait_ge(S["diffs"], it * BUFFERS + b + 1)
                            nc.scalar.activation(expd[:, 0:(SLOTS + 1) * H], diff[:, 0:(SLOTS + 1) * H], ACT.Exp, scale=scale).then_inc(S["exps"], 1)

                loop(act, TURNS, pair)
                exps_of_carries(name, H, scale)

            def edge_steps(name, H):
                S = LS[name]
                for b in range(2):
                    nc.scalar.copy(index_cols[b][:, 0:J], src_lanes[:, b * J:(b + 1) * J]).then_inc(S[f"index{b}"], 1)

                def pair(it):
                    for b in range(2):
                        act.wait_ge(S[f"landed{b}"], (it + 1) * (16 * J))
                        nc.scalar.copy(index_cols[b][:, 0:J], src_lanes[:, bass.ds(it * (2 * J) + (b + 2) * J, J)]).then_inc(S[f"index{b}"], 1)
                        if H:
                            act.wait_ge(S["diffs"], it * 2 + b + 1)
                            nc.scalar.activation(expd[:, 0:2 * J * H], diff[:, 0:2 * J * H], ACT.Exp).then_inc(S["exps"], 1)

                loop(act, EHALF, pair)
                exps_of_carries(name, H, 1.0)

            def exps_of_carries(name, H, scale):
                if H:
                    act.wait_ge(*event("V:md " + name))
                    done(nc.scalar.activation(me[:, 0:2 * H], md[:, 0:2 * H], ACT.Exp, scale=scale), "me " + name)
                    if name == "att0":
                        for k in (0, 1):
                            act.wait_ge(*event(f"V:deg{k}"))
                            done(nc.scalar.activation(sd[:, :], var[:, :], ACT.Sqrt), f"sqrt deg{k}")
                    for half, part in enumerate(halves):
                        act.wait_ge(*event(f"V:fd {name} {half}"))
                        for k in range(2):
                            at = slice((k * NT + part[0]) * H, (k * NT + part[-1] + 1) * H)
                            last = nc.scalar.activation(fe[:, at], fd[:, at], ACT.Exp, scale=scale)
                        done(last, f"fe {name} {half}")

            act.wait_ge(x_loaded, 32)

            def project(t, b):
                S = TS["proj"]
                act.wait_ge(S["first"], t + 1)
                wait(act, S[f"written{b}"], (t - b) * 16)
                nc.scalar.copy(proj[b][:, 0:2 * D], product_in[b][0][:, 0:2 * D])
                nc.scalar.copy(view(proj[b][:, 2 * D:], "p (d h) -> p h d", h=H0),
                               view(product_in[b][0][:, 2 * D:3 * D], "p (h d) -> p h d", h=H0)).then_inc(S["result"], 1)

            turned_tiles(TS["proj"], X, project)
            act.wait_ge(line_counted, NT)
            flat = view(shifted, "a b -> (a b)")
            for s in range(RUN):
                at = s * RBW + RUN - s
                nc.scalar.dma_start(view(flat[at:at + E], "(p c) -> p c", p=EP), view(a["src"], "(p c) -> p c", p=EP)).then_inc(shifted_ready, 16)
                tail = flat[at + E:(s + 1) * RBW]
                nc.scalar.dma_start(view(tail, "(o c) -> o c", o=1), zeros[0:1, 0:tail.shape[0]].bitcast(I32)).then_inc(shifted_ready, 16)
            act.wait_ge(lanes_loaded, 16 * 7)
            act.wait_ge(*event("V:IX0"))
            steps("att0", H0, float(1.0 / (D ** 0.5)))
            sqrt_var("ln1")
            act.wait_ge(*event("V:ln1"))

            def with_bias(t, b):
                S = TS["ffn"]
                act.wait_ge(S["first"], t + 1)
                wait(act, S["hidden"], t)
                for c in range(FC):
                    last = nc.scalar.activation(hb[:, c, :], product_in[b][0][:, c * 128:(c + 1) * 128], ACT.Identity, bias=b1[:, c:c + 1])
                last.then_inc(S["read"], 1)

            turned_tiles(TS["ffn"], R, with_bias)
            sqrt_var("ln2")
            sqrt_var("x0")
            edge_steps("sum1", 0)
            sqrt_var("x1")
            act.wait_ge(*event("V:x1"))

            def residual(t, b):
                act.wait_ge(TS["typed"]["first"], t + 1)
                nc.scalar.copy(R[:, bass.ds(t, 1), :], product_in[b][2][:, 0:D]).then_inc(TS["typed"]["second"], 1)

            turned_tiles(TS["typed"], X, residual)
            edge_steps("att2", H2)
            sqrt_var("x2")
            edge_steps("sum3", 0)
            act.wait_ge(*event("V:agg3"))

            def relu(t, b):
                S = TS["gcn"]
                act.wait_ge(S["first"], t + 1)
                wait(act, S["second"], t - 1)
                nc.scalar.activation(hT[:, b * 128:(b + 1) * 128], product_in[b][0][:, 0:128], ACT.Relu, bias=b3[:, 0:1]).then_inc(S["hidden"], 1)

            turned_tiles(TS["gcn"], R, relu)
            sqrt_var("x3")

        @block.tensor
        def _(pe):
            def done(ins, name):
                ins.then_inc(event("P:" + name)[0], 1)

            def open_counts():
                for u in range(2):
                    nc.tensor.matmul(ps[4][LO * u:LO * (u + 1), 0:NT], zero_b[:, 0:LO], zero_b[:, 0:NT], start=True, stop=False).then_inc(onehots_used[u], 1)

            def batch(n):
                for b in range(2):
                    pe.wait_ge(onehots_ready[b], n + 1)
                    for c in range(HA[b]):
                        for u in range(2):
                            mm = nc.tensor.matmul(ps[4][LO * u:LO * (u + 1), 0:NT], oh_lo[b][0:EP, c, :],
                                                  oh_hi[b][0:EP, c, u * NT:(u + 1) * NT], start=False, stop=False)
                    mm.then_inc(onehots_used[b], 1)

            def close_counts():
                for u in range(2):
                    mm = nc.tensor.matmul(ps[4][LO * u:LO * (u + 1), 0:NT], zero_b[:, 0:LO], zero_b[:, 0:NT], start=False, stop=True)
                done(mm, "hist")

            def turned_tiles(S, product):
                def flip(t, b):
                    pe.wait_ge(S["staged"], t + 1)
                    wait(pe, S["xT"], t - 1)
                    nc.tensor.transpose(turned_in[b][:, 0:128], xs[b][:, :], ident[:, :]).then_inc(S["turned"], 1)

                def one(t, b):
                    if not (isinstance(t, int) and t == NT - 1):
                        flip(t + 1, 1 - b)
                    pe.wait_ge(S["xT"], t + 1)
                    product(t, b)

                flip(0, 0)
                tiles(pe, one)

            pe.wait_ge(*event("V:past first"))
            for t in range(NT):
                mm = nc.tensor.matmul(ps[3][:, t:t + 1], past_first[0:EP, t * 128:(t + 1) * 128], ones_b[0:EP, :], start=True, stop=True)
            done(mm, "lines")
            pe.wait_ge(*event("V:consts"))

            pe.wait_ge(weights_loaded, 16 * len(weight_loads))

            def project(t, b):
                S = TS["proj"]
                wait(pe, S["result"], t - 1)
                nc.tensor.matmul(product_in[b][0][:, 0:3 * D], xT[b][:, :], Wqkv[:, :], start=True, stop=True).then_inc(S["first"], 1)

            turned_tiles(TS["proj"], project)
            pe.wait_ge(TS["proj"]["result"], NT)
            pe.wait_ge(*event("V:edge starts"))
            nc.tensor.matmul(ps[3][:, 0:NT], following[:, :], edge_starts[:, 0:NT], start=True, stop=False)
            done(nc.tensor.matmul(ps[3][:, 0:NT], corner[:, :], edge_starts[:, 1:NT + 1], start=False, stop=True), "edge ends")
            pe.wait_ge(*event("V:deg rows"))
            nc.tensor.matmul(ps[0][:, 0:2 * NT], before[:, :], deg_rows[:, :], start=True, stop=True)
            done(nc.tensor.matmul(ps[1][:, 0:2 * NT], ones[:, :], deg_rows[:, :], start=True, stop=True), "sums")
            pe.wait_ge(*event("V:al sums"))
            for g in range(2):
                for c, rows in al_pieces:
                    at = g * NTYPE * 32 + c * 128
                    mm = nc.tensor.matmul(ps[5][:, at:at + rows], hb[0:rows, 2 * c + g, :], ident[0:rows, 0:rows], start=True, stop=True)
            done(nc.tensor.transpose(ps[6][:, 0:128], lin_in[:, :], ident[:, :]), "al rows")
            pe.wait_ge(*event("V:cont edges"))
            nc.tensor.transpose(ps[0][0:H0, 0:128], penalty[:, :], ident[:, :])
            done(nc.tensor.transpose(ps[1][:, 0:128], wide[:, :], ident[:, :]), "cont edges")
            pe.wait_ge(*event("V:contT edges"))
            pe.wait_ge(*event("V:lane top"))
            done(nc.tensor.transpose(ps[0][0:4, 0:128], carry4[:, :], ident[:, :]), "lane top")
            pe.wait_ge(*event("V:lane excl"))
            done(nc.tensor.transpose(ps[0][:, 0:4], lane_excl[:, :], ident[0:4, 0:4]), "lane excl")
            pe.wait_ge(*event("V:cont"))
            nc.tensor.transpose(ps[0][0:H0, 0:128], penalty[:, :], ident[:, :])
            done(nc.tensor.transpose(ps[1][:, 0:128], wide[:, :], ident[:, :]), "cont")
            pe.wait_ge(*event("V:contT"))

            open_counts()

            loop(pe, NB, batch)
            close_counts()

            def carries(name, H):
                F = D + H
                if H:
                    pe.wait_ge(*event("V:steps " + name))
                    done(nc.tensor.transpose(ps[0][0:H, 0:128], lane_end[name][:, F:F + H], ident[:, :]), "m " + name)
                    pe.wait_ge(*event("V:MprevT " + name))
                    nc.tensor.transpose(ps[0][:, 0:H], MT[0:H, :], ident[0:H, 0:H])
                    done(nc.tensor.transpose(ps[0][:, H:2 * H], MprevT[0:H, :], ident[0:H, 0:H]), "MM " + name)
                if H:
                    pe.wait_ge(*event("V:EG " + name))
                    nc.tensor.transpose(ps[1][:, 0:128], Es[:, 0:D], ident[:, :])
                    nc.tensor.transpose(ps[1][0:H, 128:256], Es[:, D:F], ident[:, :])
                    nc.tensor.transpose(ps[2][:, 0:128], Gs[:, 0:D], ident[:, :])
                    done(nc.tensor.transpose(ps[2][0:H, 128:256], Gs[:, D:F], ident[:, :]), "EG " + name)
                else:
                    pe.wait_ge(*event("V:steps " + name))
                    done(nc.tensor.transpose(ps[1][:, 0:128], lane_end[name][:, 0:D], ident[:, :]), "EG " + name)
                pe.wait_ge(*event("V:CTx " + name))
                mm = nc.tensor.transpose(ps[0][:, 0:D], CTx[:, 0:128], ident[:, :])
                if H:
                    mm = nc.tensor.transpose(ps[0][:, D:F], CTx[0:H, 128:256], ident[0:H, 0:H])
                done(mm, "C " + name)

            carries("att0", H0)
            S = TS["ffn"]

            def ffn_first(t, b):
                wait(pe, S["read"], t - 1)
                for c in range(FC):
                    mm = nc.tensor.matmul(product_in[b][0][:, c * 128:(c + 1) * 128], W1[:, c * 128:(c + 1) * 128], xT[b][:, :], start=True, stop=True)
                mm.then_inc(S["first"], 1)
                if not (isinstance(t, int) and t == 0):
                    ffn_second(t - 1, 1 - b)

            def ffn_second(t, b):
                pe.wait_ge(S["hidden"], t + 1)
                wait(pe, S["result"], t - 1)
                for c in range(FC):
                    mm = nc.tensor.matmul(product_in[b][1][:, 0:D], hidden[b][:, c * 128:(c + 1) * 128], W2[:, c, :], start=(c == 0), stop=(c == FC - 1))
                mm.then_inc(S["second"], 1)

            turned_tiles(S, ffn_first)
            ffn_second(NT - 1, (NT - 1) % 2)
            carries("sum1", 0)
            S = TS["typed"]
            pe.wait_ge(*event("V:Wcat"))

            def typed(t, b):
                S = TS["typed"]
                first_types, last_types, residual = product_in[b]
                wait(pe, S["result"], t - 1)
                wait(pe, S["second"], t - 1)
                nc.tensor.matmul(first_types[:, 0:3 * HXW], xT[b][:, :], Wcat[:, 0:3 * HXW], start=True, stop=True)
                nc.tensor.matmul(last_types[:, 0:2 * HXW], xT[b][:, :], Wcat[:, 3 * HXW:5 * HXW], start=True, stop=True)
                nc.tensor.matmul(residual[:, 0:D], xT[b][:, :], Wcat[:, 5 * HXW:], start=True, stop=True).then_inc(S["first"], 1)

            turned_tiles(TS["typed"], typed)
            carries("att2", H2)
            carries("sum3", 0)

            def gcn(t, b):
                S = TS["gcn"]
                wait(pe, S["hidden"], t - 1)
                nc.tensor.matmul(product_in[b][0][:, 0:128], W3[:, :], xT[b][:, :], start=True, stop=True).then_inc(S["first"], 1)
                if not (isinstance(t, int) and t == 0):
                    gcn_second(t - 1, 1 - b)

            def gcn_second(t, b):
                S = TS["gcn"]
                pe.wait_ge(S["hidden"], t + 1)
                wait(pe, S["result"], t - 1)
                nc.tensor.matmul(product_in[b][1][:, 0:D], hT[:, b * 128:(b + 1) * 128], linT[:, :], start=True, stop=True).then_inc(S["second"], 1)

            turned_tiles(TS["gcn"], gcn)
            gcn_second(NT - 1, (NT - 1) % 2)

        @block.vector
        def _(dve):
            v = nc.vector
            n_done = [0]

            def done(ins, name=None):
                if name:
                    ins.then_inc(event("V:" + name)[0], 1)
                    dve.wait_ge(*event("V:" + name))
                else:
                    n_done[0] += 1
                    ins.then_inc(dve_done, 1)
                    dve.wait_ge(dve_done, n_done[0])

            def after_pe(name):
                dve.wait_ge(*event("P:" + name))

            def after_act(name):
                dve.wait_ge(*event("A:" + name))

            dve.wait_ge(iotas_ready, 1)
            done(v.tensor_copy(iota_f[:, :], iota_i[:, :]))
            v.tensor_copy(iota_lo_b[:, :], iota_i[:, 0:LO])
            v.tensor_copy(iota_hi_b[:, :], iota_hi_i[:, :])
            v.tensor_copy(row_f[:, :], row_i[:, :])
            done(v.tensor_copy(part_id[:, :], part_id_i[:, :]))
            dve.wait_ge(ends_loaded[0], 16)
            v.memset(ones_b[:, :], 1.0)
            done(v.tensor_copy(first_f[0:EP, :], edge_i[0:EP, 0:1]), "first ends")
            done(v.tensor_scalar(past_first[0:EP, :], node_along[0:EP, :], first_f[0:EP, 0:1], None, ALU.is_gt), "past first")
            after_pe("lines")
            done(v.tensor_copy(line_f[:, :], ps[3][:, 0:NT]))
            done(v.tensor_scalar(line_f[:, :], line_f[:, :], 1.0, 0.0, ALU.subtract, ALU.max))
            done(v.tensor_copy(line_i[:, :], line_f[:, :]), "lines")
            v.tensor_copy(node_f[:, :], node_i[:, :])
            v.tensor_scalar(following[:, :], iota_f[:, :], 1.0, None, ALU.add)
            v.tensor_scalar(corner[:, :], iota_f[:, :], 127.0, None, ALU.is_equal)
            done(v.tensor_scalar(is_first[:, :], part_id[:, :], 0.0, None, ALU.is_equal))
            done(v.tensor_scalar(following[:, :], following[:, :], part_id[:, 0:1], None, ALU.is_equal))
            done(v.tensor_scalar(corner[:, :], corner[:, :], is_first[:, 0:1], None, ALU.mult))
            v.tensor_scalar(ident[:, :], iota_f[:, :], part_id[:, 0:1], None, ALU.is_equal)
            v.tensor_scalar(before[:, :], iota_f[:, :], part_id[:, 0:1], None, ALU.is_gt)
            v.tensor_scalar(row_ok[:, :], part_id[:, :], float(LAST), None, ALU.is_lt)
            v.memset(ones[:, :], 1.0)
            v.memset(eps_c[:, :], EPS)
            v.memset(IX[:, STEPS:STEPS + BUFFERS, :], 0.0)
            for tile, H in zip(neutral, (H0, H2)):
                v.memset(tile[:, 0:D + H], 0.0)
                v.memset(tile[:, D + H:], -BIG)
            done(v.memset(zero_b[:, :], 0.0), "consts")

            for t in range(NT):
                dve.wait_ge(line_landed[t % BUFS], 16 * (t // BUFS + 1))
                v.tensor_scalar(smaller[:, :], lines[t % BUFS], node_f[:, t:t + 1], 0.0, ALU.is_lt, ALU.add,
                                accum_out=counts[:, t:t + 1]).then_inc(line_counted, 1)
                dve.wait_ge(line_counted, t + 1)
            v.memset(edge_starts[:, NT:], float(E))
            done(v.scalar_tensor_tensor(edge_starts[:, 0:NT], line_f[:, :], float(EC), counts[:, :], ALU.mult, ALU.add), "edge starts")
            after_pe("edge ends")
            done(v.tensor_tensor(deg_rows[:, 0:NT], ps[3][:, 0:NT], edge_starts[:, 0:NT], ALU.subtract))
            done(v.tensor_scalar(starts[:, 0:NT], deg_rows[:, 0:NT], 0.5 * (SLOTS - 1), 1.0 / SLOTS, ALU.add, ALU.mult))
            done(v.tensor_scalar(deg_rows[:, NT:], starts[:, 0:NT], ROUND, -ROUND, ALU.add, ALU.add), "deg rows")
            after_pe("sums")
            done(v.tensor_copy(tot[:, :], ps[1][:, 0:2 * NT]))
            for u in range(2):
                s = slice(u * NT, (u + 1) * NT)
                done(v.tensor_tensor_scan(incl[:, s], ones[:, 0:NT], tot[:, s], 0.0, ALU.mult, ALU.add))
            done(v.tensor_tensor(incl[:, :], incl[:, :], tot[:, :], ALU.subtract))
            done(v.tensor_tensor(starts[:, :], incl[:, :], ps[0][:, 0:2 * NT], ALU.add))
            v.tensor_copy(info[:, :, 0], node_i[:, :])
            v.tensor_copy(info[:, :, 1], starts[:, 0:NT])
            v.tensor_copy(info[:, :, 2], starts[:, NT:])
            v.tensor_tensor(info[:, :, 3], starts[:, 0:NT], deg_rows[:, 0:NT], ALU.add)
            v.tensor_copy(target_f[:, :], node_i[:, :])
            done(v.tensor_scalar(empty[:, :], deg_rows[:, NT:], 0.0, None, ALU.is_equal))
            done(v.tensor_scalar(target_f[:, :], target_f[:, :], float(ROWS), None, ALU.add))
            done(v.tensor_tensor(target_f[:, :], target_f[:, :], starts[:, NT:], ALU.subtract))
            done(v.tensor_tensor(target_f[:, :], target_f[:, :], empty[:, :], ALU.mult))
            done(v.tensor_tensor(target_f[:, :], target_f[:, :], starts[:, NT:], ALU.add))
            done(v.tensor_copy(row0_i[:, :], target_f[:, :]), "info")
            done(v.tensor_tensor(last_f[:, :], starts[:, NT:], deg_rows[:, NT:], ALU.add))
            done(v.tensor_scalar(last_f[:, :], last_f[:, :], -1.0 - ROWS, None, ALU.add))
            done(v.tensor_scalar(target_f[:, :], empty[:, :], -1.0, 1.0, ALU.mult, ALU.add))
            done(v.tensor_tensor(last_f[:, :], last_f[:, :], target_f[:, :], ALU.mult))
            done(v.tensor_scalar(last_i[:, :], last_f[:, :], float(ROWS), None, ALU.add))
            done(v.tensor_scalar(last_f[:, :], info[:, :, 3], -1.0 - EDGES, None, ALU.add))
            done(v.tensor_tensor(last_f[:, :], last_f[:, :], target_f[:, :], ALU.mult))
            done(v.tensor_scalar(last_edge_i[:, :], last_f[:, :], float(EDGES), None, ALU.add))
            done(v.tensor_scalar(last_f[:, :], info[:, :, 0], float(EDGES), None, ALU.add))
            done(v.tensor_tensor(last_f[:, :], last_f[:, :], empty[:, :], ALU.mult))
            done(v.tensor_tensor(target_f[:, :], target_f[:, :], starts[:, 0:NT], ALU.mult))
            done(v.tensor_tensor(first_edge_i[:, :], last_f[:, :], target_f[:, :], ALU.add))

            def col(k):
                return lane_cols[:, k:k + 1]

            def edge_lanes():
                dve.wait_ge(lanes_loaded, 16 * 7)
                done(v.tensor_copy(dst_lanes_f[:, :], dst_lanes[:, :]))
                before_lane, first, last_of, after_lane = (dst_lanes_f[:, c:c + 1] for c in (0, 1, EL, EL + 1))
                done(v.tensor_tensor(same_edge[:, :], dst_lanes_f[:, 1:EL + 1], dst_lanes_f[:, 0:EL], ALU.is_equal))
                done(v.tensor_copy(enters[:, :], same_edge[:, 0:1]))
                done(v.memset(same_edge[:, 0:1], 0.0))
                v.memset(penalty_edge[:, :, 0:1], -BIG)
                v.tensor_scalar(penalty_edge[:, :, 1:], view(same_edge[:, :], "p (s j) -> p s j", j=J), 1.0, BIG, ALU.subtract, ALU.mult)
                done(v.tensor_tensor(col(0), first, last_of, ALU.is_equal))
                done(v.tensor_tensor(cont_edge[:, :], col(0), enters[:, :], ALU.mult))
                done(v.tensor_scalar(cont2_edge[:, :], cont_edge[:, :], 1.0, BIG, ALU.subtract, ALU.mult))
                v.tensor_scalar(col(3), part_id[:, :], float(PAD), None, ALU.add)
                done(v.tensor_tensor(col(1), first, after_lane, ALU.not_equal))
                done(v.tensor_tensor(col(7), col(1), enters[:, :], ALU.mult))
                done(v.tensor_tensor(col(4), first, col(3), ALU.subtract))
                done(v.tensor_tensor(col(4), col(4), col(7), ALU.mult))
                done(v.tensor_tensor(carry_to_edge_i[:, :], col(4), col(3), ALU.add))
                v.tensor_copy(penalty[:, :], bc(cont2_edge[:, 0:1], [128, H0]))
                done(v.tensor_copy(wide[:, :], bc(cont_edge[:, 0:1], [128, 128])), "cont edges")
                after_pe("cont edges")
                v.tensor_copy(penaltyT_edge[:, :], ps[0][0:H0, 0:128])
                done(v.tensor_copy(contT_edge[:, :], ps[1][:, 0:128]), "contT edges")

            dve.wait_ge(weights_loaded, 16 * len(weight_loads))
            for c, rows in al_pieces:
                done(v.tensor_reduce(al_sums[0:rows, :, c], al_rows[0:rows, :, c, :], AX.X, ALU.add))
                for g in range(2):
                    last = v.tensor_scalar(hb[0:rows, 2 * c + g, :], ones[0:rows, :], al_sums[0:rows, g, c:c + 1], None, ALU.mult)
            done(last, "al sums")
            edge_lanes()
            after_pe("al rows")
            v.tensor_copy(linT[:, :], ps[6][:, 0:128])
            done(v.tensor_copy(view(alr[:, :, :, :], "p g t i -> p (g t i)"), ps[5][:, 0:2 * NTYPE * 32]))
            for t in range(NTYPE):
                v.tensor_copy(view(Wcat[:, t * HXW:t * HXW + D], "p (k h) -> p h k", h=H2), view(Wt_in[:, t, :], "p (h k) -> p h k", h=H2))
                for g in range(2):
                    done(v.tensor_tensor(view(Wprod[:, :], "p (h k) -> p h k", h=H2), view(Wt_in[:, t, :], "p (h k) -> p h k", h=H2),
                                         bc(alr[:, g, t, :].unsqueeze(1), [128, H2, 32]), ALU.mult))
                    done(v.tensor_reduce(Wcat[:, t * HXW + D + g * H2:t * HXW + D + (g + 1) * H2],
                                         view(Wprod[:, :], "p (h k) -> p h k", h=H2), AX.X, ALU.add), "Wcat" if (t, g) == (NTYPE - 1, 1) else None)
            dve.wait_ge(types_loaded, 16 * len(type_loads))
            done(v.tensor_copy(ntype_f[:, :], ntype_i[:, :]))
            for t in range(NTYPE):
                last = v.tensor_scalar(type_mask[:, :, t], ntype_f[:, :], float(t), None, ALU.is_equal)
            done(last)

            dve.wait_ge(rowinfo_loaded, 16)
            for c in range(4):
                last = v.tensor_tensor_scan(RS[:, c, :], rowinfo[:, :, c], rowinfo[:, :, c], 0.0, ALU.max, ALU.max)
            done(last)
            done(v.tensor_copy(carry4[:, :], RS[:, :, STEPS - 1]), "lane top")
            after_pe("lane top")
            done(v.tensor_copy(lane_in[:, :], ps[0][0:4, 0:128]))
            done(v.tensor_tensor_scan(lane_top[:, :], lane_in[:, :], lane_in[:, :], 0.0, ALU.max, ALU.max))
            v.memset(lane_excl[:, 0:1], 0.0)
            done(v.tensor_copy(lane_excl[:, 1:128], lane_top[:, 0:127]), "lane excl")
            after_pe("lane excl")
            done(v.tensor_copy(carry4[:, :], ps[0][:, 0:4]))
            for c in range(4):
                last = v.tensor_scalar(RS[:, c, :], RS[:, c, :], carry4[:, c:c + 1], None, ALU.max)
            done(last)
            row_node, row_start, row_first, row_end = (RS[:, c, :] for c in range(4))
            done(v.tensor_tensor(pos[:, :], row_f[:, :], row_first, ALU.subtract))
            done(v.tensor_scalar(pos[:, :], pos[:, :], float(SLOTS), None, ALU.mult))
            done(v.tensor_tensor(pos[:, :], pos[:, :], row_start, ALU.add))
            done(v.tensor_scalar(low_f[:, :], pos[:, :], float(E), None, ALU.min))
            done(v.tensor_copy(pos_i[:, :], low_f[:, :]))
            v.tensor_scalar(low_i[:, :], pos_i[:, :], RUN - 1, None, ALU.bitwise_and)
            done(v.tensor_scalar(high_i[:, :], pos_i[:, :], RUN.bit_length() - 1, None, ALU.arith_shift_right))
            v.tensor_copy(low_f[:, :], low_i[:, :])
            done(v.tensor_copy(high_f[:, :], high_i[:, :]))
            done(v.tensor_scalar(low_f[:, :], low_f[:, :], float(RB), 1.0, ALU.mult, ALU.add))
            done(v.tensor_tensor(low_f[:, :], low_f[:, :], high_f[:, :], ALU.add))
            done(v.tensor_copy(fetch_row_i[:, :], view(low_f[:, :], "p (k g) -> p k g", g=GROUP)[:, :, 0]), "table rows")
            offset = view(table_row[:, :], "p (k g) -> p k g", g=GROUP)
            by_group = view(pos[:, :], "p (k g) -> p k g", g=GROUP)
            done(v.tensor_tensor(offset, by_group, bc(by_group[:, :, 0:1], [128, GROUPS, GROUP]), ALU.subtract))
            done(v.tensor_tensor(BOUND[:, :, :], bc(pos[:, :].unsqueeze(2), [128, STEPS, SLOTS]),
                                 bc(iota_f[:, 0:SLOTS].unsqueeze(1), [128, STEPS, SLOTS]), ALU.add))
            done(v.tensor_tensor(VALID[:, :, :], BOUND[:, :, :], bc(row_end.unsqueeze(2), [128, STEPS, SLOTS]), ALU.is_lt))
            done(v.tensor_scalar(BOUND[:, :, :], VALID[:, :, :], 0.5, 2 * BIG, ALU.subtract, ALU.mult))
            v.memset(same[:, 0:1], 0.0)
            done(v.tensor_tensor(same[:, 1:], RS[:, 0, 1:STEPS], RS[:, 0, 0:STEPS - 1], ALU.is_equal))
            v.tensor_scalar(same_bound[:, :], same[:, :], 0.5, 2 * BIG, ALU.subtract, ALU.mult)
            v.tensor_tensor(cont[:, :], RS[:, 0, 0:1], RS[:, 0, STEPS - 1:STEPS], ALU.is_equal)
            done(v.tensor_tensor(cont2[:, :], RS[:, 0, 0:1], carry4[:, 0:1], ALU.is_equal))
            done(v.tensor_tensor(cont[:, :], cont[:, :], cont2[:, :], ALU.mult))
            done(v.tensor_scalar(cont2[:, :], cont[:, :], 1.0, BIG, ALU.subtract, ALU.mult))
            v.tensor_tensor(col(0), RS[:, 0, 0:1], carry4[:, 0:1], ALU.is_equal)
            v.tensor_tensor(col(1), pos[:, 0:1], RS[:, 3, 0:1], ALU.is_lt)
            v.tensor_scalar(col(3), part_id[:, :], float(PAD), None, ALU.add)
            done(v.tensor_scalar(col(2), pos[:, 0:1], float(SLOTS * STEPS), None, ALU.add))
            done(v.tensor_tensor(col(5), col(2), RS[:, 3, 0:1], ALU.is_ge))
            done(v.tensor_tensor(col(6), col(0), col(1), ALU.mult))
            done(v.tensor_tensor(col(7), col(6), col(5), ALU.mult))
            done(v.tensor_tensor(col(4), RS[:, 0, 0:1], col(3), ALU.subtract))
            done(v.tensor_tensor(col(4), col(4), col(7), ALU.mult))
            done(v.tensor_tensor(carry_to_i[:, :], col(4), col(3), ALU.add))
            v.tensor_copy(penalty[:, :], bc(cont2[:, 0:1], [128, H0]))
            done(v.tensor_copy(wide[:, :], bc(cont[:, 0:1], [128, 128])), "cont")
            after_pe("cont")
            v.tensor_copy(penaltyT[:, :], ps[0][0:H0, 0:128])
            done(v.tensor_copy(contT[:, :], ps[1][:, 0:128]), "contT")
            def batch(n, b):
                dve.wait_ge(onehots_used[b], n + 1)
                for oh, iota, part in ((oh_lo, iota_lo_b, lo_b), (oh_hi, iota_hi_b, hi_b)):
                    w = oh[b].shape[2]
                    ins = v.tensor_tensor(oh[b][0:EP, :, :], bc(iota[0:EP, :].unsqueeze(1), [EP, HA[b], w]),
                                          bc(part[0:EP, bass.ds(n * BATCH + b * HA[0], HA[b])].unsqueeze(2), [EP, HA[b], w]), ALU.is_equal)
                ins.then_inc(onehots_ready[b], 1)

            for b in range(BUFFERS):
                v.memset(state[b][:, :], 0.0).then_inc(LS["att0"][f"free{b}"], 1)
                dve.wait_ge(LS["att0"][f"free{b}"], 1)

            done(v.tensor_copy(IX[:, 0:STEPS, SLOTS], row_node))
            for c in range(CHUNKS):
                ks = slice(c * CHUNK, (c + 1) * CHUNK)
                dve.wait_ge(fetch_landed[c], 16 * CHUNK)
                done(v.tensor_scalar(fetched_f[:, ks, :], fetched[:, ks, :], -float(N), None, ALU.add))
                for g in range(GROUP):
                    found = fetched_f[:, ks, 0:SLOTS] if g == 0 else picked[:, :, :]
                    if g:
                        places = range(g, SLOTS * g + 1)
                        for n, o in enumerate(places):
                            part = view(picked_parts[:, n * CHUNK * SLOTS:(n + 1) * CHUNK * SLOTS], "p (k j) -> p k j", j=SLOTS)
                            last = v.scalar_tensor_tensor(part, bc(offset[:, ks, g:g + 1], [128, CHUNK, SLOTS]), float(o),
                                                          fetched_f[:, ks, o:o + SLOTS], ALU.is_equal, ALU.mult)
                        done(last)
                        done(v.tensor_reduce(view(picked[:, :, :], "p k j -> p (k j)"),
                                             view(picked_parts[:, 0:len(places) * CHUNK * SLOTS], "p (o e) -> p e o", o=len(places)), AX.X, ALU.add))
                    done(v.tensor_tensor(picked[:, :, :], found, view(VALID[:, :, :], "p (k g) j -> p k g j", g=GROUP)[:, ks, g, :], ALU.mult))
                    done(v.tensor_scalar(view(IX[:, 0:STEPS, :], "p (k g) j -> p k g j", g=GROUP)[:, ks, g, 0:SLOTS], picked[:, :, :], float(N), None, ALU.add), f"IX{c}" if g == GROUP - 1 else None)
            dve.wait_ge(ends_loaded[1], 16)
            v.tensor_scalar(part_i[0:EP, :], edge_i[0:EP, :], LO - 1, None, ALU.bitwise_and)
            done(v.tensor_scalar(edge_i[0:EP, :], edge_i[0:EP, :], LO.bit_length() - 1, None, ALU.arith_shift_right))
            v.tensor_copy(lo_b[0:EP, :], part_i[0:EP, :])
            done(v.tensor_copy(hi_b[0:EP, :], edge_i[0:EP, :]))

            def degree_scales():
                after_pe("hist")
                done(v.tensor_copy(outdeg[:, :], ps[4][:, 0:NT]))
                for k, deg in ((0, outdeg[:, :]), (1, deg_rows[:, 0:NT])):
                    if k:
                        after_act("sqrt deg0")
                    done(v.tensor_scalar(var[:, :], deg, 1.0, None, ALU.add), f"deg{k}")
                    after_act(f"sqrt deg{k}")
                    done(v.reciprocal(dis[k][:, :], sd[:, :]))

            def attention_steps(name, H, U):
                S = LS[name]
                F = D + H
                n_chain = [0]
                per = 7

                def turn(it):
                    n_chain[0] = 0

                    def link(ins):
                        n_chain[0] += 1
                        ins.then_inc(S["chain"], 1)
                        dve.wait_ge(S["chain"], it * (BUFFERS * per) + n_chain[0])

                    for b in range(BUFFERS):
                        new, old = state[b], state[b - 1]
                        g = view(gathered[b][:, 0:SLOTS * 2 * D], "p (j w) -> p j w", w=2 * D)
                        sc = scores[:, :, 0:H]
                        i = it * BUFFERS + b
                        dve.wait_ge(S[f"landed{b}"], (it + 1) * (16 * (SLOTS + 1)))
                        link(v.tensor_tensor(prod[:, :, :], g[:, :, 0:D], bc(dst_row[b][:, :].unsqueeze(1), [128, SLOTS, D]), ALU.mult))
                        link(v.tensor_reduce(sc, view(prod[:, :, :], "p j (h u) -> p j h u", h=H), AX.X, ALU.add))
                        value = g[:, :, D:]
                        link(v.tensor_tensor(sc, sc, bc(BOUND[:, bass.ds(i, 1), :].rearrange("p o j -> p (o j)").unsqueeze(2), [128, SLOTS, H]), ALU.min))
                        link(v.tensor_reduce(top[:, 0:H], view(sc, "p j h -> p h j"), AX.X, ALU.max))
                        wait(dve, S[f"stored{b}"], it * 16)
                        link(v.scalar_tensor_tensor(new[:, F:F + H], old[:, F:F + H], same_bound[:, bass.ds(i, 1)], top[:, 0:H], ALU.min, ALU.max))
                        v.scalar_tensor_tensor(diff[:, 0:H], old[:, F:F + H], same_bound[:, bass.ds(i, 1)], new[:, F:F + H], ALU.min, ALU.subtract)
                        v.tensor_tensor(view(diff[:, H:(SLOTS + 1) * H], "p (j h) -> p j h", h=H), sc,
                                        bc(new[:, F:F + H].unsqueeze(1), [128, SLOTS, H]), ALU.subtract).then_inc(S["diffs"], 1)
                        dve.wait_ge(S["exps"], i + 1)
                        m = view(msg[:, 0:SLOTS * F], "p (j f) -> p j f", f=F)
                        link(v.tensor_tensor(m[:, :, D:], view(expd[:, H:(SLOTS + 1) * H], "p (j h) -> p j h", h=H),
                                             bc(VALID[:, bass.ds(i, 1), :].rearrange("p o j -> p (o j)").unsqueeze(2), [128, SLOTS, H]), ALU.mult))
                        v.tensor_tensor(view(m[:, :, 0:D], "p j (u h) -> p j u h", h=H), view(value, "p j (u h) -> p j u h", h=H),
                                        bc(m[:, :, D:].unsqueeze(2), [128, SLOTS, U, H]), ALU.mult).then_inc(S[f"free{b}"], 1)
                        dve.wait_ge(S[f"free{b}"], it + 2)
                        v.tensor_reduce(slot_sum[:, 0:F], view(m, "p j f -> p f j"), AX.X, ALU.add)
                        link(v.scalar_tensor_tensor(view(scaled[:, 0:F], "p (u h) -> p u h", h=H), view(old[:, 0:F], "p (u h) -> p u h", h=H),
                                                    same[:, bass.ds(i, 1)], bc(expd[:, 0:H].unsqueeze(1), [128, U + 1, H]), ALU.mult, ALU.mult))
                        v.tensor_tensor(new[:, 0:F], scaled[:, 0:F], slot_sum[:, 0:F], ALU.add).then_inc(S["state_ready"], 1)
                        dve.wait_ge(S["state_ready"], i + 1)
                    assert n_chain[0] == BUFFERS * per

                def turns_and_batch(n):
                    for b in range(2):
                        turn(n * 2 + b)
                        batch(n, b)

                loop(dve, NB, turns_and_batch)
                for it in range(2 * NB, TURNS):
                    turn(it)

            def edge_attention_steps(name, H, U):
                S = LS[name]
                F = D + H
                w = F + H
                per = 4 + 2 * J - 1
                n_chain = [0]
                for b in range(2):
                    v.memset(run[b][:, 0:(J + 1) * w], 0.0).then_inc(S[f"ready{b}"], 1)
                    dve.wait_ge(S[f"ready{b}"], 1)
                    v.memset(weighted[:, :], 0.0).then_inc(S[f"free{b}"], 1)
                    dve.wait_ge(S[f"free{b}"], 1)
                dve.wait_ge(hr_entered, 16)
                done(v.tensor_scalar(hr_enter[:, :], hr_enter[:, :], enters[:, 0:1], None, ALU.mult))
                dve.wait_ge(score_ends_loaded, 16)
                done(v.tensor_tensor(score_ends[:, 0, :], score_ends[:, 0, :], hr_enter[:, :], ALU.add))
                for h in range(H):
                    last = v.tensor_tensor_scan(score_ends[:, :, h], same_edge[:, :], score_ends[:, :, h], 0.0, ALU.mult, ALU.add)
                done(last)

                def pair(it):
                    n_chain[0] = 0

                    def link(ins):
                        n_chain[0] += 1
                        ins.then_inc(S["chain"], 1)
                        dve.wait_ge(S["chain"], it * (2 * per) + n_chain[0])

                    for b in range(2):
                        i = it * 2 + b
                        g = view(gathered[b][:, 0:J * F], "p (j f) -> p j f", f=F)
                        states = view(run[b][:, 0:(J + 1) * w], "p (j w) -> p j w", w=w)
                        entry = run[1 - b][:, J * w:(J + 1) * w]
                        penalties = penalty_edge[:, bass.ds(i, 1), :].rearrange("p o j -> p (o j)")
                        dve.wait_ge(S[f"landed{b}"], (it + 1) * (16 * J))
                        sc = edge_scores[:, 1:, :]
                        v.tensor_copy(edge_scores[:, 0, :], entry[:, F:w])
                        link(v.tensor_tensor(sc, g[:, :, D:], score_ends[:, bass.ds(i * J, J), :], ALU.add))
                        link(v.scalar_tensor_tensor(sc, sc, NEG_SLOPE, sc, ALU.mult, ALU.max))
                        wait(dve, S[f"stored{b}"], it * 16)
                        for h in range(H):
                            last = v.tensor_tensor_scan(states[:, :, F + h], penalties, edge_scores[:, :, h], -BIG, ALU.add, ALU.max)
                        link(last)
                        link(v.tensor_tensor(last_maximum[:, :, :], states[:, 0:J, F:w], bc(penalties[:, 1:].unsqueeze(2), [128, J, H]), ALU.add))
                        d = view(diff[:, 0:2 * J * H], "p (k j h) -> p k j h", k=2, h=H)
                        v.tensor_tensor(d[:, 0], last_maximum[:, :, :], states[:, 1:, F:w], ALU.subtract)
                        v.tensor_tensor(d[:, 1], sc, states[:, 1:, F:w], ALU.subtract).then_inc(S["diffs"], 1)
                        dve.wait_ge(S["exps"], i + 1)
                        decay, e = (view(expd[:, k * J * H:(k + 1) * J * H], "p (j h) -> p j h", h=H) for k in range(2))
                        items = view(weighted[:, :], "p (j f) -> p j f", f=F)
                        v.tensor_copy(items[:, :, D:], e)
                        v.tensor_tensor(view(items[:, :, 0:D], "p j (u h) -> p j u h", h=H), view(g[:, :, 0:D], "p j (u h) -> p j u h", h=H),
                                        bc(e.unsqueeze(2), [128, J, U, H]), ALU.mult).then_inc(S[f"free{b}"], 1)
                        dve.wait_ge(S[f"free{b}"], it + 2)
                        for j in range(J):
                            so_far = entry[:, 0:F] if j == 0 else states[:, j, 0:F]
                            link(v.tensor_tensor(view(scaled[:, 0:F], "p (u h) -> p u h", h=H), view(so_far, "p (u h) -> p u h", h=H),
                                                 bc(decay[:, j, :].unsqueeze(1), [128, U + 1, H]), ALU.mult))
                            ins = v.tensor_tensor(states[:, j + 1, 0:F], scaled[:, 0:F], items[:, j, :], ALU.add)
                            if j < J - 1:
                                link(ins)
                        ins.then_inc(S[f"ready{b}"], 1)
                        dve.wait_ge(S[f"ready{b}"], it + 2)
                    assert n_chain[0] == 2 * per

                loop(dve, EHALF, pair)
                done(v.tensor_copy(state[1][:, 0:w], run[1][:, J * w:(J + 1) * w]))

            def edge_sum_steps(name):
                S = LS[name]
                for b in range(2):
                    v.memset(run[b][:, 0:J * D], 0.0).then_inc(S[f"ready{b}"], 1)
                    dve.wait_ge(S[f"ready{b}"], 1)

                def pair(it):
                    for b in range(2):
                        i = it * 2 + b
                        dve.wait_ge(S[f"landed{b}"], (it + 1) * (16 * J))
                        wait(dve, S[f"stored{b}"], it * 16)
                        so_far = run[1 - b][:, (J - 1) * D:J * D]
                        for j in range(J):
                            new = run[b][:, j * D:(j + 1) * D]
                            ins = v.scalar_tensor_tensor(new, so_far, same_edge[:, bass.ds(i * J + j, 1)], gathered[b][:, j * D:(j + 1) * D], ALU.mult, ALU.add)
                            if j < J - 1:
                                ins.then_inc(S["chain"], 1)
                                dve.wait_ge(S["chain"], i * (J - 1) + (j + 1))
                            so_far = new
                        ins.then_inc(S[f"ready{b}"], 1)
                        dve.wait_ge(S[f"ready{b}"], it + 2)

                loop(dve, EHALF, pair)
                done(v.tensor_copy(state[1][:, 0:D], run[1][:, (J - 1) * D:J * D]))

            cont_row, cont2_row = cont, cont2

            def carries(name, H, U):
                F = D + H
                end = lane_end[name]
                rows = name == "att0"
                penalties, goes_on, cont, cont2 = ((penaltyT, contT, cont_row, cont2_row) if rows else
                                                   (penaltyT_edge, contT_edge, cont_edge, cont2_edge))
                done(v.memset(CTx[:, :], 0.0), "steps " + name)
                if H:
                    after_pe("m " + name)
                    done(v.tensor_copy(mT[0:H, :], ps[0][0:H, 0:128]))
                    done(v.tensor_tensor_scan(MT[0:H, :], penalties[0:H, :], mT[0:H, :], -BIG, ALU.add, ALU.max))
                    v.memset(MprevT[0:H, 0:1], -BIG)
                    done(v.tensor_copy(MprevT[0:H, 1:128], MT[0:H, 0:127]), "MprevT " + name)
                    after_pe("MM " + name)
                    done(v.tensor_copy(MM[:, 0:2 * H], ps[0][:, 0:2 * H]))
                    v.tensor_tensor(md[:, 0:H], end[:, F:F + H], MM[:, 0:H], ALU.subtract)
                    done(v.scalar_tensor_tensor(md[:, H:2 * H], MM[:, H:2 * H], cont2[:, 0:1], MM[:, 0:H], ALU.add, ALU.subtract), "md " + name)
                    after_act("me " + name)
                    done(v.tensor_scalar(me[:, H:2 * H], me[:, H:2 * H], cont[:, 0:1], None, ALU.mult))
                    v.tensor_tensor(view(Es[:, 0:F], "p (u h) -> p u h", h=H), view(end[:, 0:F], "p (u h) -> p u h", h=H),
                                    bc(me[:, 0:H].unsqueeze(1), [128, U + 1, H]), ALU.mult)
                    done(v.tensor_copy(view(Gs[:, 0:F], "p (u h) -> p u h", h=H), bc(me[:, H:2 * H].unsqueeze(1), [128, U + 1, H])), "EG " + name)
                after_pe("EG " + name)
                done(v.tensor_copy(EsT[:, 0:128], ps[1][:, 0:128]))
                if H:
                    v.tensor_copy(EsT[0:H, 128:256], ps[1][0:H, 128:256])
                    v.tensor_copy(GsT[:, 0:128], ps[2][:, 0:128])
                    done(v.tensor_copy(GsT[0:H, 128:256], ps[2][0:H, 128:256]))
                    v.tensor_tensor_scan(CT[:, 0:128], GsT[:, 0:128], EsT[:, 0:128], 0.0, ALU.mult, ALU.add)
                    done(v.tensor_tensor_scan(CT[0:H, 128:256], GsT[0:H, 128:256], EsT[0:H, 128:256], 0.0, ALU.mult, ALU.add))
                    v.tensor_copy(CTx[0:H, 129:256], CT[0:H, 128:255])
                else:
                    done(v.tensor_tensor_scan(CT[:, 0:128], goes_on[:, :], EsT[:, 0:128], 0.0, ALU.mult, ALU.add))
                done(v.tensor_copy(CTx[:, 1:128], CT[:, 0:127]), "CTx " + name)
                after_pe("C " + name)
                if H:
                    v.tensor_copy(carry_row[:, F:F + H], MM[:, H:2 * H])
                done(v.tensor_copy(carry_row[:, 0:F], ps[0][:, 0:F]), "carry " + name)

            def merge_softmax(name, H, U, target, finish):
                F = D + H
                w = F + H
                fs = view(final_state[:, 0:NT * w], "p (t w) -> p t w", w=w)
                fc = view(final_carry[:, 0:NT * w], "p (t w) -> p t w", w=w)
                d4 = view(fd[:, 0:2 * NT * H], "p (g t h) -> p g t h", g=2, h=H)
                e4 = view(fe[:, 0:2 * NT * H], "p (g t h) -> p g t h", g=2, h=H)
                dve.wait_ge(carries_landed, 16 * (layers.index(name) + 1))
                for half, part in enumerate(halves):
                    n = len(part)
                    ts = slice(part[0], part[-1] + 1)
                    m, mf, mc = fm[:, ts, 0:H], fs[:, ts, F:], fc[:, ts, F:]
                    d, e = d4[:, :, ts, :], e4[:, :, ts, :]
                    dve.wait_ge(LS[name][f"final_landed{half}"], 16 * n)
                    done(v.tensor_tensor(m, mf, mc, ALU.max))
                    v.tensor_tensor(d[:, 0], mf, m, ALU.subtract)
                    done(v.tensor_tensor(d[:, 1], mc, m, ALU.subtract), f"fd {name} {half}")
                    after_act(f"fe {name} {half}")
                    for side, f in ((fs, 0), (fc, 1)):
                        p4 = view(side[:, ts, 0:F], "p t (u h) -> p t u h", h=H)
                        last = v.tensor_tensor(p4, p4, bc(e[:, f].unsqueeze(2), [128, n, U + 1, H]), ALU.mult)
                    done(last)
                    done(v.tensor_tensor(fs[:, ts, 0:F], fs[:, ts, 0:F], fc[:, ts, 0:F], ALU.add))
                    done(v.tensor_scalar(den[:, ts, 0:H], fs[:, ts, D:F], 1e-30, None, ALU.max))
                    done(v.reciprocal(den[:, ts, 0:H], den[:, ts, 0:H]))
                    done(v.tensor_tensor(target[:, ts], view(fs[:, ts, 0:D], "p t (u h) -> p t u h", h=H),
                                         bc(den[:, ts, 0:H].unsqueeze(2), [128, n, U, H]), ALU.mult))
                    finish(ts)

            every = slice(0, NT)

            def over_nodes(col):
                return bc(col[:, :].unsqueeze(2), [128, NT, D])

            def over_tiles(row):
                return bc(row[:, :].unsqueeze(1), [128, NT, D])

            def count(Y, ts):
                for t in range(ts.start, ts.stop):
                    last = v.bn_stats(stats[:, t, :], Y[:, t, :])
                done(last)

            def layernorm(Y, name, g=None, b=None, masked=False):
                v.tensor_tensor(mean[:, :], stats[:, :, 1], stats[:, :, 4], ALU.add)
                v.tensor_tensor(apart[:, :], stats[:, :, 1], stats[:, :, 4], ALU.subtract)
                done(v.tensor_tensor(var[:, :], stats[:, :, 2], stats[:, :, 5], ALU.add))
                v.tensor_scalar(mean[:, :], mean[:, :], 0.5, None, ALU.mult)
                v.tensor_scalar(var[:, :], var[:, :], 1.0 / D, None, ALU.mult)
                done(v.scalar_tensor_tensor(apart[:, :], apart[:, :], 0.25, apart[:, :], ALU.mult, ALU.mult))
                done(v.tensor_tensor(var[:, :], var[:, :], apart[:, :], ALU.add), "var " + name)
                after_act("sd " + name)
                done(v.reciprocal(rstd[:, :], sd[:, :]))
                for t in range(NT):
                    last = v.tensor_scalar(Y[:, t, :], Y[:, t, :], mean[:, t:t + 1], rstd[:, t:t + 1], ALU.subtract, ALU.mult)
                done(last, None if g is not None or masked else name)
                if g is not None:
                    done(v.tensor_tensor(Y[:, :, :], Y[:, :, :], over_tiles(g), ALU.mult))
                    done(v.tensor_tensor(Y[:, :, :], Y[:, :, :], over_tiles(b), ALU.add), name)

            def bias_and_count(S, Y, bias, t):
                dve.wait_ge(S["result"], t + 1)
                row = Y[:, bass.ds(t, 1), :].rearrange("p o d -> p (o d)")
                v.tensor_tensor(row, row, bias[:, :], ALU.add).then_inc(S["biased"], 1)
                dve.wait_ge(S["biased"], t + 1)
                v.bn_stats(stats[:, bass.ds(t, 1), :].rearrange("p o s -> p (o s)"), row).then_inc(S["counted"], 1)

            def next_x(name):
                layernorm(X, name, masked=True)
                done(v.tensor_scalar(X[:, NT - 1, :], X[:, NT - 1, :], row_ok[:, 0:1], None, ALU.mult), name)

            final_carry_sq = view(final_carry[:, 0:NT * D], "p (t d) -> p t d", d=D)

            attention_steps("att0", H0, D // H0)
            carries("att0", H0, D // H0)
            degree_scales()

            def with_x(ts):
                done(v.tensor_tensor(R[:, ts, :], R[:, ts, :], X[:, ts, :], ALU.add))
                count(R, ts)

            merge_softmax("att0", H0, D // H0, view(R[:, :, :], "p t (h u) -> p t u h", h=H0), with_x)
            layernorm(R, "ln1", rows_in["L0_gnn_ln1_g"], rows_in["L0_gnn_ln1_b"])
            S = TS["ffn"]

            def ffn(t, b):
                dve.wait_ge(S["read"], t + 1)
                v.scalar_tensor_tensor(hn[:, :, :], hb[:, :, :], 0.0, bc(pw[:, :].unsqueeze(2), [128, FC, 128]), ALU.min, ALU.mult).then_inc(S["chain"], 1)
                dve.wait_ge(S["chain"], t + 1)
                v.scalar_tensor_tensor(view(hidden[b], "p (c n) -> p c n", c=FC), hb[:, :, :], 0.0, hn[:, :, :], ALU.max, ALU.add).then_inc(S["hidden"], 1)
                dve.wait_ge(S["hidden"], t + 1)
                if not (isinstance(t, int) and t == 0):
                    ffn_result(t - 1, 1 - b)

            def ffn_result(t, b):
                dve.wait_ge(S["second"], t + 1)
                v.tensor_tensor(R[:, bass.ds(t, 1), :], R[:, bass.ds(t, 1), :], product_in[b][1][:, 0:D].unsqueeze(1), ALU.add).then_inc(S["result"], 1)
                bias_and_count(S, R, rows_in["L0_gnn_b2"], t)

            tiles(dve, ffn)
            ffn_result(NT - 1, (NT - 1) % 2)
            dve.wait_ge(S["counted"], NT)
            layernorm(R, "ln2", rows_in["L0_gnn_ln2_g"], rows_in["L0_gnn_ln2_b"])
            done(v.tensor_tensor(X[:, :, :], X[:, :, :], R[:, :, :], ALU.add))
            count(X, every)
            next_x("x0")

            def gcn_sum(name, k):
                done(v.tensor_tensor(T1[:, :, :], X[:, :, :], over_nodes(dis[k]), ALU.mult), "table " + name)
                edge_sum_steps(name)
                carries(name, 0, D)
                fs = view(final_state[:, 0:NT * D], "p (t w) -> p t w", w=D)
                fc = final_carry_sq
                dve.wait_ge(carries_landed, 16 * (layers.index(name) + 1))
                done(v.tensor_tensor(T1[:, :, :], T1[:, :, :], fc, ALU.add))
                for half, part in enumerate(halves):
                    ts = slice(part[0], part[-1] + 1)
                    dve.wait_ge(LS[name][f"final_landed{half}"], 16 * len(part))
                    done(v.tensor_tensor(T1[:, ts, :], T1[:, ts, :], fs[:, ts, :], ALU.add))
                    for t in part:
                        if k == 0:
                            last = v.scalar_tensor_tensor(X[:, t, :], T1[:, t, :], dis[k][:, t:t + 1], X[:, t, :], ALU.mult, ALU.add)
                        else:
                            last = v.tensor_scalar(R[:, t, :], T1[:, t, :], dis[k][:, t:t + 1], None, ALU.mult)
                    done(last, "agg3" if k and half else None)
                    if k == 0:
                        count(X, ts)

            gcn_sum("sum1", 0)
            next_x("x1")

            S = TS["typed"]

            def typed(t, b):
                S = TS["typed"]
                wait(dve, S["result"], t)
                dve.wait_ge(S["first"], t + 1)
                for k in range(NTYPE):
                    bank, at = (product_in[b][0], k * HXW) if k < 3 else (product_in[b][1], (k - 3) * HXW)
                    mask = view(type_mask[:, :, :], "p t k -> p (t k)")[:, bass.ds(t * NTYPE + k, 1)]
                    dest = hx2[b] if k == NTYPE - 1 else hx
                    if k == NTYPE - 1:
                        wait(dve, S[f"written{b}"], (t - b) * 16)
                        wait(dve, hr_scattered[b], (t - b) * 8)
                    if k == 0:
                        ins = v.tensor_scalar(dest[:, :], bank[:, at:at + HXW], mask, None, ALU.mult)
                    else:
                        ins = v.scalar_tensor_tensor(dest[:, :], bank[:, at:at + HXW], mask, hx[:, :], ALU.mult, ALU.add)
                    if k < NTYPE - 1:
                        ins.then_inc(S["chain"], 1)
                        dve.wait_ge(S["chain"], t * (NTYPE - 1) + (k + 1))
                ins.then_inc(S["result"], 1)

            tiles(dve, typed)
            edge_attention_steps("att2", H2, D // H2)
            carries("att2", H2, D // H2)
            dve.wait_ge(TS["typed"]["second"], NT)

            def with_residual(ts):
                n = ts.stop - ts.start
                done(v.tensor_tensor(R[:, ts, :], R[:, ts, :], T1[:, ts, :], ALU.add))
                done(v.tensor_tensor(R[:, ts, :], R[:, ts, :], bc(rows_in["L2_gnn_b_res"][:, :].unsqueeze(1), [128, n, D]), ALU.add))
                done(v.scalar_tensor_tensor(X[:, ts, :], R[:, ts, :], 0.0, X[:, ts, :], ALU.max, ALU.add))
                count(X, ts)

            merge_softmax("att2", H2, D // H2, view(T1[:, :, :], "p t (u h) -> p t u h", h=H2), with_residual)
            next_x("x2")

            gcn_sum("sum3", 1)
            S = TS["gcn"]

            def add(t, b):
                dve.wait_ge(S["second"], t + 1)
                v.tensor_tensor(X[:, bass.ds(t, 1), :], X[:, bass.ds(t, 1), :], product_in[b][1][:, 0:D].unsqueeze(1), ALU.add).then_inc(S["result"], 1)
                bias_and_count(S, X, rows_in["L3_gnn_lin_b"], t)

            tiles(dve, add)
            dve.wait_ge(S["counted"], NT)
            layernorm(X, "x3")


NAMES = ("x", "src", "dst", "node_type_5", "L0_gnn_Wq", "L0_gnn_Wk", "L0_gnn_Wv", "L0_gnn_ln1_g",
         "L0_gnn_ln1_b", "L0_gnn_ln2_g", "L0_gnn_ln2_b", "L0_gnn_W1", "L0_gnn_b1", "L0_gnn_prelu_w",
         "L0_gnn_W2", "L0_gnn_b2", "L2_gnn_W_typed", "L2_gnn_al_w", "L2_gnn_ar_w", "L2_gnn_W_res",
         "L2_gnn_b_res", "L3_gnn_W", "L3_gnn_b", "L3_gnn_lin_W", "L3_gnn_lin_b")


def kernel(**inputs):
    import numpy as np
    import concourse.bacc as bacc
    from concourse.bass_utils import run_bass_kernel_spmd as run

    nc = bacc.Bacc("TRN2", target_bir_lowering=False, num_devices=1)
    arrays, aps = {}, {}
    for name in NAMES:
        array = np.ascontiguousarray(inputs[name])
        arrays["in_" + name] = array
        aps[name] = nc.dram_tensor("in_" + name, array.shape, mybir.dt.from_np(array.dtype), kind="ExternalInput").ap()
    out = nc.dram_tensor("out_x", tuple(inputs["x"].shape), F32, kind="ExternalOutput").ap()
    gnn_kernel(nc, aps, out)
    return run(nc, [arrays], core_ids=[0]).results[0]["out_x"]
```
